# Optimizing a Trainium2 kernel written in Bass

```python
import numpy as np
import jax
import jax.numpy as jnp

def _softmax(x, axis=-1):
    return jax.nn.softmax(x, axis=axis)

def _gelu(x):
    return jax.nn.gelu(x, approximate=True)

def _silu(x):
    return jax.nn.silu(x)

def _sigmoid(x):
    return jax.nn.sigmoid(x)

def _layernorm(x, axis=-1, eps=1e-05):
    m = jnp.mean(x, axis=axis, keepdims=True)
    v = jnp.var(x, axis=axis, keepdims=True)
    return (x - m) / jnp.sqrt(v + eps)

def _scatter_add(tgt, idx, src, axis=0):
    return tgt.at[idx].add(src)

def _segment_sum(src, seg, n):
    return jax.ops.segment_sum(src, seg, n)
kernel_name = 'mk_perceiver_d1_seqx_r2_5fcfb3'

def setup_inputs(seed: int=0):
    np.random.seed(seed)
    _w = jnp.asarray

    def _rec_inputs():
        import jax
        import jax.numpy as jnp
        _rk = jax.random.key(seed)
        x = 7.22e-05 + 1 * jax.random.normal(jax.random.fold_in(_rk, 1), (2, 512, 512), jnp.float32)
        _lenS = 512 - jax.random.randint(jax.random.fold_in(_rk, 7), (2,), 0, max(1, 512 // 4) + 1, jnp.int32)
        _lenS2 = 8192 - jax.random.randint(jax.random.fold_in(_rk, 8), (2,), 0, max(1, 8192 // 4) + 1, jnp.int32)
        _ctx_1024P = jax.random.normal(jax.random.fold_in(_rk, 11), (2, 16, 512), jnp.float32)
        _ctx_1024c = jax.random.dirichlet(jax.random.fold_in(_rk, 511), 0.3 * jnp.ones((16,), jnp.float32), (2, 8192))
        _ctx_1024t = jnp.einsum('bsk,bkd->bsd', _ctx_1024c, _ctx_1024P)
        _ctx_1024t = _ctx_1024t * jax.lax.rsqrt(jnp.mean(jnp.square(_ctx_1024t)) + 1e-12) * 0.953939
        ctx_1024 = 4.13588e-05 + 0.999923 * (_ctx_1024t + 0.3 * jax.random.normal(jax.random.fold_in(_rk, 611), (2, 8192, 512), jnp.float32))
        return (x, ctx_1024)
    x, ctx_1024 = _rec_inputs()

    def _L0_xattn_setup():
        import jax, jax.numpy as jnp
        import numpy as np
        D = 512
        H = 16
        HD = D // H
        key = jax.random.key(seed)
        ks = jax.random.split(key, 11)
        B, T = (4, 1024)
        s = 1.0 / np.sqrt(D)
        inp = {'q': jax.random.normal(ks[0], (B, T, D), jnp.float32), 'k': jax.random.normal(ks[1], (B, T, D), jnp.float32), 'v': jax.random.normal(ks[2], (B, T, D), jnp.float32), 'Wq': jax.random.normal(ks[3], (D, D), jnp.float32) * s, 'bq': jnp.zeros((D,), jnp.float32), 'Wk': jax.random.normal(ks[4], (D, D), jnp.float32) * s, 'bk': jnp.zeros((D,), jnp.float32), 'Wv': jax.random.normal(ks[5], (D, D), jnp.float32) * s, 'bv': jnp.zeros((D,), jnp.float32), 'Wo': jax.random.normal(ks[6], (D, D), jnp.float32) * s, 'bo': jnp.zeros((D,), jnp.float32)}
        return inp
    _L0_xattn_all = _L0_xattn_setup()
    _L0_xattn_in = {k: v for k, v in _L0_xattn_all.items() if k in ('Wq', 'bq', 'Wk', 'bk', 'Wv', 'bv', 'Wo', 'bo')}
    del _L0_xattn_all

    def _L0_attn_setup():
        import jax, jax.numpy as jnp
        import numpy as np
        import math
        EPS_A = 0.0001
        EPS = 1e-12

        def _l2_bounded(W, bound=1.0):
            sigma = jnp.linalg.svd(W, compute_uv=False)[0]
            return W / jnp.maximum(sigma / bound, 1.0)
        B, T, D = (4, 2048, 512)
        N, D_out = (512, 512)
        key = jax.random.key(seed)
        ks = jax.random.split(key, 4)
        u = jax.random.normal(ks[0], (B, T, D), jnp.float32)
        W_in = 0.02 * jax.random.normal(ks[1], (N, D), jnp.float32)
        W_out = 0.02 * jax.random.normal(ks[2], (D_out, N), jnp.float32)
        Wp = 0.02 * jax.random.normal(ks[3], (3 * N, D), jnp.float32)
        bp = jnp.zeros((3 * N,), jnp.float32)
        rho, delta0 = (0.99, 1.0)
        alpha0 = -math.log(rho) / delta0
        alpha_log = jnp.full((N,), math.log(math.expm1(alpha0)), jnp.float32)
        delta_bias = jnp.full((N,), math.log(math.expm1(delta0)), jnp.float32)
        log_gamma = jnp.array(0.0, jnp.float32)
        return dict(u=u, W_in=W_in, W_out=W_out, Wp=Wp, bp=bp, alpha_log=alpha_log, delta_bias=delta_bias, log_gamma=log_gamma)
    _L0_attn_all = _L0_attn_setup()
    _L0_attn_in = {k: v for k, v in _L0_attn_all.items() if k in ('W_in', 'W_out', 'Wp', 'bp', 'alpha_log', 'delta_bias', 'log_gamma')}
    del _L0_attn_all

    def _L0_ffn_setup():
        import jax, jax.numpy as jnp
        import numpy as np
        H = 512
        I = 1024
        E = 32
        B, S = (4, 1024)

        def _grouped_mm(a, w, group_sizes):
            return jax.lax.ragged_dot(a, w, group_sizes)

        def _swiglu(x, gw, uw, dw):
            return jax.nn.silu(x @ gw) * (x @ uw) @ dw
        key = jax.random.key(seed)
        ks = jax.random.split(key, 8)
        scale = 0.02
        inp = {'hidden_states': jax.random.normal(ks[0], (B, S, H), dtype=jnp.float32), 'gate_w': jax.random.normal(ks[1], (H, E), dtype=jnp.float32) * scale, 'shared_gate_w': jax.random.normal(ks[2], (H, I), dtype=jnp.float32) * scale, 'shared_up_w': jax.random.normal(ks[3], (H, I), dtype=jnp.float32) * scale, 'shared_down_w': jax.random.normal(ks[4], (I, H), dtype=jnp.float32) * scale, 'routed_gate_w': jax.random.normal(ks[5], (E, H, I), dtype=jnp.float32) * scale, 'routed_up_w': jax.random.normal(ks[6], (E, H, I), dtype=jnp.float32) * scale, 'routed_down_w': jax.random.normal(ks[7], (E, I, H), dtype=jnp.float32) * scale}
        return inp
    _L0_ffn_all = _L0_ffn_setup()
    _L0_ffn_in = {k: v for k, v in _L0_ffn_all.items() if k in ('gate_w', 'shared_gate_w', 'shared_up_w', 'shared_down_w', 'routed_gate_w', 'routed_up_w', 'routed_down_w')}
    del _L0_ffn_all
    return {'x': x, 'ctx_1024': ctx_1024, 'L0_xattn_Wq': _L0_xattn_in['Wq'], 'L0_xattn_bq': _L0_xattn_in['bq'], 'L0_xattn_Wk': _L0_xattn_in['Wk'], 'L0_xattn_bk': _L0_xattn_in['bk'], 'L0_xattn_Wv': _L0_xattn_in['Wv'], 'L0_xattn_bv': _L0_xattn_in['bv'], 'L0_xattn_Wo': _L0_xattn_in['Wo'], 'L0_xattn_bo': _L0_xattn_in['bo'], 'L0_attn_W_in': _L0_attn_in['W_in'], 'L0_attn_W_out': _L0_attn_in['W_out'], 'L0_attn_Wp': _L0_attn_in['Wp'], 'L0_attn_bp': _L0_attn_in['bp'], 'L0_attn_alpha_log': _L0_attn_in['alpha_log'], 'L0_attn_delta_bias': _L0_attn_in['delta_bias'], 'L0_attn_log_gamma': _L0_attn_in['log_gamma'], 'L0_ffn_gate_w': _L0_ffn_in['gate_w'], 'L0_ffn_shared_gate_w': _L0_ffn_in['shared_gate_w'], 'L0_ffn_shared_up_w': _L0_ffn_in['shared_up_w'], 'L0_ffn_shared_down_w': _L0_ffn_in['shared_down_w'], 'L0_ffn_routed_gate_w': _L0_ffn_in['routed_gate_w'], 'L0_ffn_routed_up_w': _L0_ffn_in['routed_up_w'], 'L0_ffn_routed_down_w': _L0_ffn_in['routed_down_w']}

def reference(x, ctx_1024, L0_xattn_Wq, L0_xattn_bq, L0_xattn_Wk, L0_xattn_bk, L0_xattn_Wv, L0_xattn_bv, L0_xattn_Wo, L0_xattn_bo, L0_attn_W_in, L0_attn_W_out, L0_attn_Wp, L0_attn_bp, L0_attn_alpha_log, L0_attn_delta_bias, L0_attn_log_gamma, L0_ffn_gate_w, L0_ffn_shared_gate_w, L0_ffn_shared_up_w, L0_ffn_shared_down_w, L0_ffn_routed_gate_w, L0_ffn_routed_up_w, L0_ffn_routed_down_w):
    import jax
    import jax.numpy as jnp

    def _L0_xattn_ref(q, k, v, Wq, bq, Wk, bk, Wv, bv, Wo, bo):
        import jax, jax.numpy as jnp
        import numpy as np
        D = 512
        H = 16
        HD = D // H
        B, Tq, _ = q.shape
        Tk = k.shape[1]
        qw = q @ Wq + bq
        kw = k @ Wk + bk
        vw = v @ Wv + bv
        qh = qw.reshape(B, Tq, H, HD)
        kh = kw.reshape(B, Tk, H, HD)
        vh = vw.reshape(B, Tk, H, HD)
        scale = 1.0 / np.sqrt(HD).astype(np.float32)
        logits = jnp.einsum('bqhd,bkhd->bhqk', qh, kh) * scale
        causal = jnp.tril(jnp.ones((Tq, Tk), bool))
        logits = jnp.where(causal, logits, -jnp.inf)
        attn = jax.nn.softmax(logits, axis=-1)
        out = jnp.einsum('bhqk,bkhd->bqhd', attn, vh).reshape(B, Tq, D)
        return out @ Wo + bo

    def _L0_attn_ref(u, W_in, W_out, Wp, bp, alpha_log, delta_bias, log_gamma):
        import jax, jax.numpy as jnp
        import numpy as np
        import math
        EPS_A = 0.0001
        EPS = 1e-12

        def _l2_bounded(W, bound=1.0):
            sigma = jnp.linalg.svd(W, compute_uv=False)[0]
            return W / jnp.maximum(sigma / bound, 1.0)
        Win_n = _l2_bounded(W_in)
        Wout_n = _l2_bounded(W_out)
        u_scaled = jnp.exp(log_gamma) * jnp.einsum('btd,nd->btn', u, Win_n)
        raw = jnp.einsum('btd,kd->btk', u, Wp) + bp
        delta_raw, b_raw, c_raw = jnp.split(raw, 3, axis=-1)
        delta = jax.nn.softplus(delta_raw + delta_bias)
        alpha = jax.nn.softplus(alpha_log)
        a = jnp.minimum(jnp.exp(-delta * alpha), 1.0 - EPS_A)
        b = jnp.tanh(b_raw)
        c = jnp.tanh(c_raw)
        p = a * a + c * c
        r = b * b
        q = a * b
        disc = (p - r) * (p - r) + 4.0 * q * q
        lam_max = 0.5 * (p + r + jnp.sqrt(disc + EPS))
        sigma = jnp.sqrt(lam_max + EPS)
        scale = jnp.maximum(sigma, 1.0)
        a = a / scale
        b = b / scale
        c = c / scale
        bu = b * u_scaled

        def combine(left, right):
            a1, b1 = left
            a2, b2 = right
            return (a2 * a1, a2 * b1 + b2)
        a_p, b_p = jax.lax.associative_scan(combine, (a, bu), axis=1)
        z_bt = jnp.concatenate([jnp.zeros_like(b_p[:, :1]), b_p[:, :-1]], axis=1)
        y_hat = c * z_bt
        y = jnp.einsum('btn,on->bto', y_hat, Wout_n)
        return y

    def _L0_ffn_ref(hidden_states, gate_w, shared_gate_w, shared_up_w, shared_down_w, routed_gate_w, routed_up_w, routed_down_w):
        import jax, jax.numpy as jnp
        import numpy as np
        H = 512
        I = 1024
        E = 32
        B, S = (4, 1024)

        def _grouped_mm(a, w, group_sizes):
            return jax.lax.ragged_dot(a, w, group_sizes)

        def _swiglu(x, gw, uw, dw):
            return jax.nn.silu(x @ gw) * (x @ uw) @ dw
        b, s, h = hidden_states.shape
        x = hidden_states.reshape(-1, h)
        shared_out = _swiglu(x, shared_gate_w, shared_up_w, shared_down_w)
        logits = x @ gate_w
        topk_ids = jnp.argmax(logits, axis=-1)
        topk_val = jnp.max(logits, axis=-1)
        scores = jax.nn.sigmoid(topk_val)[:, None]
        xs = x * scores
        tokens_per_expert = jnp.zeros((E,), jnp.int32).at[topk_ids].add(1)
        order = jnp.argsort(topk_ids)
        sorted_x = xs[order]
        g = _grouped_mm(sorted_x, routed_gate_w, tokens_per_expert)
        u = _grouped_mm(sorted_x, routed_up_w, tokens_per_expert)
        d = _grouped_mm(jax.nn.silu(g) * u, routed_down_w, tokens_per_expert)
        inv = jnp.argsort(order)
        routed_out = d[inv]
        return (shared_out + routed_out).reshape(b, s, h)
    x = x + _L0_xattn_ref(_layernorm(x, axis=-1), ctx_1024, ctx_1024, L0_xattn_Wq, L0_xattn_bq, L0_xattn_Wk, L0_xattn_bk, L0_xattn_Wv, L0_xattn_bv, L0_xattn_Wo, L0_xattn_bo)
    x = x + _L0_attn_ref(_layernorm(x, axis=-1), L0_attn_W_in, L0_attn_W_out, L0_attn_Wp, L0_attn_bp, L0_attn_alpha_log, L0_attn_delta_bias, L0_attn_log_gamma)
    x = x + _L0_ffn_ref(_layernorm(x, axis=-1), L0_ffn_gate_w, L0_ffn_shared_gate_w, L0_ffn_shared_up_w, L0_ffn_shared_down_w, L0_ffn_routed_gate_w, L0_ffn_routed_up_w, L0_ffn_routed_down_w)
    return x

_drawn_inputs = setup_inputs


def setup_inputs(seed=0):
    import zlib

    import numpy as np

    out = dict(_drawn_inputs(seed))
    spreads = {'L0_xattn_bq': (0.0, 0.363),
     'L0_xattn_bk': (0.0, 0.8),
     'L0_xattn_bv': (0.0, 0.1),
     'L0_xattn_bo': (0.0, 0.1),
     'L0_attn_bp': (0.0, 0.357),
     'L0_attn_alpha_log': (-4.595119953155518, 0.6),
     'L0_attn_delta_bias': (0.5413248538970947, 0.6)}
    factors = {}
    for name, (base, spread) in spreads.items():
        noise = np.random.default_rng([zlib.crc32(name.encode()), seed]).standard_normal(out[name].shape)
        drawn = base * np.exp(spread * noise) if base else spread * noise
        out[name] = jnp.asarray(drawn.astype(out[name].dtype))
    for name, factor in factors.items():
        out[name] = (out[name] * factor).astype(out[name].dtype)
    return out
```

```python
import concourse.bass as bass
from concourse import mybir
from contextlib import ExitStack

B, T, D = 2, 512, 512
TOK = B * T
H, HD = 16, 32
NCH = 512
E, I = 32, 1024
P = 128
KD = D // P
NT = TOK // P
QT_N = T // P
HB = P // HD
CAP = 64
XTRA = TOK // CAP - 1
SLOTS = (E + XTRA + 1) * CAP
WORDS = 12288
GU = KD * I

COL_BQ, COL_BK, COL_BP, COL_DB, COL_AL, COL_LG = 0, 4, 8, 20, 24, 28
COLS = 29
C_IDENT, C_MASK, C_IOTA = 0, 128, 256
CONSTS = 288
MASKED = -1.0e30


def perceiver_layer(nc, x, ctxT, Wq, Wk, Wv, Wo, WinT, WoutT, WpT, gate_w, sg, su, sd, rg, ru, rd,
                    cols_in, rows_in, consts_in, out):
    f32, bf16, i32, u32 = mybir.dt.float32, mybir.dt.bfloat16, mybir.dt.int32, mybir.dt.uint32
    ALU, ACT, AX = mybir.AluOpType, mybir.ActivationFunctionType, mybir.AxisListType

    xs_sorted = nc.dram_tensor("xs_sorted", [SLOTS, D], f32, kind="Internal").ap()
    ys_sorted = nc.dram_tensor("ys_sorted", [SLOTS, D], f32, kind="Internal").ap()

    with ExitStack() as ctx:
        def sb(name, shape, dt=f32):
            return ctx.enter_context(nc.sbuf_tensor(name, shape, dt))

        def sem(name):
            return ctx.enter_context(nc.semaphore(name))

        xres = sb("xres", [P, NT, D])
        xT = sb("xT", [P, KD, TOK])
        ring0 = sb("ring0", [P, WORDS])
        ZONE = 17408
        area = sb("area", [P, WORDS + ZONE])
        consts = sb("consts", [P, CONSTS])
        cols = sb("cols", [P, COLS])
        rows = sb("rows", [P, 2, D])
        ones32 = sb("ones32", [P, P])
        onesb = sb("onesb", [P, P], bf16)
        trib = sb("trib", [P, P], bf16)
        eps = sb("eps", [P, 3])
        bnst = sb("bnst", [P, NT, 6])
        mv = sb("mv", [P, NT, 2])
        rstd = sb("rstd", [P, NT])
        colb = sb("colb", [P, 8])
        spec = sb("spec", [P, 16])
        zero = sb("zero", [P, D])
        flag = sb("flag", [P, 1], i32)
        mx = sb("mx", [P, 2, HB])
        nmx = sb("nmx", [P, 2, HB])
        rsum = sb("rsum", [P, 2, HB])
        gw = sb("gw", [P, KD, E])
        ohb = sb("ohb", [P, NT, E], bf16)
        top8 = sb("top8", [P, NT, 8])
        idx8 = sb("idx8", [P, NT, 8], u32)
        idxf = sb("idxf", [P, NT])
        score = sb("score", [P, NT])
        pos = sb("pos", [P, 6, NT])
        slot = sb("slot", [P, NT], i32)
        ecnt = sb("ecnt", [P, 6, E])
        ecnti = sb("ecnti", [P, E], i32)
        ovs = sb("ovs", [P, XTRA + 1])
        ovi = sb("ovi", [P, XTRA + 1], i32)
        ps = ctx.enter_context(nc.psum_tensor("ps", [P, 8, 512], f32))

        def at(off, n):
            return area[:, off:off + n]

        ident = consts[:, C_IDENT:C_IDENT + P]
        mask = consts[:, C_MASK:C_MASK + P]

        spw = [at(WORDS + 2048 * m, 2048).rearrange("p (k n) -> p k n", k=KD) for m in range(2)]
        spp = [[at(WORDS + 4096 + 2048 * m + 1024 * j, 1024).bitcast(bf16).rearrange("p (k n) -> p k n", k=KD)
                for j in range(2)] for m in range(2)]
        g_a, g_p, g_junk = (ring0[:, 2048 * j:2048 * j + 2048].rearrange("p (k n) -> p k n", k=KD) for j in range(3))
        cT = at(0, 4096).rearrange("p (k n) -> p k n", k=KD)
        oT = cT
        wq_s, wk_s, wv_s = (at(4096 + 2048 * j, 2048).rearrange("p (k n) -> p k n", k=KD) for j in range(3))
        pr = [at(4096 + 2048 * j, 2048).rearrange("p (h n) -> p h n", h=HB) for j in range(2)]
        pT = [at(10240 + 2048 * j, 2048).rearrange("p (h n) -> p h n", h=HB) for j in range(2)]
        qT = at(15360, 4096).rearrange("p (k n) -> p k n", k=KD)
        kT = at(19456, 4096).rearrange("p (k n) -> p k n", k=KD)
        vv = at(23552, 4096).rearrange("p (t n) -> p t n", t=NT)
        wo_s = at(27648, 2048).rearrange("p (k n) -> p k n", k=KD)
        xn = [at(14336 + 512 * j, 512) for j in range(2)]
        wp_s = at(15360, 6144).rearrange("p (k n) -> p k n", k=KD)
        win_s = at(21504, 2048).rearrange("p (k n) -> p k n", k=KD)
        wout_s = at(23552, 2048).rearrange("p (k n) -> p k n", k=KD)
        rA, rB, rC, rU, t1, t2, t3 = (at(2048 * j, 2048).rearrange("p (c n) -> p c n", c=2) for j in range(7))
        yh = at(25600, 4096).rearrange("p (c n) -> p c n", c=4)
        Z = WORDS
        hsT = at(Z, 8192).rearrange("p (c n) -> p c n", c=I // P)
        gtmp = [at(Z + 8192 + 512 * j, 512) for j in range(2)]
        xe = at(Z + 9216, 512)
        xeT = at(Z + 10240, 512).rearrange("p (k n) -> p k n", k=KD)
        ge = [at(Z + 10752 + 512 * j, 512) for j in range(2)]
        he = [at(Z + 11776 + 512 * j, 512) for j in range(2)]
        heT = [at(Z + 12800 + 512 * j, 512) for j in range(2)]
        ye = [at(Z + 13824 + 256 * j, 256) for j in range(2)]
        xsc = [at(Z + 14336 + 512 * j, 512) for j in range(2)]
        fin = [at(Z + 512 * j, 512) for j in range(4)]
        ovl = at(Z + 11776, XTRA * E).rearrange("p (o e) -> p o e", o=XTRA)
        oh = at(Z + 12800, NT * E).rearrange("p (t e) -> p t e", t=NT)
        lg = at(Z + 13056, NT * E).rearrange("p (t e) -> p t e", t=NT)

        ring = [ring0, area[:, 0:WORDS]]

        def w_gate(s):
            return ring[s][:, 0:GU].rearrange("p (k n) -> p k n", k=KD)

        def w_up(s):
            return ring[s][:, GU:2 * GU].rearrange("p (k n) -> p k n", k=KD)

        def w_down(s):
            return ring[s][:, 2 * GU:3 * GU].rearrange("p (k n) -> p k n", k=I // P)

        ld_spec, ld_const, ld_x, ld_ctx, ld_wk, ld_wv, ld_wq, ld_wo, ld_rec, ld_gw = (
            sem(n) for n in ("ld_spec", "ld_const", "ld_x", "ld_ctx", "ld_wk", "ld_wv", "ld_wq", "ld_wo", "ld_rec", "ld_gw"))
        ld_gate, ld_up, ld_down = ([sem(f"{n}{j}") for j in range(2)] for n in ("ld_gate", "ld_up", "ld_down"))
        zeroed, filled = sem("zeroed"), sem("filled")
        sp_conv, sp_sq, sp_ev0, sp_ev1 = sem("sp_conv"), sem("sp_sq"), sem("sp_ev0"), sem("sp_ev1")
        sp_sum, sp_tot, sp_flag, sp_done = sem("sp_sum"), sem("sp_tot"), sem("sp_flag"), sem("sp_done")
        gp_mm, gp_ev, gp_ssq, gp_tot, gp_rt, gp_nrm, gp_a = (sem(n) for n in ("gp_mm", "gp_ev", "gp_ssq", "gp_tot", "gp_rt", "gp_nrm", "gp_a"))
        lg_exp, ready_c = sem("lg_exp"), sem("ready_c")
        ln_stat, ln_sqrt, ln_xn, ln_tr, ln_xT = (sem(n) for n in ("ln_stat", "ln_sqrt", "ln_xn", "ln_tr", "ln_xT"))
        pj_mm, pj_act, pj_dve = sem("pj_mm"), sem("pj_act"), sem("pj_dve")
        at_s, at_nm, at_exp, at_p, at_tr, at_ev, at_pv, at_o = (
            sem(n) for n in ("at_s", "at_nm", "at_exp", "at_p", "at_tr", "at_ev", "at_pv", "at_o"))
        wo_mm, wo_x = sem("wo_mm"), sem("wo_x")
        rc_mm, rc_free, rc_cap, rc_sp, rc_delta, rc_a, rc_th, rc_disc, rc_sq1, rc_lam, rc_sq2, rc_y, rc_al = (
            sem(n) for n in ("rc_mm", "rc_free", "rc_cap", "rc_sp", "rc_delta", "rc_a", "rc_th", "rc_disc", "rc_sq1",
                             "rc_lam", "rc_sq2", "rc_y", "rc_al"))
        ro_mm, ro_x = sem("ro_mm"), sem("ro_x")
        rt_lg, rt_lgs, rt_oh, rt_rank, rt_max, rt_sig, rt_slot, rt_xs, rt_sc, rt_tab, sc_done = (
            sem(n) for n in ("rt_lg", "rt_lgs", "rt_oh", "rt_rank", "rt_max", "rt_sig", "rt_slot", "rt_xs", "rt_sc",
                             "rt_tab", "sc_done"))
        sh_gu, sh_silu, sh_h, sh_y, sh_x = (sem(n) for n in ("sh_gu", "sh_silu", "sh_h", "sh_y", "sh_x"))
        ex_x, ex_tr, ex_xT, ex_g, ex_u, ex_silu, ex_h, ex_ht, ex_hT, ex_y, ex_ye = (
            sem(n) for n in ("ex_x", "ex_tr", "ex_xT", "ex_g", "ex_u", "ex_silu", "ex_h", "ex_ht", "ex_hT", "ex_y", "ex_ye"))
        ex_st = [sem(f"ex_st{j}") for j in range(2)]
        ov_w, ov_x, ov_tr, ov_xT, ov_gu, ov_silu, ov_h, ov_ht, ov_hT, ov_y, ov_ye, ov_st = (
            sem(n) for n in ("ov_w", "ov_x", "ov_tr", "ov_xT", "ov_gu", "ov_silu", "ov_h", "ov_ht", "ov_hT", "ov_y",
                             "ov_ye", "ov_st"))
        moe_done = sem("moe_done")
        gat = [sem(f"gat{j}") for j in range(4)]
        fin_add = sem("fin_add")
        stored = [sem(f"stored{j}") for j in range(4)]
        dve_own, dve_own2 = sem("dve_own"), sem("dve_own2")

        GENERAL_STEPS = 16
        GROUPS = [(b, k, q) for b in range(B) for k in range(KD) for q in range(QT_N)]

        PJ = ([("k", k, b) for k in range(KD) for b in range(B)] + [("v", t, 0) for t in range(NT)]
              + [("q", k, b) for k in range(KD) for b in range(B)])
        PJ_EV, n_act, n_dve = [], 0, 0
        for kind, _, _ in PJ:
            if kind == "v":
                n_dve += 1
                PJ_EV.append((pj_dve, n_dve))
            else:
                n_act += 1
                PJ_EV.append((pj_act, n_act))
        N_K, N_Q = KD * B, KD * B

        block = ctx.enter_context(nc.Block())

        @block.sync
        def _(sp):
            def kmaj(w):
                return w.rearrange("(k p) n -> p k n", p=P)

            sp.dma_start(spw[0], kmaj(WinT)).then_inc(ld_spec, 16)
            sp.dma_start(spw[1], kmaj(WoutT)).then_inc(ld_spec, 16)
            sp.dma_start(consts[:, :], consts_in).then_inc(ld_const, 16)
            sp.dma_start(cols[:, :], cols_in).then_inc(ld_const, 16)
            sp.dma_start(rows[:, :, :], rows_in).then_inc(ld_const, 16)
            sp.dma_start(cT, kmaj(ctxT)).then_inc(ld_ctx, 16)
            sp.dma_start(wk_s, kmaj(Wk)).then_inc(ld_wk, 16)
            sp.dma_start(wv_s, kmaj(Wv)).then_inc(ld_wv, 16)
            sp.dma_start(xres[:, :, :], x.rearrange("(t p) n -> p t n", p=P)).then_inc(ld_x, 16)
            sp.dma_start(wq_s, kmaj(Wq)).then_inc(ld_wq, 16)
            sp.dma_start(gw[:, :, :], kmaj(gate_w)).then_inc(ld_gw, 16)
            sp.wait_ge(sp_done, 1)
            sp.dma_start(wo_s, kmaj(Wo)).then_inc(ld_wo, 16)
            sp.dma_start(w_gate(0), kmaj(sg)).then_inc(ld_gate[0], 16)
            sp.dma_start(w_up(0), kmaj(su)).then_inc(ld_up[0], 16)
            sp.dma_start(w_down(0), kmaj(sd)).then_inc(ld_down[0], 16)
            sp.wait_ge(zeroed, 1)
            for t in range(SLOTS // P):
                sp.dma_start(xs_sorted[t * P:(t + 1) * P, :], zero[:, :]).then_inc(filled, 16)
            for t in range(E * CAP // P, SLOTS // P):
                sp.dma_start(ys_sorted[t * P:(t + 1) * P, :], zero[:, :]).then_inc(filled, 16)
            sp.wait_ge(at_pv, len(GROUPS))
            sp.dma_start(wp_s, kmaj(WpT)).then_inc(ld_rec, 16)
            sp.dma_start(win_s, kmaj(WinT)).then_inc(ld_rec, 16)
            sp.dma_start(wout_s, kmaj(WoutT)).then_inc(ld_rec, 16)
            sp.wait_ge(ro_mm, NT)
            with sp.Fori(0, E // 2) as i:
                for j in range(2):
                    s = 1 - j
                    e = i * 2 + j
                    sp.wait_ge(ex_u, i * 2 + j)
                    sp.dma_start(w_gate(s), rg[bass.ds(e, 1), :, :].rearrange("a (k p) n -> p (a k) n", p=P)).then_inc(ld_gate[s], 16)
                    sp.dma_start(w_up(s), ru[bass.ds(e, 1), :, :].rearrange("a (k p) n -> p (a k) n", p=P)).then_inc(ld_up[s], 16)
                    sp.wait_ge(ex_y, i * 2 + j)
                    sp.dma_start(w_down(s), rd[bass.ds(e, 1), :, :].rearrange("a (k p) n -> p (a k) n", p=P)).then_inc(ld_down[s], 16)
            sp.wait_ge(rt_tab, 1)
            extra = sp.value_load(ovi[0:1, XTRA:XTRA + 1], min_val=0, max_val=XTRA)
            with sp.If(extra > 0):
                sp.wait_ge(ex_y, E + 1)
                with sp.Fori(0, extra) as o:
                    sp.wait_ge(ov_y, o)
                    e = sp.value_load(ovi[0:1, bass.ds(o, 1)], min_val=0, max_val=E - 1)
                    sp.dma_start(w_gate(1), rg[bass.ds(e, 1), :, :].rearrange("a (k p) n -> p (a k) n", p=P)).then_inc(ov_w, 16)
                    sp.dma_start(w_up(1), ru[bass.ds(e, 1), :, :].rearrange("a (k p) n -> p (a k) n", p=P)).then_inc(ov_w, 16)
                    sp.dma_start(w_down(1), rd[bass.ds(e, 1), :, :].rearrange("a (k p) n -> p (a k) n", p=P)).then_inc(ov_w, 16)

        @block.gpsimd
        def _(pool):
            nc.gpsimd.memset(ones32[:, :], 1.0)
            nc.gpsimd.memset(onesb[:, :], 1.0)
            nc.gpsimd.memset(eps[:, 0:1], 1e-5)
            nc.gpsimd.memset(eps[:, 1:2], 1e-12)
            nc.gpsimd.memset(eps[:, 2:3], 1.0)
            nc.gpsimd.memset(zero[:, :], 0.0).then_inc(zeroed, 1)
            pool.wait_ge(zeroed, 1)
            nc.gpsimd.affine_select(out=trib[:, :], in_=onesb[:, :], compare_op=ALU.is_gt, fill=0.0, base=0,
                                    pattern=[[1, P]], channel_multiplier=-1).then_inc(ready_c, 1)

            pool.wait_ge(filled, 16 * (2 * SLOTS // P - E * CAP // P))
            pool.wait_ge(rt_slot, 1)
            for t in range(NT):
                pool.wait_ge(rt_xs, t + 1)
                nc.gpsimd.indirect_dma_start(
                    xs_sorted[:, :], bass.IndirectOffsetOnAxis(ap=slot[:, t:t + 1], axis=0), xsc[t % 2], None,
                ).then_inc(sc_done, 16)
                pool.wait_ge(sc_done, 16 * (t + 1))
                pool.sem_inc(rt_sc, 1)

            nc.gpsimd.dma_start(xe, xs_sorted[0:P, :]).then_inc(ex_x, 16)
            with pool.Fori(0, E // 2 - 1) as i:
                pool.wait_ge(ex_tr, i + 1)
                nc.gpsimd.dma_start(xe, xs_sorted[bass.ds(i * P + P, P), :]).then_inc(ex_x, 16)

            pool.wait_ge(rt_tab, 1)
            extra = pool.value_load(ovi[0:1, XTRA:XTRA + 1], min_val=0, max_val=XTRA)
            with pool.If(extra > 0):
                pool.wait_ge(ex_tr, E // 2)
                with pool.Fori(0, extra) as o:
                    pool.wait_ge(ov_y, o)
                    nc.gpsimd.dma_start(xe, xs_sorted[bass.ds(o * CAP + E * CAP, P), :]).then_inc(ov_x, 16)

            pool.wait_ge(moe_done, 1)
            for t in range(NT):
                if t >= 4:
                    pool.wait_ge(stored[t % 4], 16 * (t // 4))
                nc.gpsimd.indirect_dma_start(
                    fin[t % 4], None, ys_sorted[:, :], bass.IndirectOffsetOnAxis(ap=slot[:, t:t + 1], axis=0),
                ).then_inc(gat[t % 4], 16)

        @block.scalar
        def _(act):
            act.wait_ge(ld_spec, 32)
            nc.scalar.copy(spp[0][0], spw[0]).then_inc(sp_conv, 1)
            for s in range(4):
                act.wait_ge(sp_sq, 2 * s + 1)
                nc.scalar.copy(spp[0][(s + 1) % 2], ps[:, 0:4, :]).then_inc(sp_ev0, 1)
            for m in range(2):
                act.wait_ge(sp_sq, 9 + m)
                nc.scalar.activation(spp[m][1], ps[:, 4 * m:4 * m + 4, :], ACT.Square,
                                     accum_out=spec[:, m:m + 1]).then_inc(sp_sum, 1)
            act.wait_ge(ld_const, 48)
            nc.scalar.activation(spec[:, 8:9], cols[:, COL_LG:COL_LG + 1], ACT.Exp).then_inc(lg_exp, 1)
            act.wait_ge(sp_flag, 1)
            general = act.value_load(flag[0:1, 0:1], min_val=0, max_val=1)
            with act.If(general > 0):
                for m in range(2):
                    with act.Fori(0, GENERAL_STEPS + 1) as i:
                        n = i + m * (GENERAL_STEPS + 2)
                        act.wait_ge(gp_tot, n + 1)
                        nc.scalar.activation(spec[:, 5:6], ps[:, 4, 0:1], ACT.Sqrt).then_inc(gp_rt, 1)
                    act.wait_ge(gp_nrm, (m + 1) * (GENERAL_STEPS + 2))
                    nc.scalar.activation(spec[:, 5:6], spec[:, 6:7], ACT.Sqrt).then_inc(gp_rt, 1)

            def project_out(n):
                kind, k, b = PJ[n]
                dst, col = (kT, COL_BK) if kind == "k" else (qT, COL_BQ)
                act.wait_ge(pj_mm, n + 1)
                nc.scalar.activation(dst[:, k, b * T:(b + 1) * T], ps[:, 2 + n % 6, :], ACT.Identity,
                                     bias=cols[:, col + k:col + k + 1]).then_inc(pj_act, 1)

            def layernorm_root(n):
                act.wait_ge(ln_stat, n + 1)
                nc.scalar.activation(rstd[:, :], mv[:, :, 1], ACT.Sqrt, bias=eps[:, 0:1]).then_inc(ln_sqrt, 1)

            def transposed_out(n, t):
                act.wait_ge(ln_tr, n * NT + t + 1)
                nc.scalar.copy(xT[:, :, t * P:(t + 1) * P],
                               ps[:, t % 2, :].rearrange("p (k n) -> p k n", k=KD)).then_inc(ln_xT, 1)

            act.wait_ge(ready_c, 1)
            layernorm_root(0)
            for n, (kind, _, _) in enumerate(PJ):
                if kind == "k":
                    project_out(n)
            for t in range(NT):
                transposed_out(0, t)
            for n, (kind, _, _) in enumerate(PJ):
                if kind == "q":
                    project_out(n)

            def exps(g):
                b, k, q = GROUPS[g]
                n = (q + 1) * P
                act.wait_ge(at_nm, g + 1)
                if g >= 2:
                    act.wait_ge(at_tr, 4 * (g - 1))
                for h in range(HB):
                    nc.scalar.activation(pr[g % 2][:, h, 0:n], ps[:, h, 0:n], ACT.Exp, bias=nmx[:, g % 2, h:h + 1],
                                         scale=HD ** -0.5, accum_out=rsum[:, g % 2, h:h + 1]).then_inc(at_exp, 1)

            def probs_out(g):
                b, k, q = GROUPS[g]
                n = (q + 1) * P
                if g >= 2:
                    act.wait_ge(at_pv, g - 1)
                for h in range(HB):
                    act.wait_ge(at_tr, 4 * g + h + 1)
                    nc.scalar.copy(pT[g % 2][:, h, 0:n], ps[:, 4 + h % 2, 0:n]).then_inc(at_ev, 1)

            for g in range(len(GROUPS)):
                exps(g)
                if g >= 1:
                    probs_out(g - 1)
            probs_out(len(GROUPS) - 1)

            nc.scalar.activation(colb[:, 4:8], cols[:, COL_AL:COL_AL + 4], ACT.Exp).then_inc(rc_al, 1)
            act.wait_ge(rc_al, 1)
            nc.scalar.activation(colb[:, 4:8], colb[:, 4:8], ACT.Ln, bias=eps[:, 2:3]).then_inc(rc_al, 1)
            act.wait_ge(wo_x, NT)
            layernorm_root(1)
            for t in range(NT):
                transposed_out(1, t)
            for pair in range(2):
                act.wait_ge(rc_cap, pair + 1)
                nc.scalar.activation(t1, t1, ACT.Exp).then_inc(rc_sp, 1)
                act.wait_ge(rc_sp, 2 * pair + 1)
                nc.scalar.activation(t1, t1, ACT.Ln, bias=eps[:, 2:3]).then_inc(rc_sp, 1)
                act.wait_ge(rc_delta, pair + 1)
                for c in range(2):
                    nb = 2 * pair + c
                    nc.scalar.activation(rA[:, c, :], t1[:, c, :], ACT.Exp, scale=colb[:, 4 + nb:5 + nb]).then_inc(rc_a, 1)
                for q, dst in ((1, rB), (2, rC)):
                    act.wait_ge(rc_mm, 4 * pair + q + 1)
                    for c in range(2):
                        nb = 2 * pair + c
                        nc.scalar.activation(dst[:, c, :], ps[:, 4 * (q % 2) + 2 * c:4 * (q % 2) + 2 * c + 2, :].rearrange("p a n -> p (a n)"),
                                             ACT.Tanh, bias=cols[:, COL_BP + 4 * q + nb:COL_BP + 4 * q + nb + 1]).then_inc(rc_th, 1)
                act.wait_ge(rc_disc, pair + 1)
                nc.scalar.activation(t3, t3, ACT.Sqrt, bias=eps[:, 1:2]).then_inc(rc_sq1, 1)
                act.wait_ge(rc_lam, pair + 1)
                nc.scalar.activation(t1, t1, ACT.Sqrt, bias=eps[:, 1:2], scale=0.5).then_inc(rc_sq2, 1)

            act.wait_ge(ro_x, NT)
            layernorm_root(2)
            for t in range(NT):
                transposed_out(2, t)
            act.wait_ge(rt_max, 1)
            nc.scalar.activation(score[:, :], top8[:, :, 0], ACT.Sigmoid).then_inc(rt_sig, 1)
            for c in range(I // P):
                for b in range(B):
                    n = c * B + b
                    act.wait_ge(sh_gu, 2 * n + 1)
                    if n >= 2:
                        act.wait_ge(sh_h, n - 1)
                    nc.scalar.activation(gtmp[n % 2], ps[:, 2 * (n % 3), :], ACT.Silu).then_inc(sh_silu, 1)

            with act.Fori(0, E // 2) as i:
                for j in range(2):
                    e = i * 2 + j
                    if j == 0:
                        act.wait_ge(ex_tr, i + 1)
                        nc.scalar.copy(xeT, ps[:, 4, :].rearrange("p (k n) -> p k n", k=KD)).then_inc(ex_xT, 1)
                    act.wait_ge(ex_g, e + 1)
                    nc.scalar.activation(ge[j], ps[:, 2 * j, :], ACT.Silu).then_inc(ex_silu, 1)
                    act.wait_ge(ex_y, e + 2)
                    act.wait_ge(ex_st[j], i * 32)
                    nc.scalar.copy(ye[j], ps[:, 6 + j, 0:256]).then_inc(ex_ye, 1)
                    act.wait_ge(ex_ye, e + 1)
                    for half in range(2):
                        act.dma_start(ys_sorted[bass.ds(i * (2 * CAP) + j * CAP, CAP), half * 256:(half + 1) * 256],
                                      ye[j][half * CAP:(half + 1) * CAP, :]).then_inc(ex_st[j], 16)

            act.wait_ge(rt_tab, 1)
            extra = act.value_load(ovi[0:1, XTRA:XTRA + 1], min_val=0, max_val=XTRA)
            for j in range(2):
                act.wait_ge(ex_st[j], 32 * (E // 2))
            with act.If(extra > 0):
                with act.Fori(0, extra) as o:
                    act.wait_ge(ov_tr, o + 1)
                    nc.scalar.copy(xeT, ps[:, 4, :].rearrange("p (k n) -> p k n", k=KD)).then_inc(ov_xT, 1)
                    act.wait_ge(ov_gu, o + 1)
                    nc.scalar.activation(ge[0], ps[:, 0, :], ACT.Silu).then_inc(ov_silu, 1)
                    act.wait_ge(ov_y, o + 1)
                    nc.scalar.copy(ye[0], ps[:, 6, 0:256]).then_inc(ov_ye, 1)
                    act.wait_ge(ov_ye, o + 1)
                    for half in range(2):
                        act.dma_start(ys_sorted[bass.ds(o * CAP + E * CAP, CAP), half * 256:(half + 1) * 256],
                                      ye[0][half * CAP:(half + 1) * CAP, :]).then_inc(ov_st, 16)
                    act.wait_ge(ov_st, o * 32 + 32)
            act.sem_inc(moe_done, 1)

            for t in range(NT):
                act.wait_ge(fin_add, t + 1)
                act.dma_start(out[t * P:(t + 1) * P, :], fin[t % 4]).then_inc(stored[t % 4], 16)
            for j in range(4):
                act.wait_ge(stored[j], 16 * (NT // 4))

        @block.vector
        def _(dve):
            own = [0]

            def step(ins):
                own[0] += 1
                ins.then_inc(dve_own, 1)
                dve.wait_ge(dve_own, own[0])

            step(nc.vector.memset(spec[:, 2:4], 1.0))
            dve.wait_ge(ld_spec, 32)
            nc.vector.tensor_copy(spp[1][0], spw[1]).then_inc(sp_conv, 1)
            for s in range(4):
                dve.wait_ge(sp_sq, 2 * s + 2)
                nc.vector.tensor_copy(spp[1][(s + 1) % 2], ps[:, 4:8, :]).then_inc(sp_ev1, 1)
            dve.wait_ge(sp_tot, 1)
            step(nc.vector.tensor_scalar(spec[:, 10:12], ps[:, 0, 0:2], 0.01, None, ALU.is_le))
            step(nc.vector.tensor_tensor(spec[:, 12:13], spec[:, 10:11], spec[:, 11:12], ALU.mult))
            nc.vector.tensor_scalar(flag[:, :], spec[:, 12:13], -1.0, 1.0, ALU.mult, ALU.add).then_inc(sp_flag, 1)
            dve.wait_ge(sp_flag, 1)
            general = dve.value_load(flag[0:1, 0:1], min_val=0, max_val=1)
            with dve.If(general > 0):
                for m in range(2):
                    base = m * (GENERAL_STEPS + 2)
                    dve.wait_ge(gp_mm, base + 1)
                    nc.vector.tensor_copy(g_a, ps[:, 0:4, :]).then_inc(gp_a, 1)
                    with dve.Fori(0, GENERAL_STEPS + 1) as i:
                        dve.wait_ge(gp_mm, i + (base + 1))
                        nc.vector.tensor_copy(g_p, ps[:, 0:4, :]).then_inc(gp_ev, 1)
                        dve.wait_ge(gp_ev, i + (m * (GENERAL_STEPS + 1) + 1))
                        nc.vector.tensor_tensor_reduce(out=g_junk, in0=g_p, in1=g_p, scale=1.0, scalar=0.0,
                                                       op0=ALU.mult, op1=ALU.add, accum_out=spec[:, 4:5]).then_inc(gp_ssq, 1)
                        dve.wait_ge(gp_rt, i + (base + 1))
                        nc.vector.tensor_scalar(spec[:, 7:8], spec[:, 5:6], 1e-30, None, ALU.max).then_inc(gp_ssq, 1)
                        dve.wait_ge(gp_ssq, i * 3 + (3 * base + 2))
                        nc.vector.reciprocal(spec[:, 7:8], spec[:, 7:8]).then_inc(gp_ssq, 1)
                        dve.wait_ge(gp_ssq, i * 3 + (3 * base + 3))
                        nc.vector.tensor_scalar(g_p, g_p, spec[:, 7:8], None, ALU.mult).then_inc(gp_nrm, 1)
                    dve.wait_ge(gp_mm, base + GENERAL_STEPS + 2)
                    dve.wait_ge(gp_nrm, base + GENERAL_STEPS + 1)
                    k3 = 3 * (base + GENERAL_STEPS + 1)
                    nc.vector.tensor_tensor_reduce(out=g_junk, in0=ps[:, 0:4, :], in1=g_p, scale=1.0, scalar=0.0,
                                                   op0=ALU.mult, op1=ALU.add, accum_out=spec[:, 4:5]).then_inc(gp_ssq, 1)
                    dve.wait_ge(gp_ssq, k3 + 1)
                    nc.vector.tensor_tensor_reduce(out=g_junk, in0=g_p, in1=g_p, scale=1.0, scalar=0.0,
                                                   op0=ALU.mult, op1=ALU.add, accum_out=spec[:, 13:14]).then_inc(gp_ssq, 1)
                    dve.wait_ge(gp_tot, base + GENERAL_STEPS + 2)
                    nc.vector.reciprocal(spec[:, 14:15], ps[:, 4, 1:2]).then_inc(gp_ssq, 1)
                    dve.wait_ge(gp_ssq, k3 + 3)
                    step(nc.vector.tensor_tensor(spec[:, 15:16], ps[:, 4, 0:1], spec[:, 14:15], ALU.mult))
                    nc.vector.tensor_scalar(spec[:, 6:7], spec[:, 15:16], 1.0, None, ALU.max).then_inc(gp_nrm, 1)
                    dve.wait_ge(gp_rt, base + GENERAL_STEPS + 2)
                    step(nc.vector.reciprocal(spec[:, 2 + m:3 + m], spec[:, 5:6]))
            nc.vector.tensor_tensor(spec[:, 9:10], spec[:, 2:3], spec[:, 3:4], ALU.mult).then_inc(sp_done, 1)

            own2 = [0]

            def step(ins):
                own2[0] += 1
                ins.then_inc(dve_own2, 1)
                dve.wait_ge(dve_own2, own2[0])

            dve.wait_ge(sp_done, 1)
            dve.wait_ge(lg_exp, 1)
            step(nc.vector.tensor_tensor(spec[:, 9:10], spec[:, 9:10], spec[:, 8:9], ALU.mult))

            def layernorm_stats(n):
                for t in range(NT):
                    last = nc.vector.bn_stats(bnst[:, t, :], xres[:, t, :])
                step(last)
                for t in range(NT):
                    last = nc.vector.bn_aggr(mv[:, t, :], bnst[:, t, :])
                last.then_inc(ln_stat, 1)

            def layernorm_apply(n):
                dve.wait_ge(ln_sqrt, n + 1)
                step(nc.vector.reciprocal(rstd[:, :], rstd[:, :]))
                for t in range(NT):
                    if t >= 2:
                        dve.wait_ge(ln_tr, n * NT + t - 1)
                    nc.vector.tensor_scalar(xn[t % 2], xres[:, t, :], mv[:, t, 0:1], rstd[:, t:t + 1],
                                            ALU.subtract, ALU.mult).then_inc(ln_xn, 1)

            dve.wait_ge(ld_x, 16)
            layernorm_stats(0)
            dve.wait_ge(ld_const, 48)
            for n, (kind, t, _) in enumerate(PJ):
                if kind == "v":
                    dve.wait_ge(pj_mm, n + 1)
                    nc.vector.tensor_tensor(vv[:, t, :], ps[:, 2 + n % 6, :], rows[:, 0, :], ALU.add).then_inc(pj_dve, 1)
            layernorm_apply(0)
            for t in range(NT):
                if t == 0:
                    dve.wait_ge(ln_xn, NT)
                last = nc.vector.tensor_tensor(xres[:, t, :], xres[:, t, :], rows[:, 1, :], ALU.add)
            step(last)

            def row_max(g):
                b, k, q = GROUPS[g]
                n = (q + 1) * P
                dve.wait_ge(at_s, g + 1)
                if g >= 2:
                    dve.wait_ge(at_exp, 4 * (g - 1))
                step(nc.vector.tensor_tensor(ps[:, 0:HB, q * P:n], ps[:, 0:HB, q * P:n],
                                             mask.rearrange("p (a n) -> p a n", a=1).broadcast_to([P, HB, P]), ALU.add))
                step(nc.vector.tensor_reduce(mx[:, g % 2, :], ps[:, 0:HB, 0:n], AX.X, ALU.max))
                nc.vector.tensor_scalar(nmx[:, g % 2, :], mx[:, g % 2, :], -(HD ** -0.5), None, ALU.mult).then_inc(at_nm, 1)

            def normalise(g):
                b, k, q = GROUPS[g]
                n = (q + 1) * P
                dve.wait_ge(at_exp, 4 * (g + 1))
                step(nc.vector.reciprocal(rsum[:, g % 2, :], rsum[:, g % 2, :]))
                for h in range(HB):
                    last = nc.vector.tensor_scalar(pr[g % 2][:, h, 0:n], pr[g % 2][:, h, 0:n], rsum[:, g % 2, h:h + 1],
                                                   None, ALU.mult)
                last.then_inc(at_p, 1)

            def heads_out(g):
                b, k, q = GROUPS[g]
                dve.wait_ge(at_pv, g + 1)
                nc.vector.tensor_copy(oT[:, k, b * T:(b + 1) * T], ps[:, 6 + (g // QT_N) % 2, :]).then_inc(at_o, 1)

            row_max(0)
            for g in range(len(GROUPS)):
                normalise(g)
                if g + 1 < len(GROUPS):
                    row_max(g + 1)
                if g % QT_N == 0 and g:
                    heads_out(g - 1)
            heads_out(len(GROUPS) - 1)
            for t in range(NT):
                dve.wait_ge(wo_mm, t + 1)
                nc.vector.tensor_tensor(xres[:, t, :], xres[:, t, :], ps[:, t, :], ALU.add).then_inc(wo_x, 1)
            dve.wait_ge(wo_x, NT)

            layernorm_stats(1)
            dve.wait_ge(rc_al, 2)
            step(nc.vector.tensor_scalar(colb[:, 4:8], colb[:, 4:8], -1.0, None, ALU.mult))
            step(nc.vector.tensor_tensor(colb[:, 0:4], cols[:, COL_BP:COL_BP + 4], cols[:, COL_DB:COL_DB + 4], ALU.add))
            layernorm_apply(1)

            def bank4(m, c):
                return ps[:, 4 * m + 2 * c:4 * m + 2 * c + 2, :].rearrange("p a n -> p (a n)")

            def tt(o, a, b, op):
                step(nc.vector.tensor_tensor(o, a, b, op))

            for pair in range(2):
                dve.wait_ge(rc_mm, 4 * pair + 1)
                for c in range(2):
                    nb = 2 * pair + c
                    last = nc.vector.tensor_scalar(t1[:, c, :], bank4(0, c), colb[:, nb:nb + 1], 20.0, ALU.add, ALU.min)
                last.then_inc(rc_cap, 1)
                dve.wait_ge(rc_sp, 2 * pair + 2)
                for c in range(2):
                    nb = 2 * pair + c
                    last = nc.vector.scalar_tensor_tensor(out=t1[:, c, :], in0=bank4(0, c), scalar=colb[:, nb:nb + 1],
                                                          in1=t1[:, c, :], op0=ALU.add, op1=ALU.max)
                last.then_inc(rc_delta, 1)
                dve.wait_ge(rc_a, 2 * pair + 2)
                step(nc.vector.tensor_scalar(rA, rA, 1.0 - 1e-4, None, ALU.min))
                dve.wait_ge(rc_th, 4 * pair + 2)
                tt(t2, rB, rB, ALU.mult)
                dve.wait_ge(rc_th, 4 * pair + 4)
                tt(t3, rC, rC, ALU.mult)
                tt(t1, rA, rA, ALU.mult)
                tt(t1, t1, t3, ALU.add)
                tt(t3, t1, t2, ALU.subtract)
                tt(t1, t1, t2, ALU.add)
                tt(t2, rA, rB, ALU.mult)
                tt(t2, t2, t2, ALU.mult)
                tt(t3, t3, t3, ALU.mult)
                nc.vector.scalar_tensor_tensor(out=t3, in0=t2, scalar=4.0, in1=t3, op0=ALU.mult, op1=ALU.add).then_inc(rc_disc, 1)
                dve.wait_ge(rc_mm, 4 * pair + 4)
                for c in range(2):
                    last = nc.vector.tensor_copy(rU[:, c, :], bank4(1, c))
                last.then_inc(rc_free, 1)
                dve.wait_ge(rc_free, pair + 1)
                tt(rB, rB, rU, ALU.mult)
                dve.wait_ge(rc_sq1, pair + 1)
                nc.vector.tensor_tensor(t1, t1, t3, ALU.add).then_inc(rc_lam, 1)
                dve.wait_ge(rc_sq2, pair + 1)
                step(nc.vector.tensor_scalar(t1, t1, 1.0, None, ALU.max))
                step(nc.vector.reciprocal(t1, t1))
                nc.vector.tensor_tensor(rA, rA, t1, ALU.mult)
                nc.vector.tensor_tensor(rB, rB, t1, ALU.mult)
                tt(rC, rC, t1, ALU.mult)
                for c in range(2):
                    for b in range(B):
                        last = nc.vector.tensor_tensor_scan(t2[:, c, b * T:(b + 1) * T], rA[:, c, b * T:(b + 1) * T],
                                                            rB[:, c, b * T:(b + 1) * T], 0.0, ALU.mult, ALU.add)
                        nc.vector.memset(yh[:, 2 * pair + c, b * T:b * T + 1], 0.0)
                step(last)
                for c in range(2):
                    for b in range(B):
                        last = nc.vector.tensor_tensor(yh[:, 2 * pair + c, b * T + 1:(b + 1) * T], rC[:, c, b * T + 1:(b + 1) * T],
                                                       t2[:, c, b * T:(b + 1) * T - 1], ALU.mult)
                last.then_inc(rc_y, 1)
                dve.wait_ge(rc_y, pair + 1)
            for t in range(NT):
                dve.wait_ge(ro_mm, t + 1)
                nc.vector.scalar_tensor_tensor(out=xres[:, t, :], in0=ps[:, t, :], scalar=spec[:, 9:10],
                                               in1=xres[:, t, :], op0=ALU.mult, op1=ALU.add).then_inc(ro_x, 1)
            dve.wait_ge(ro_x, NT)

            layernorm_stats(2)
            layernorm_apply(2)
            dve.wait_ge(rt_lg, 1)
            nc.vector.tensor_copy(lg[:, :, :], ps[:, 7, 0:NT * E].rearrange("p (t e) -> p t e", t=NT)).then_inc(rt_lgs, 1)
            dve.wait_ge(rt_lgs, 1)
            for t in range(NT):
                last = nc.vector.max(top8[:, t, :], lg[:, t, :])
            last.then_inc(rt_max, 1)
            dve.wait_ge(rt_max, 1)
            for t in range(NT):
                last = nc.vector.max_index(idx8[:, t, :], top8[:, t, :], lg[:, t, :])
            step(last)
            step(nc.vector.tensor_copy(idxf[:, :], idx8[:, :, 0]))
            iota = consts[:, C_IOTA:C_IOTA + E]
            for t in range(NT):
                last = nc.vector.tensor_scalar(oh[:, t, :], iota, idxf[:, t:t + 1], None, ALU.is_equal)
            step(last)
            nc.vector.tensor_copy(ohb[:, :, :], oh[:, :, :]).then_inc(rt_oh, 1)
            dve.wait_ge(rt_rank, 1)
            step(nc.vector.tensor_scalar(ecnti[:, :], ps[:, 6, NT * E:NT * E + E], float(CAP - 1), None, ALU.add))
            step(nc.vector.tensor_scalar(ecnti[:, :], ecnti[:, :], CAP.bit_length() - 1, None, ALU.logical_shift_right))
            step(nc.vector.tensor_copy(ecnt[:, 0, :], ecnti[:, :]))
            step(nc.vector.tensor_scalar(ecnt[:, 0, :], ecnt[:, 0, :], -1.0, 0.0, ALU.add, ALU.max))
            step(nc.vector.tensor_tensor_scan(ecnt[:, 1, :], ones32[:, 0:E], ecnt[:, 0, :], 0.0, ALU.mult, ALU.add))
            step(nc.vector.tensor_tensor(ecnt[:, 2, :], ecnt[:, 1, :], ecnt[:, 0, :], ALU.subtract))
            step(nc.vector.tensor_tensor(lg[:, :, :], oh[:, :, :], ps[:, 6, 0:NT * E].rearrange("p (t e) -> p t e", t=NT), ALU.mult))
            step(nc.vector.tensor_reduce(pos[:, 0, :], lg[:, :, :], AX.X, ALU.add))
            step(nc.vector.tensor_tensor(lg[:, :, :], oh[:, :, :],
                                         ecnt[:, 2:3, :].broadcast_to([P, NT, E]), ALU.mult))
            step(nc.vector.tensor_reduce(pos[:, 1, :], lg[:, :, :], AX.X, ALU.add))
            step(nc.vector.tensor_scalar(pos[:, 2, :], idxf[:, :], float(CAP), None, ALU.mult))
            step(nc.vector.tensor_scalar(pos[:, 3, :], pos[:, 1, :], float(CAP), float(CAP * (E - 1)), ALU.mult, ALU.add))
            step(nc.vector.tensor_tensor(pos[:, 3, :], pos[:, 3, :], pos[:, 2, :], ALU.subtract))
            step(nc.vector.tensor_scalar(pos[:, 4, :], pos[:, 0, :], float(CAP), None, ALU.is_ge))
            step(nc.vector.tensor_tensor(pos[:, 3, :], pos[:, 3, :], pos[:, 4, :], ALU.mult))
            step(nc.vector.tensor_tensor(pos[:, 2, :], pos[:, 2, :], pos[:, 3, :], ALU.add))
            nc.vector.tensor_tensor(slot[:, :], pos[:, 0, :], pos[:, 2, :], ALU.add).then_inc(rt_slot, 1)
            for o in range(XTRA):
                last = nc.vector.tensor_scalar(ovl[:, o, :], ecnt[:, 1, :], float(o), None, ALU.is_le)
            step(last)
            step(nc.vector.tensor_reduce(ovs[:, 0:XTRA], ovl[:, :, :], AX.X, ALU.add))
            step(nc.vector.tensor_scalar(ovs[:, 0:XTRA], ovs[:, 0:XTRA], float(E - 1), None, ALU.min))
            step(nc.vector.tensor_copy(ovs[:, XTRA:XTRA + 1], ecnt[:, 1, E - 1:E]))
            nc.vector.tensor_copy(ovi[:, :], ovs[:, :]).then_inc(rt_tab, 1)
            dve.wait_ge(rt_sig, 1)
            step(nc.vector.tensor_tensor(score[:, :], score[:, :], rstd[:, :], ALU.mult))
            for t in range(NT):
                if t >= 2:
                    dve.wait_ge(rt_sc, t - 1)
                nc.vector.tensor_scalar(xsc[t % 2], xres[:, t, :], mv[:, t, 0:1], score[:, t:t + 1],
                                        ALU.subtract, ALU.mult).then_inc(rt_xs, 1)
            for c in range(I // P):
                for b in range(B):
                    n = c * B + b
                    dve.wait_ge(sh_silu, n + 1)
                    dve.wait_ge(sh_gu, 2 * n + 2)
                    nc.vector.tensor_tensor(hsT[:, c, b * T:(b + 1) * T], gtmp[n % 2], ps[:, 2 * (n % 3) + 1, :],
                                            ALU.mult).then_inc(sh_h, 1)
            dve.wait_ge(rt_xs, NT)
            for t in range(NT):
                dve.wait_ge(sh_y, t + 1)
                nc.vector.tensor_tensor(xres[:, t, :], xres[:, t, :], ps[:, 6 + t % 2, :], ALU.add).then_inc(sh_x, 1)

            with dve.Fori(0, E // 2) as i:
                for j in range(2):
                    e = i * 2 + j
                    dve.wait_ge(ex_silu, e + 1)
                    dve.wait_ge(ex_u, e + 2)
                    nc.vector.tensor_tensor(he[j], ge[j], ps[:, 2 * j + 1, :], ALU.mult).then_inc(ex_h, 1)
                    dve.wait_ge(ex_ht, e + 1)
                    nc.vector.tensor_copy(heT[j], ps[:, 5, :]).then_inc(ex_hT, 1)

            dve.wait_ge(rt_tab, 1)
            extra = dve.value_load(ovi[0:1, XTRA:XTRA + 1], min_val=0, max_val=XTRA)
            with dve.If(extra > 0):
                with dve.Fori(0, extra) as o:
                    dve.wait_ge(ov_silu, o + 1)
                    nc.vector.tensor_tensor(he[0], ge[0], ps[:, 1, :], ALU.mult).then_inc(ov_h, 1)
                    dve.wait_ge(ov_ht, o + 1)
                    nc.vector.tensor_copy(heT[0], ps[:, 5, :]).then_inc(ov_hT, 1)

            dve.wait_ge(sh_x, NT)
            for t in range(NT):
                dve.wait_ge(gat[t % 4], 16 * (t // 4 + 1))
                nc.vector.tensor_tensor(fin[t % 4], fin[t % 4], xres[:, t, :], ALU.add).then_inc(fin_add, 1)

        @block.tensor
        def _(pe):
            mm = nc.tensor.matmul

            def gram(banks, w):
                for r in range(KD):
                    for k in range(KD):
                        last = mm(ps[:, banks + r, :], w[:, k, r * P:(r + 1) * P], w[:, k, :], start=(k == 0), stop=(k == KD - 1))
                return last

            pe.wait_ge(sp_conv, 2)
            for s in range(5):
                if s:
                    pe.wait_ge(sp_ev0, s)
                gram(0, spp[0][s % 2]).then_inc(sp_sq, 1)
                if s:
                    pe.wait_ge(sp_ev1, s)
                gram(4, spp[1][s % 2]).then_inc(sp_sq, 1)
            pe.wait_ge(zeroed, 1)
            pe.wait_ge(sp_sum, 2)
            mm(ps[:, 0, 0:2], ones32[:, :], spec[:, 0:2], start=True, stop=True).then_inc(sp_tot, 1)
            pe.wait_ge(sp_flag, 1)
            general = pe.value_load(flag[0:1, 0:1], min_val=0, max_val=1)
            with pe.If(general > 0):
                for m in range(2):
                    base = m * (GENERAL_STEPS + 2)
                    if m:
                        pe.wait_ge(gp_nrm, base)
                    gram(0, spw[m]).then_inc(gp_mm, 1)
                    pe.wait_ge(gp_ssq, 3 * base + 1)
                    mm(ps[:, 4, 0:1], ones32[:, :], spec[:, 4:5], start=True, stop=True).then_inc(gp_tot, 1)
                    with pe.Fori(0, GENERAL_STEPS) as i:
                        pe.wait_ge(gp_nrm, i + (base + 1))
                        gram(0, g_p).then_inc(gp_mm, 1)
                        pe.wait_ge(gp_ssq, i * 3 + (3 * base + 4))
                        mm(ps[:, 4, 0:1], ones32[:, :], spec[:, 4:5], start=True, stop=True).then_inc(gp_tot, 1)
                    pe.wait_ge(gp_a, m + 1)
                    pe.wait_ge(gp_nrm, base + GENERAL_STEPS + 1)
                    for r in range(KD):
                        for k in range(KD):
                            last = mm(ps[:, r, :], g_a[:, k, r * P:(r + 1) * P], g_p[:, k, :], start=(k == 0), stop=(k == KD - 1))
                    last.then_inc(gp_mm, 1)
                    pe.wait_ge(gp_ssq, 3 * (base + GENERAL_STEPS + 1) + 2)
                    mm(ps[:, 4, 0:1], ones32[:, :], spec[:, 4:5], start=True, stop=True)
                    mm(ps[:, 4, 1:2], ones32[:, :], spec[:, 13:14], start=True, stop=True).then_inc(gp_tot, 1)

            def product(dst, lhs, rhs, chunks=KD):
                for k in range(chunks):
                    last = mm(dst, lhs(k), rhs(k), start=(k == 0), stop=(k == chunks - 1))
                return last

            def transposes(n):
                for t in range(NT):
                    pe.wait_ge(ln_xn, n * NT + t + 1)
                    if t >= 2:
                        pe.wait_ge(ln_xT, n * NT + t - 1)
                    for k in range(KD):
                        last = mm(ps[:, t % 2, k * P:(k + 1) * P], xn[t % 2][:, k * P:(k + 1) * P], ident,
                                  start=True, stop=True, is_transpose=True)
                    last.then_inc(ln_tr, 1)

            def project(n):
                kind, a, b = PJ[n]
                if n >= 6:
                    pe.wait_ge(*PJ_EV[n - 6])
                bank = ps[:, 2 + n % 6, :]
                if kind == "k":
                    last = product(bank, lambda k: wk_s[:, k, a * P:(a + 1) * P], lambda k: cT[:, k, b * T:(b + 1) * T])
                elif kind == "v":
                    last = product(bank, lambda k: cT[:, k, a * P:(a + 1) * P], lambda k: wv_s[:, k, :])
                else:
                    last = product(bank, lambda k: wq_s[:, k, a * P:(a + 1) * P], lambda k: xT[:, k, b * T:(b + 1) * T])
                last.then_inc(pj_mm, 1)

            pe.wait_ge(ld_ctx, 16)
            pe.wait_ge(ld_wk, 16)
            for n in range(N_K):
                project(n)
            pe.wait_ge(ld_wv, 16)
            for n in range(N_K, N_K + NT):
                project(n)
            pe.wait_ge(ld_const, 48)
            transposes(0)
            pe.wait_ge(ld_wq, 16)
            pe.wait_ge(ln_xT, NT)
            for n in range(N_K + NT, len(PJ)):
                project(n)

            def scores(g):
                b, k, q = GROUPS[g]
                n = (q + 1) * P
                if g:
                    pe.wait_ge(at_exp, 4 * g)
                for h in range(HB):
                    hp = slice(HD * h, HD * h + HD)
                    last = mm(ps[:, h, 0:n], qT[hp, k, b * T + q * P:b * T + (q + 1) * P], kT[hp, k, b * T:b * T + n],
                              start=True, stop=True)
                last.then_inc(at_s, 1)

            def probs_transposed(g):
                b, k, q = GROUPS[g]
                pe.wait_ge(at_p, g + 1)
                for h in range(HB):
                    if 4 * g + h >= 2:
                        pe.wait_ge(at_ev, 4 * g + h - 1)
                    for c in range(q + 1):
                        last = mm(ps[:, 4 + h % 2, c * P:(c + 1) * P], pr[g % 2][:, h, c * P:(c + 1) * P], ident,
                                  start=True, stop=True, is_transpose=True)
                    last.then_inc(at_tr, 1)

            def values(g):
                b, k, q = GROUPS[g]
                pe.wait_ge(at_ev, 4 * (g + 1))
                if q == 0 and g >= 2 * QT_N:
                    pe.wait_ge(at_o, g // QT_N - 1)
                for c in range(q + 1):
                    for h in range(HB):
                        last = mm(ps[HD * h:HD * h + HD, 6 + (g // QT_N) % 2, q * P:(q + 1) * P],
                                  vv[:, b * QT_N + c, k * P + HD * h:k * P + HD * h + HD],
                                  pT[g % 2][:, h, c * P:(c + 1) * P], start=(c == 0), stop=(c == q))
                last.then_inc(at_pv, 1)

            pe.wait_ge(pj_act, N_K + N_Q)
            pe.wait_ge(pj_dve, NT)
            scores(0)
            for g in range(len(GROUPS)):
                if g + 1 < len(GROUPS):
                    scores(g + 1)
                probs_transposed(g)
                values(g)
            pe.wait_ge(ld_wo, 16)
            pe.wait_ge(at_o, B * KD)
            for t in range(NT):
                product(ps[:, t, :], lambda k: oT[:, k, t * P:(t + 1) * P], lambda k: wo_s[:, k, :]).then_inc(wo_mm, 1)

            transposes(1)
            pe.wait_ge(ln_xT, 2 * NT)
            pe.wait_ge(ld_rec, 48)
            for pair in range(2):
                for q in range(4):
                    if q == 0 and pair:
                        pe.wait_ge(rc_th, 4)
                    elif q == 1 and pair:
                        pe.wait_ge(rc_free, 1)
                    elif q == 2:
                        pe.wait_ge(rc_delta, pair + 1)
                    elif q == 3:
                        pe.wait_ge(rc_th, 4 * pair + 2)
                    for c in range(2):
                        nb = 2 * pair + c
                        w = (lambda k: wp_s[:, k, NCH * q + nb * P:NCH * q + (nb + 1) * P]) if q < 3 else (
                            lambda k: win_s[:, k, nb * P:(nb + 1) * P])
                        for b in range(B):
                            last = product(ps[:, 4 * (q % 2) + 2 * c + b, :], w, lambda k: xT[:, k, b * T:(b + 1) * T])
                    last.then_inc(rc_mm, 1)
            pe.wait_ge(rc_y, 2)
            for t in range(NT):
                product(ps[:, t, :], lambda k: yh[:, k, t * P:(t + 1) * P], lambda k: wout_s[:, k, :]).then_inc(ro_mm, 1)

            transposes(2)
            pe.wait_ge(ln_xT, 3 * NT)
            pe.wait_ge(ld_gw, 16)
            for t in range(NT):
                last = product(ps[:, 7, t * E:(t + 1) * E], lambda k: xT[:, k, t * P:(t + 1) * P], lambda k: gw[:, k, :])
            last.then_inc(rt_lg, 1)

            def ranks():
                pe.wait_ge(rt_oh, 1)
                pe.wait_ge(ready_c, 1)
                for t in range(NT):
                    for j in range(t):
                        mm(ps[:, 6, t * E:(t + 1) * E], onesb[:, :], ohb[:, j, :], start=(j == 0), stop=False)
                    mm(ps[:, 6, t * E:(t + 1) * E], trib[:, :], ohb[:, t, :], start=(t == 0), stop=True)
                product(ps[:, 6, NT * E:NT * E + E], lambda k: onesb[:, :], lambda k: ohb[:, k, :], NT).then_inc(rt_rank, 1)

            pe.wait_ge(ld_gate[0], 16)
            pe.wait_ge(ld_up[0], 16)
            for c in range(I // P):
                for b in range(B):
                    n = c * B + b
                    if n == 3:
                        ranks()
                    if n >= 3:
                        pe.wait_ge(sh_h, n - 2)
                    for w, bank in ((w_gate(0), 2 * (n % 3)), (w_up(0), 2 * (n % 3) + 1)):
                        product(ps[:, bank, :], lambda k: w[:, k, c * P:(c + 1) * P], lambda k: xT[:, k, b * T:(b + 1) * T]).then_inc(sh_gu, 1)
            pe.wait_ge(sh_h, B * I // P)
            pe.sem_inc(ex_u, 1)
            pe.wait_ge(ld_down[0], 16)
            pe.wait_ge(rt_slot, 1)
            for t in range(NT):
                if t >= 2:
                    pe.wait_ge(sh_x, t - 1)
                product(ps[:, 6 + t % 2, :], lambda k: hsT[:, k, t * P:(t + 1) * P], lambda k: w_down(0)[:, k, :], I // P).then_inc(sh_y, 1)
            pe.wait_ge(sh_x, NT)
            pe.sem_inc(ex_y, 1)

            def tile_x():
                for k in range(KD):
                    last = mm(ps[:, 4, k * P:(k + 1) * P], xe[:, k * P:(k + 1) * P], ident, start=True, stop=True,
                              is_transpose=True)
                return last

            def tile_up(j, w, bank):
                for k in range(KD):
                    for half in range(2):
                        last = mm(ps[CAP * half:CAP * half + CAP, bank, :], xeT[:, k, j * CAP:(j + 1) * CAP], w[:, k, half * 512:(half + 1) * 512],
                                  start=(k == 0), stop=(k == KD - 1))
                return last

            def tile_h(j):
                for c in range(4):
                    last = mm(ps[:, 5, c * P:(c + 1) * P], he[j][:, c * P:(c + 1) * P], ident, start=True, stop=True,
                              is_transpose=True)
                return last

            def tile_down(j, w, bank):
                for c in range(I // P):
                    lhs = heT[j][:, (c % 4) * P + (c // 4) * CAP:(c % 4) * P + (c // 4) * CAP + CAP]
                    for half in range(2):
                        last = mm(ps[CAP * half:CAP * half + CAP, bank, 0:256], lhs, w[:, c, half * 256:(half + 1) * 256],
                                  start=(c == 0), stop=(c == I // P - 1))
                return last

            with pe.Fori(0, E // 2) as i:
                for j in range(2):
                    s, e = 1 - j, i * 2 + j
                    if j == 0:
                        pe.wait_ge(ex_x, i * 16 + 16)
                        tile_x().then_inc(ex_tr, 1)
                        pe.wait_ge(ex_xT, i + 1)
                    pe.wait_ge(ld_gate[s], i * 16 + 16 * (j + 1))
                    tile_up(j, w_gate(s), 2 * j).then_inc(ex_g, 1)
                    pe.wait_ge(ld_up[s], i * 16 + 16 * (j + 1))
                    tile_up(j, w_up(s), 2 * j + 1).then_inc(ex_u, 1)
                    pe.wait_ge(ex_h, e + 1)
                    pe.wait_ge(ex_hT, e)
                    tile_h(j).then_inc(ex_ht, 1)
                    pe.wait_ge(ex_hT, e + 1)
                    pe.wait_ge(ld_down[s], i * 16 + 16 * (j + 1))
                    pe.wait_ge(ex_ye, i * 2)
                    tile_down(j, w_down(s), 6 + j).then_inc(ex_y, 1)

            pe.wait_ge(rt_tab, 1)
            extra = pe.value_load(ovi[0:1, XTRA:XTRA + 1], min_val=0, max_val=XTRA)
            with pe.If(extra > 0):
                pe.wait_ge(ex_ye, E)
                with pe.Fori(0, extra) as o:
                    pe.wait_ge(ov_x, o * 16 + 16)
                    pe.wait_ge(ov_ye, o)
                    tile_x().then_inc(ov_tr, 1)
                    pe.wait_ge(ov_xT, o + 1)
                    pe.wait_ge(ov_w, o * 48 + 48)
                    tile_up(0, w_gate(1), 0)
                    tile_up(0, w_up(1), 1).then_inc(ov_gu, 1)
                    pe.wait_ge(ov_h, o + 1)
                    tile_h(0).then_inc(ov_ht, 1)
                    pe.wait_ge(ov_hT, o + 1)
                    tile_down(0, w_down(1), 6).then_inc(ov_y, 1)


def kernel(x, ctx_1024, L0_xattn_Wq, L0_xattn_bq, L0_xattn_Wk, L0_xattn_bk, L0_xattn_Wv, L0_xattn_bv, L0_xattn_Wo,
           L0_xattn_bo, L0_attn_W_in, L0_attn_W_out, L0_attn_Wp, L0_attn_bp, L0_attn_alpha_log, L0_attn_delta_bias,
           L0_attn_log_gamma, L0_ffn_gate_w, L0_ffn_shared_gate_w, L0_ffn_shared_up_w, L0_ffn_shared_down_w,
           L0_ffn_routed_gate_w, L0_ffn_routed_up_w, L0_ffn_routed_down_w):
    import numpy as np
    import concourse.bacc as bacc
    from concourse.bass_utils import run_bass_kernel_spmd

    def col(v):
        return np.asarray(v).reshape(-1, P).T

    consts = np.zeros((P, CONSTS), np.float32)
    consts[:, C_IDENT:C_IDENT + P] = np.eye(P)
    consts[:, C_MASK:C_MASK + P] = np.triu(np.full((P, P), MASKED), 1)
    consts[:, C_IOTA:C_IOTA + E] = np.arange(E)

    columns = np.concatenate([col(L0_xattn_bq), col(L0_xattn_bk), col(L0_attn_bp), col(L0_attn_delta_bias),
                              col(L0_attn_alpha_log), np.broadcast_to(np.asarray(L0_attn_log_gamma), (P, 1))], axis=1)
    rows = np.stack([np.broadcast_to(np.asarray(L0_xattn_bv), (P, D)), np.broadcast_to(np.asarray(L0_xattn_bo), (P, D))], axis=1)
    arrays = {
        "x": np.asarray(x).reshape(TOK, D),
        "ctxT": np.asarray(ctx_1024)[:, :T, :].transpose(2, 0, 1).reshape(D, TOK),
        "Wq": L0_xattn_Wq, "Wk": L0_xattn_Wk, "Wv": L0_xattn_Wv, "Wo": L0_xattn_Wo,
        "WinT": np.asarray(L0_attn_W_in).T, "WoutT": np.asarray(L0_attn_W_out).T, "WpT": np.asarray(L0_attn_Wp).T,
        "gate_w": L0_ffn_gate_w, "sg": L0_ffn_shared_gate_w, "su": L0_ffn_shared_up_w, "sd": L0_ffn_shared_down_w,
        "rg": L0_ffn_routed_gate_w, "ru": L0_ffn_routed_up_w, "rd": L0_ffn_routed_down_w,
        "cols": columns, "rows": rows, "consts": consts,
    }
    arrays = {"in_" + n: np.ascontiguousarray(a) for n, a in arrays.items()}
    nc = bacc.Bacc("TRN2", target_bir_lowering=False, num_devices=1)
    aps = [nc.dram_tensor(n, a.shape, mybir.dt.from_np(a.dtype), kind="ExternalInput").ap() for n, a in arrays.items()]
    out = nc.dram_tensor("out_0", (TOK, D), mybir.dt.float32, kind="ExternalOutput").ap()
    perceiver_layer(nc, *aps, out)
    r = run_bass_kernel_spmd(nc, [arrays], core_ids=[0])
    return r.results[0]["out_0"].reshape(B, T, D)
```

```python
import concourse.bass as bass
from concourse import mybir
from contextlib import ExitStack

B, T, D = 2, 512, 512
TOK = B * T
H, HD = 16, 32
NCH = 512
E, I = 32, 1024
P = 128
KD = D // P
NT = TOK // P
QT_N = T // P
HB = P // HD
CAP = 64
XTRA = TOK // CAP - 1
SLOTS = (E + XTRA + 1) * CAP
WORDS = 12288
GU = KD * I

COL_BQ, COL_BK, COL_BP, COL_DB, COL_AL, COL_LG = 0, 4, 8, 20, 24, 28
COLS = 29
C_IDENT, C_MASK, C_IOTA = 0, 128, 256
CONSTS = 288
MASKED = -1.0e30


def perceiver_layer(nc, x, ctxT, Wq, Wk, Wv, Wo, WinT, WoutT, WpT, gate_w, sg, su, sd, rg, ru, rd,
                    cols_in, rows_in, consts_in, out):
    f32, f32r, bf16, i32, u32 = (mybir.dt.float32, mybir.dt.float32r, mybir.dt.bfloat16, mybir.dt.int32,
                                 mybir.dt.uint32)
    ALU, ACT, AX = mybir.AluOpType, mybir.ActivationFunctionType, mybir.AxisListType

    kq_parts = nc.dram_tensor("kq_parts", [2, 2, 2, HB, HD, T], mybir.dt.float32, kind="Internal").ap()
    xT_tiles = nc.dram_tensor("xT_tiles", [NT, P, D], f32, kind="Internal").ap()
    xs_sorted = nc.dram_tensor("xs_sorted", [SLOTS, D], f32, kind="Internal").ap()
    ys_sorted = nc.dram_tensor("ys_sorted", [SLOTS, D], f32, kind="Internal").ap()

    with ExitStack() as ctx:
        def sb(name, shape, dt=f32):
            return ctx.enter_context(nc.sbuf_tensor(name, shape, dt))

        def sem(name):
            return ctx.enter_context(nc.semaphore(name))

        FENCE, BASE = 49152, 16512
        fence = sb("fence", [P, FENCE])

        def place(name, off, shape, dt=f32):
            words = 1
            for n in shape:
                words *= n
            words = words // 2 if dt == bf16 else words
            assert off + words <= FENCE
            t = nc.alloc_sbuf_tensor_at(name, [P, *shape], dt, offset=BASE + 4 * off)
            return t[(slice(None),) * (len(shape) + 1)]

        consts = sb("consts", [P, CONSTS])
        cols = sb("cols", [P, COLS])
        rows = sb("rows", [P, 2, D])
        ones32 = sb("ones32", [P, P])
        onesb = sb("onesb", [P, P], bf16)
        trib = sb("trib", [P, P], bf16)
        eps = sb("eps", [P, 3])
        bnst = sb("bnst", [P, NT, 6])
        mv = sb("mv", [P, NT, 2])
        rstd = sb("rstd", [P, NT])
        colb = sb("colb", [P, 8])
        spec = sb("spec", [P, 16])
        zero = sb("zero", [P, D])
        flag = sb("flag", [P, 1], i32)
        mx = sb("mx", [P, 3, 2])
        nmx = sb("nmx", [P, 3, 2])
        rsum = sb("rsum", [P, 3, 2])
        identb = sb("identb", [P, P], bf16)
        maskb = sb("maskb", [P, P], bf16)
        gw = sb("gw", [P, KD, E])
        ohb = sb("ohb", [P, NT, E], bf16)
        top8 = sb("top8", [P, NT, 8])
        idx8 = sb("idx8", [P, NT, 8], u32)
        idxf = sb("idxf", [P, NT])
        score = sb("score", [P, NT])
        pos = sb("pos", [P, 6, NT])
        slot = sb("slot", [P, NT], i32)
        ecnt = sb("ecnt", [P, 6, E])
        ecnti = sb("ecnti", [P, E], i32)
        ovs = sb("ovs", [P, XTRA + 1])
        ovi = sb("ovi", [P, XTRA + 1], i32)
        ps = ctx.enter_context(nc.psum_tensor("ps", [P, 8, 512], f32))

        ident = consts[:, C_IDENT:C_IDENT + P]
        mask = consts[:, C_MASK:C_MASK + P]

        xres = place("xres", 0, [NT, D])
        xT = place("xT", 4096, [KD, TOK])
        xn = [place(f"xn{j}", 32768 + 512 * j, [D]) for j in range(2)]
        spw = [place(f"spw{m}", 38912 + 2048 * m, [KD, 512]) for m in range(2)]
        spp = [[place(f"spp{m}{j}", 43008 + 2048 * m + 1024 * j, [KD, 512], bf16) for j in range(2)] for m in range(2)]
        g_a, g_p, g_junk = (place(n, 30720 + 2048 * j, [KD, 512]) for j, n in enumerate(("g_a", "g_p", "g_junk")))
        cT = place("cT", 8192, [KD, TOK])
        wk_s, wq_s, wv_s = (place(n, 12288 + 2048 * j, [KD, D]) for j, n in enumerate(("wk_s", "wq_s", "wv_s")))
        vv = place("vv", 18432, [NT, D])
        oT = place("oT", 22528, [KD, TOK])
        wo_s = place("wo_s", 26624, [KD, D])
        parts = {n: place(n, 28672 + 512 * j, [T], f32r) for j, n in enumerate(("k_hi", "k_lo", "q_hi", "q_lo"))}
        kst = [place(f"kst{j}", 30720 + 4096 * j, [HB, T], f32r) for j in range(2)]
        qst = [place(f"qst{j}", 32768 + 4096 * j, [HB, T], f32r) for j in range(2)]
        pr = [place(f"pr{j}", 38912 + 1024 * j, [2, T]) for j in range(3)]
        pT = [place(f"pT{j}", 41984 + 1024 * j, [2, T]) for j in range(4)]
        wp_s = place("wp_s", 8192, [KD, 3 * NCH])
        win_s = place("win_s", 14336, [KD, NCH])
        wout_s = place("wout_s", 16384, [KD, D])
        rA, rB, rC, rZ, t1, t2, t3 = (place(n, 18432 + 2048 * j, [2, TOK])
                                      for j, n in enumerate(("rA", "rB", "rC", "rZ", "t1", "t2", "t3")))
        yh = place("yh", 32768, [4, TOK])
        w_shared = place("w_shared", 36864, [WORDS])
        ring = [place(f"ring{j}", 8192 + WORDS * j, [WORDS]) for j in range(2)]
        xe = [place(f"xe{j}", (4096, 34304)[j], [D]) for j in range(2)]
        xeT = place("xeT", 4608, [KD, P])
        ge = place("ge", 5120, [512])
        he = place("he", 5632, [512])
        ye = [place(f"ye{j}", 6144 + 256 * j, [256]) for j in range(4)]
        sgt = place("sgt", 7168, [512])
        hs = place("hs", 7680, [512])
        xsc = [place(f"xsc{t}", 32768 + 512 * (t % 6), [D]) for t in range(6)]
        ovl = place("ovl", 35840, [XTRA, E])
        oh = place("oh", 36352, [NT, E])
        lg = place("lg", 36608, [NT, E])
        heT = place("heT", 32768, [4, P])
        hsT = place("hsT", 33280, [4, P])
        xsT = place("xsT", 33792, [KD, P])
        xsT_in = place("xsT_in", 34816, [KD, P])
        fin = [place(f"fin{t}", 8192 + 512 * t, [D]) for t in range(NT)]

        def w_gate(w):
            return w[:, 0:GU].rearrange("p (k n) -> p k n", k=KD)

        def w_up(w):
            return w[:, GU:2 * GU].rearrange("p (k n) -> p k n", k=KD)

        def w_down(w):
            return w[:, 2 * GU:3 * GU].rearrange("p (k n) -> p k n", k=I // P)

        ld_spec, ld_const, ld_x, ld_ctx, ld_wk, ld_wv, ld_wq, ld_wo, ld_rec, ld_gw = (
            sem(n) for n in ("ld_spec", "ld_const", "ld_x", "ld_ctx", "ld_wk", "ld_wv", "ld_wq", "ld_wo", "ld_rec", "ld_gw"))
        ld_gate, ld_up, ld_down = ([sem(f"{n}{j}") for j in range(2)] for n in ("ld_gate", "ld_up", "ld_down"))
        zeroed, filled = sem("zeroed"), sem("filled")
        sp_conv, sp_sq, sp_ev0, sp_ev1 = sem("sp_conv"), sem("sp_sq"), sem("sp_ev0"), sem("sp_ev1")
        sp_sum, sp_tot, sp_flag, sp_done = sem("sp_sum"), sem("sp_tot"), sem("sp_flag"), sem("sp_done")
        gp_mm, gp_ev, gp_ssq, gp_tot, gp_rt, gp_nrm, gp_a = (sem(n) for n in ("gp_mm", "gp_ev", "gp_ssq", "gp_tot", "gp_rt", "gp_nrm", "gp_a"))
        lg_exp, ready_c = sem("lg_exp"), sem("ready_c")
        ln_stat, ln_sqrt, ln_xn, ln_tr, ln_xT = (sem(n) for n in ("ln_stat", "ln_sqrt", "ln_xn", "ln_tr", "ln_xT"))
        v_mm, v_out, kq_mm, kq_hi, kq_lo, kq_st, consts_b = (
            sem(n) for n in ("v_mm", "v_out", "kq_mm", "kq_hi", "kq_lo", "kq_st", "consts_b"))
        kq_ld = [sem(f"kq_ld{j}") for j in range(2)]
        at_s, at_nm, at_exp, at_p, at_tr, at_ev0, at_ev1, at_pv, at_o = (
            sem(n) for n in ("at_s", "at_nm", "at_exp", "at_p", "at_tr", "at_ev0", "at_ev1", "at_pv", "at_o"))
        wo_mm, wo_x = sem("wo_mm"), sem("wo_x")
        rc_mm, rc_cap, rc_sp, rc_delta, rc_a, rc_amin, rc_th, rc_sq, rc_d, rc_disc, rc_sq1, rc_lam, rc_sq2, rc_bu, rc_y, rc_al = (
            sem(n) for n in ("rc_mm", "rc_cap", "rc_sp", "rc_delta", "rc_a", "rc_amin", "rc_th", "rc_sq", "rc_d", "rc_disc",
                             "rc_sq1", "rc_lam", "rc_sq2", "rc_bu", "rc_y", "rc_al"))
        ro_mm, ro_x = sem("ro_mm"), sem("ro_x")
        rt_lg, rt_lgs, rt_oh, rt_rank, rt_max, rt_sig, rt_slot, rt_xs, rt_tab = (
            sem(n) for n in ("rt_lg", "rt_lgs", "rt_oh", "rt_rank", "rt_max", "rt_sig", "rt_slot", "rt_xs",
                             "rt_tab"))
        sc_done = [sem(f"sc_done{t}") for t in range(NT)]
        ld_shared, xt_st, xt_ld, xs_cp = sem("ld_shared"), sem("xt_st"), sem("xt_ld"), sem("xs_cp")
        sh_g, sh_u, sh_silu, sh_h, sh_tr, sh_T, sh_y, sh_x = (
            sem(n) for n in ("sh_g", "sh_u", "sh_silu", "sh_h", "sh_tr", "sh_T", "sh_y", "sh_x"))
        ex_tr, ex_xT, ex_g, ex_u, ex_silu, ex_h, ex_ht, ex_hT, ex_y, ex_ye = (
            sem(n) for n in ("ex_tr", "ex_xT", "ex_g", "ex_u", "ex_silu", "ex_h", "ex_ht", "ex_hT", "ex_y", "ex_ye"))
        ex_x = [sem(f"ex_x{j}") for j in range(2)]
        ex_st = [sem(f"ex_st{j}") for j in range(4)]
        ov_w = [sem(f"ov_w{j}") for j in range(3)]
        ov_x, ov_tr, ov_xT, ov_g, ov_u, ov_silu, ov_h, ov_ht, ov_hT, ov_y, ov_ye, ov_st = (
            sem(n) for n in ("ov_x", "ov_tr", "ov_xT", "ov_g", "ov_u", "ov_silu", "ov_h", "ov_ht", "ov_hT", "ov_y",
                             "ov_ye", "ov_st"))
        moe_done = sem("moe_done")
        gat = [sem(f"gat{t}") for t in range(NT)]
        fin_add = sem("fin_add")
        stored = sem("stored")
        dve_own, dve_own2 = sem("dve_own"), sem("dve_own2")

        GENERAL_STEPS = 16
        UNITS = [(b, k) for b in range(B) for k in range(KD)]
        STEPS = [(u, q, hp) for u in range(len(UNITS)) for q in range(QT_N) for hp in range(2)]
        PER_UNIT = 2 * QT_N

        block = ctx.enter_context(nc.Block())

        @block.sync
        def _(sp):
            def kmaj(w):
                return w.rearrange("(k p) n -> p k n", p=P)

            sp.dma_start(spw[0], kmaj(WinT)).then_inc(ld_spec, 16)
            sp.dma_start(spw[1], kmaj(WoutT)).then_inc(ld_spec, 16)
            sp.dma_start(consts[:, :], consts_in).then_inc(ld_const, 16)
            sp.dma_start(cols[:, :], cols_in).then_inc(ld_const, 16)
            sp.dma_start(rows[:, :, :], rows_in).then_inc(ld_const, 16)
            sp.dma_start(cT, kmaj(ctxT)).then_inc(ld_ctx, 16)
            sp.dma_start(wv_s, kmaj(Wv)).then_inc(ld_wv, 16)
            sp.dma_start(wk_s, kmaj(Wk)).then_inc(ld_wk, 16)
            sp.dma_start(xres, x.rearrange("(t p) n -> p t n", p=P)).then_inc(ld_x, 16)
            sp.dma_start(wq_s, kmaj(Wq)).then_inc(ld_wq, 16)
            sp.dma_start(wo_s, kmaj(Wo)).then_inc(ld_wo, 16)
            sp.dma_start(gw[:, :, :], kmaj(gate_w)).then_inc(ld_gw, 16)

            for u in range(len(UNITS)):
                for i, name in enumerate("kq"):
                    sp.wait_ge(kq_lo, 2 * u + i + 1)
                    if u >= 2:
                        sp.wait_ge(at_s, PER_UNIT * (u - 1))
                    for part, sfx in enumerate(("hi", "lo")):
                        sp.dma_start(kq_parts[u % 2, i, part, :, :, :].rearrange("h d n -> (h d) n"),
                                     parts[f"{name}_{sfx}"].bitcast(f32)).then_inc(kq_st, 16)
                    sp.wait_ge(kq_st, 32 * (2 * u + i + 1))
                    dst = (kst, qst)[i][u % 2]
                    for g in range(4):
                        part = g % 2 if i == 0 else g // 2
                        sp.dma_start(dst[HD * g:HD * g + HD, :, :].bitcast(f32),
                                     kq_parts[u % 2, i, part, :, :, :].rearrange("h d n -> d h n")).then_inc(kq_ld[u % 2], 16)
                if u == 1:
                    sp.wait_ge(zeroed, 1)
                    for t in range(SLOTS // P):
                        sp.dma_start(xs_sorted[t * P:(t + 1) * P, :], zero[:, :]).then_inc(filled, 16)
                    for t in range(E * CAP // P, SLOTS // P):
                        sp.dma_start(ys_sorted[t * P:(t + 1) * P, :], zero[:, :]).then_inc(ex_st[t % 4], 16)
            sp.wait_ge(kq_mm, 2 * len(UNITS))
            sp.dma_start(wp_s, kmaj(WpT)).then_inc(ld_rec, 16)
            sp.dma_start(win_s, kmaj(WinT)).then_inc(ld_rec, 16)
            sp.dma_start(wout_s, kmaj(WoutT)).then_inc(ld_rec, 16)
            sp.wait_ge(at_pv, len(UNITS) * QT_N)
            sp.dma_start(w_gate(w_shared), kmaj(sg)).then_inc(ld_shared, 16)
            sp.dma_start(w_up(w_shared), kmaj(su)).then_inc(ld_shared, 16)
            sp.dma_start(w_down(w_shared), kmaj(sd)).then_inc(ld_shared, 16)

            def load_expert(e, j, part):
                w, view, done = ((rg, w_gate, ld_gate), (ru, w_up, ld_up), (rd, w_down, ld_down))[part]
                sp.dma_start(view(ring[j]), w[e, :, :].rearrange("a (k p) n -> p (a k) n", p=P)).then_inc(done[j], 16)

            sp.sem_inc(ex_g, 2)
            sp.sem_inc(ex_u, 2)
            sp.sem_inc(ex_y, 2)
            sp.wait_ge(rc_mm, 8)
            for part in range(2):
                load_expert(slice(0, 1), 0, part)
            sp.wait_ge(ro_mm, NT)
            load_expert(slice(0, 1), 0, 2)
            for part in range(3):
                load_expert(slice(1, 2), 1, part)
            with sp.Fori(0, E // 2 - 1) as i:
                for j in range(2):
                    for part, used in enumerate((ex_g, ex_u, ex_y)):
                        sp.wait_ge(used, i * 2 + j + 3)
                        load_expert(bass.ds(i * 2 + j + 2, 1), j, part)
            sp.wait_ge(rt_tab, 1)
            extra = sp.value_load(ovi[0:1, XTRA:XTRA + 1], min_val=0, max_val=XTRA)
            with sp.If(extra > 0):
                sp.wait_ge(ex_y, E + 1)
                for used in (ov_g, ov_u, ov_y):
                    sp.sem_inc(used, 1)
                with sp.Fori(0, extra) as o:
                    e = sp.value_load(ovi[0:1, bass.ds(o, 1)], min_val=0, max_val=E - 1)
                    for part, (w, view, used) in enumerate(((rg, w_gate, ov_g), (ru, w_up, ov_u), (rd, w_down, ov_y))):
                        sp.wait_ge(used, o + 1)
                        sp.dma_start(view(ring[0]), w[bass.ds(e, 1), :, :].rearrange("a (k p) n -> p (a k) n", p=P)).then_inc(ov_w[part], 16)

        @block.gpsimd
        def _(pool):
            nc.gpsimd.memset(ones32[:, :], 1.0)
            nc.gpsimd.memset(onesb[:, :], 1.0)
            nc.gpsimd.memset(eps[:, 0:1], 1e-5)
            nc.gpsimd.memset(eps[:, 1:2], 1e-12)
            nc.gpsimd.memset(eps[:, 2:3], 1.0)
            nc.gpsimd.memset(zero[:, :], 0.0).then_inc(zeroed, 1)
            pool.wait_ge(zeroed, 1)
            nc.gpsimd.affine_select(out=trib[:, :], in_=onesb[:, :], compare_op=ALU.is_gt, fill=0.0, base=0,
                                    pattern=[[1, P]], channel_multiplier=-1).then_inc(ready_c, 1)

            pool.wait_ge(ld_const, 48)
            nc.gpsimd.tensor_copy(identb[:, :], ident).then_inc(consts_b, 1)
            nc.gpsimd.tensor_copy(maskb[:, :], mask).then_inc(consts_b, 1)

            for pair in range(2):
                pool.wait_ge(rc_sq, 3 * pair + 3)
                nc.gpsimd.tensor_tensor(t1, t1, t3, ALU.add).then_inc(rc_d, 1)
                pool.wait_ge(rc_d, 3 * pair + 1)
                nc.gpsimd.tensor_tensor(t3, t1, t2, ALU.subtract).then_inc(rc_d, 1)
                nc.gpsimd.tensor_tensor(t1, t1, t2, ALU.add).then_inc(rc_d, 1)

            pool.wait_ge(filled, 16 * (SLOTS // P))
            pool.wait_ge(rt_slot, 1)
            for t in range(NT):
                pool.wait_ge(rt_xs, t + 1)
                nc.gpsimd.indirect_dma_start(
                    xs_sorted[:, :], bass.IndirectOffsetOnAxis(ap=slot[:, t:t + 1], axis=0), xsc[t % 6], None,
                ).then_inc(sc_done[t], 16)

            for t in range(NT):
                pool.wait_ge(sc_done[t], 16)
            pool.wait_ge(xt_st, 16 * NT)
            for j in range(2):
                nc.gpsimd.dma_start(xe[j], xs_sorted[j * P:(j + 1) * P, :]).then_inc(ex_x[j], 16)
            nc.gpsimd.dma_start(xsT_in, xT_tiles[0, :, :].rearrange("p (k n) -> p k n", k=KD)).then_inc(xt_ld, 16)
            with pool.Fori(0, E // 4 - 1) as i:
                pool.wait_ge(xs_cp, i + 1)
                nc.gpsimd.dma_start(xsT_in, xT_tiles[bass.ds(i + 1, 1), :, :].rearrange("a p (k n) -> p (a k) n", k=KD)).then_inc(xt_ld, 16)
                for j in range(2):
                    pool.wait_ge(ex_tr, i * 2 + j + 1)
                    nc.gpsimd.dma_start(xe[j], xs_sorted[bass.ds(i * (2 * P) + (j + 2) * P, P), :]).then_inc(ex_x[j], 16)

            pool.wait_ge(rt_tab, 1)
            extra = pool.value_load(ovi[0:1, XTRA:XTRA + 1], min_val=0, max_val=XTRA)
            with pool.If(extra > 0):
                pool.wait_ge(ex_tr, E // 2)
                pool.sem_inc(ov_tr, 1)
                with pool.Fori(0, extra) as o:
                    pool.wait_ge(ov_tr, o + 1)
                    nc.gpsimd.dma_start(xe[0], xs_sorted[bass.ds(o * CAP + E * CAP, P), :]).then_inc(ov_x, 16)

            pool.wait_ge(moe_done, 1)
            for t in range(NT):
                nc.gpsimd.indirect_dma_start(
                    fin[t], None, ys_sorted[:, :], bass.IndirectOffsetOnAxis(ap=slot[:, t:t + 1], axis=0),
                ).then_inc(gat[t], 16)

        @block.scalar
        def _(act):
            act.wait_ge(ld_spec, 32)
            nc.scalar.copy(spp[0][0], spw[0]).then_inc(sp_conv, 1)
            for s in range(4):
                act.wait_ge(sp_sq, 2 * s + 1)
                nc.scalar.copy(spp[0][(s + 1) % 2], ps[:, 0:4, :]).then_inc(sp_ev0, 1)
            for m in range(2):
                act.wait_ge(sp_sq, 9 + m)
                nc.scalar.activation(spp[m][1], ps[:, 4 * m:4 * m + 4, :], ACT.Square,
                                     accum_out=spec[:, m:m + 1]).then_inc(sp_sum, 1)
            act.wait_ge(ld_const, 48)
            nc.scalar.activation(spec[:, 8:9], cols[:, COL_LG:COL_LG + 1], ACT.Exp).then_inc(lg_exp, 1)
            act.wait_ge(sp_flag, 1)
            general = act.value_load(flag[0:1, 0:1], min_val=0, max_val=1)
            with act.If(general > 0):
                for m in range(2):
                    with act.Fori(0, GENERAL_STEPS + 1) as i:
                        n = i + m * (GENERAL_STEPS + 2)
                        act.wait_ge(gp_tot, n + 1)
                        nc.scalar.activation(spec[:, 5:6], ps[:, 4, 0:1], ACT.Sqrt).then_inc(gp_rt, 1)
                    act.wait_ge(gp_nrm, (m + 1) * (GENERAL_STEPS + 2))
                    nc.scalar.activation(spec[:, 5:6], spec[:, 6:7], ACT.Sqrt).then_inc(gp_rt, 1)

            def layernorm_root(n):
                act.wait_ge(ln_stat, n + 1)
                nc.scalar.activation(rstd[:, :], mv[:, :, 1], ACT.Sqrt, bias=eps[:, 0:1]).then_inc(ln_sqrt, 1)

            def transposed_out(n, t):
                act.wait_ge(ln_tr, n * NT + t + 1)
                nc.scalar.copy(xT[:, :, t * P:(t + 1) * P],
                               ps[:, t % 2, :].rearrange("p (k n) -> p k n", k=KD)).then_inc(ln_xT, 1)

            def upper_part(u, i):
                b, k = UNITS[u]
                n = 2 * u + i
                act.wait_ge(kq_mm, n + 1)
                if u:
                    act.wait_ge(kq_st, 32 * (n - 1))
                nc.scalar.activation(parts[("k_hi", "q_hi")[i]], ps[:, 7, :], ACT.Identity,
                                     bias=cols[:, (COL_BK, COL_BQ)[i] + k:(COL_BK, COL_BQ)[i] + k + 1]).then_inc(kq_hi, 1)

            act.wait_ge(ready_c, 1)
            layernorm_root(0)
            for t in range(NT):
                transposed_out(0, t)
            upper_part(0, 0)
            upper_part(0, 1)

            def exps(v):
                u, q, hp = STEPS[v]
                n = (q + 1) * P
                act.wait_ge(at_nm, v + 1)
                if v >= 3:
                    act.wait_ge(at_tr, 2 * (v - 2))
                for h in range(2):
                    nc.scalar.activation(pr[v % 3][:, h, 0:n], ps[:, 2 * (v % 2) + h, 0:n], ACT.Exp,
                                         bias=nmx[:, v % 3, h:h + 1], scale=HD ** -0.5,
                                         accum_out=rsum[:, v % 3, h:h + 1]).then_inc(at_exp, 1)

            def probs_out(v):
                u, q, hp = STEPS[v]
                n = (q + 1) * P
                if v >= 4:
                    act.wait_ge(at_pv, v // 2 - 1)
                act.wait_ge(at_tr, 2 * v + 1)
                nc.scalar.copy(pT[v % 4][:, 0, 0:n], ps[:, 4, 0:n]).then_inc(at_ev0, 1)

            for v in range(len(STEPS)):
                exps(v)
                if v >= 1:
                    probs_out(v - 1)
                u, at_step = divmod(v, PER_UNIT)
                if u + 1 < len(UNITS) and at_step in (2, 5):
                    upper_part(u + 1, (at_step - 2) // 3)
            probs_out(len(STEPS) - 1)

            nc.scalar.activation(colb[:, 4:8], cols[:, COL_AL:COL_AL + 4], ACT.Exp).then_inc(rc_al, 1)
            act.wait_ge(rc_al, 1)
            nc.scalar.activation(colb[:, 4:8], colb[:, 4:8], ACT.Ln, bias=eps[:, 2:3]).then_inc(rc_al, 1)
            act.wait_ge(wo_x, NT)
            layernorm_root(1)
            for t in range(NT):
                transposed_out(1, t)
            def tanh(pair, q, dst):
                act.wait_ge(rc_mm, 4 * pair + q + 1)
                col = COL_BP + NCH // P * (2 if dst is rC else 1) + 2 * pair
                for c in range(2):
                    nc.scalar.activation(dst[:, c, :], ps[:, 4 * (q % 2) + 2 * c:4 * (q % 2) + 2 * c + 2, :].rearrange("p a n -> p (a n)"),
                                         ACT.Tanh, bias=cols[:, col + c:col + c + 1]).then_inc(rc_th, 1)

            for pair in range(2):
                act.wait_ge(rc_cap, pair + 1)
                nc.scalar.activation(t1, t1, ACT.Exp).then_inc(rc_sp, 1)
                act.wait_ge(rc_sp, 2 * pair + 1)
                nc.scalar.activation(t1, t1, ACT.Ln, bias=eps[:, 2:3]).then_inc(rc_sp, 1)
                act.wait_ge(rc_delta, pair + 1)
                for c in range(2):
                    nb = 2 * pair + c
                    nc.scalar.activation(rA[:, c, :], t1[:, c, :], ACT.Exp, scale=colb[:, 4 + nb:5 + nb]).then_inc(rc_a, 1)
                tanh(pair, 1, rC)
                act.wait_ge(rc_amin, pair + 1)
                nc.scalar.activation(t1, rA, ACT.Square).then_inc(rc_sq, 1)
                act.wait_ge(rc_th, 4 * pair + 2)
                nc.scalar.activation(t3, rC, ACT.Square).then_inc(rc_sq, 1)
                tanh(pair, 2, rB)
                act.wait_ge(rc_th, 4 * pair + 4)
                nc.scalar.activation(t2, rB, ACT.Square).then_inc(rc_sq, 1)
                act.wait_ge(rc_d, 3 * pair + 3)
                nc.scalar.activation(t3, t3, ACT.Square).then_inc(rc_sq1, 1)
                act.wait_ge(rc_disc, 2 * pair + 1)
                nc.scalar.activation(t2, t2, ACT.Square, scale=2.0).then_inc(rc_sq1, 1)
                act.wait_ge(rc_disc, 2 * pair + 2)
                nc.scalar.activation(t3, t3, ACT.Sqrt, bias=eps[:, 1:2]).then_inc(rc_sq1, 1)
                act.wait_ge(rc_lam, pair + 1)
                nc.scalar.activation(t1, t1, ACT.Sqrt, bias=eps[:, 1:2], scale=0.5).then_inc(rc_sq2, 1)

            act.wait_ge(ro_x, NT)
            layernorm_root(2)
            for t in range(NT):
                transposed_out(2, t)
                act.wait_ge(ln_xT, 2 * NT + t + 1)
                act.dma_start(xT_tiles[t, :, :].rearrange("p (k n) -> p k n", k=KD), xT[:, :, t * P:(t + 1) * P]).then_inc(xt_st, 16)
            act.wait_ge(rt_max, 1)
            nc.scalar.activation(score[:, :], top8[:, :, 0], ACT.Sigmoid).then_inc(rt_sig, 1)

            act.wait_ge(xt_st, 16 * NT)
            for t in range(NT):
                act.wait_ge(sc_done[t], 16)
            act.sem_inc(ex_ye, 1)
            with act.Fori(0, E // 4) as i:
                for j in range(4):
                    e = i * 4 + j
                    if j == 0:
                        act.wait_ge(xt_ld, i * 16 + 16)
                        nc.scalar.copy(xsT, xsT_in).then_inc(xs_cp, 1)
                    act.wait_ge(ex_g, e + 3)
                    nc.scalar.activation(ge, ps[:, 0, :], ACT.Silu).then_inc(ex_silu, 1)
                    if j % 2 == 0:
                        act.wait_ge(sh_g, i * 2 + j // 2 + 1)
                        nc.scalar.activation(sgt, ps[:, 2, :], ACT.Silu).then_inc(sh_silu, 1)
                    else:
                        act.wait_ge(sh_tr, i * 2 + j // 2 + 1)
                        nc.scalar.copy(hsT, ps[:, 4, :].rearrange("p (k n) -> p k n", k=KD)).then_inc(sh_T, 1)
                    act.wait_ge(ex_y, e + 3)
                    act.wait_ge(ex_st[j], i * 32 + 32)
                    nc.scalar.copy(ye[j], ps[:, 6, 0:256]).then_inc(ex_ye, 1)
                    act.wait_ge(ex_ye, e + 2)
                    for half in range(2):
                        act.dma_start(ys_sorted[bass.ds(i * (4 * CAP) + j * CAP, CAP), half * 256:(half + 1) * 256],
                                      ye[j][half * CAP:(half + 1) * CAP, :]).then_inc(ex_st[j], 16)
            for j in range(4):
                act.wait_ge(ex_st[j], 32 * (E // 4) + 32)

            act.wait_ge(rt_tab, 1)
            extra = act.value_load(ovi[0:1, XTRA:XTRA + 1], min_val=0, max_val=XTRA)
            with act.If(extra > 0):
                act.sem_inc(ov_ye, 1)
                with act.Fori(0, extra) as o:
                    act.wait_ge(ov_tr, o + 2)
                    nc.scalar.copy(xeT, ps[:, 4, :].rearrange("p (k n) -> p k n", k=KD)).then_inc(ov_xT, 1)
                    act.wait_ge(ov_g, o + 2)
                    nc.scalar.activation(ge, ps[:, 0, :], ACT.Silu).then_inc(ov_silu, 1)
                    act.wait_ge(ov_y, o + 2)
                    nc.scalar.copy(ye[0], ps[:, 6, 0:256]).then_inc(ov_ye, 1)
                    act.wait_ge(ov_ye, o + 2)
                    for half in range(2):
                        act.dma_start(ys_sorted[bass.ds(o * CAP + E * CAP, CAP), half * 256:(half + 1) * 256],
                                      ye[0][half * CAP:(half + 1) * CAP, :]).then_inc(ov_st, 16)
                    act.wait_ge(ov_st, o * 32 + 32)
            act.sem_inc(moe_done, 1)

            for t in range(NT):
                act.wait_ge(fin_add, t + 1)
                act.dma_start(out[t * P:(t + 1) * P, :], fin[t]).then_inc(stored, 16)
            act.wait_ge(stored, 16 * NT)

        @block.vector
        def _(dve):
            own = [0]

            def step(ins):
                own[0] += 1
                ins.then_inc(dve_own, 1)
                dve.wait_ge(dve_own, own[0])

            step(nc.vector.memset(spec[:, 2:4], 1.0))
            dve.wait_ge(ld_spec, 32)
            nc.vector.tensor_copy(spp[1][0], spw[1]).then_inc(sp_conv, 1)
            for s in range(4):
                dve.wait_ge(sp_sq, 2 * s + 2)
                nc.vector.tensor_copy(spp[1][(s + 1) % 2], ps[:, 4:8, :]).then_inc(sp_ev1, 1)
            dve.wait_ge(sp_tot, 1)
            step(nc.vector.tensor_scalar(spec[:, 10:12], ps[:, 0, 0:2], 0.01, None, ALU.is_le))
            step(nc.vector.tensor_tensor(spec[:, 12:13], spec[:, 10:11], spec[:, 11:12], ALU.mult))
            nc.vector.tensor_scalar(flag[:, :], spec[:, 12:13], -1.0, 1.0, ALU.mult, ALU.add).then_inc(sp_flag, 1)
            dve.wait_ge(sp_flag, 1)
            general = dve.value_load(flag[0:1, 0:1], min_val=0, max_val=1)
            with dve.If(general > 0):
                for m in range(2):
                    base = m * (GENERAL_STEPS + 2)
                    dve.wait_ge(gp_mm, base + 1)
                    nc.vector.tensor_copy(g_a, ps[:, 0:4, :]).then_inc(gp_a, 1)
                    with dve.Fori(0, GENERAL_STEPS + 1) as i:
                        dve.wait_ge(gp_mm, i + (base + 1))
                        nc.vector.tensor_copy(g_p, ps[:, 0:4, :]).then_inc(gp_ev, 1)
                        dve.wait_ge(gp_ev, i + (m * (GENERAL_STEPS + 1) + 1))
                        nc.vector.tensor_tensor_reduce(out=g_junk, in0=g_p, in1=g_p, scale=1.0, scalar=0.0,
                                                       op0=ALU.mult, op1=ALU.add, accum_out=spec[:, 4:5]).then_inc(gp_ssq, 1)
                        dve.wait_ge(gp_rt, i + (base + 1))
                        nc.vector.tensor_scalar(spec[:, 7:8], spec[:, 5:6], 1e-30, None, ALU.max).then_inc(gp_ssq, 1)
                        dve.wait_ge(gp_ssq, i * 3 + (3 * base + 2))
                        nc.vector.reciprocal(spec[:, 7:8], spec[:, 7:8]).then_inc(gp_ssq, 1)
                        dve.wait_ge(gp_ssq, i * 3 + (3 * base + 3))
                        nc.vector.tensor_scalar(g_p, g_p, spec[:, 7:8], None, ALU.mult).then_inc(gp_nrm, 1)
                    dve.wait_ge(gp_mm, base + GENERAL_STEPS + 2)
                    dve.wait_ge(gp_nrm, base + GENERAL_STEPS + 1)
                    k3 = 3 * (base + GENERAL_STEPS + 1)
                    nc.vector.tensor_tensor_reduce(out=g_junk, in0=ps[:, 0:4, :], in1=g_p, scale=1.0, scalar=0.0,
                                                   op0=ALU.mult, op1=ALU.add, accum_out=spec[:, 4:5]).then_inc(gp_ssq, 1)
                    dve.wait_ge(gp_ssq, k3 + 1)
                    nc.vector.tensor_tensor_reduce(out=g_junk, in0=g_p, in1=g_p, scale=1.0, scalar=0.0,
                                                   op0=ALU.mult, op1=ALU.add, accum_out=spec[:, 13:14]).then_inc(gp_ssq, 1)
                    dve.wait_ge(gp_tot, base + GENERAL_STEPS + 2)
                    nc.vector.reciprocal(spec[:, 14:15], ps[:, 4, 1:2]).then_inc(gp_ssq, 1)
                    dve.wait_ge(gp_ssq, k3 + 3)
                    step(nc.vector.tensor_tensor(spec[:, 15:16], ps[:, 4, 0:1], spec[:, 14:15], ALU.mult))
                    nc.vector.tensor_scalar(spec[:, 6:7], spec[:, 15:16], 1.0, None, ALU.max).then_inc(gp_nrm, 1)
                    dve.wait_ge(gp_rt, base + GENERAL_STEPS + 2)
                    step(nc.vector.reciprocal(spec[:, 2 + m:3 + m], spec[:, 5:6]))
            nc.vector.tensor_tensor(spec[:, 9:10], spec[:, 2:3], spec[:, 3:4], ALU.mult).then_inc(sp_done, 1)

            own2 = [0]

            def step(ins):
                own2[0] += 1
                ins.then_inc(dve_own2, 1)
                dve.wait_ge(dve_own2, own2[0])

            dve.wait_ge(sp_done, 1)
            dve.wait_ge(lg_exp, 1)
            step(nc.vector.tensor_tensor(spec[:, 9:10], spec[:, 9:10], spec[:, 8:9], ALU.mult))

            def layernorm_stats(n):
                for t in range(NT):
                    last = nc.vector.bn_stats(bnst[:, t, :], xres[:, t, :])
                step(last)
                for t in range(NT):
                    last = nc.vector.bn_aggr(mv[:, t, :], bnst[:, t, :])
                last.then_inc(ln_stat, 1)

            def layernorm_apply(n):
                dve.wait_ge(ln_sqrt, n + 1)
                step(nc.vector.reciprocal(rstd[:, :], rstd[:, :]))
                for t in range(NT):
                    if t >= 2:
                        dve.wait_ge(ln_tr, n * NT + t - 1)
                    nc.vector.tensor_scalar(xn[t % 2], xres[:, t, :], mv[:, t, 0:1], rstd[:, t:t + 1],
                                            ALU.subtract, ALU.mult).then_inc(ln_xn, 1)

            dve.wait_ge(ld_x, 16)
            layernorm_stats(0)
            dve.wait_ge(ld_const, 48)
            for t in range(NT):
                dve.wait_ge(v_mm, t + 1)
                nc.vector.tensor_tensor(vv[:, t, :], ps[:, 2 + t % 5, :], rows[:, 0, :], ALU.add).then_inc(v_out, 1)
            layernorm_apply(0)
            dve.wait_ge(ln_xn, NT)
            for t in range(NT):
                last = nc.vector.tensor_tensor(xres[:, t, :], xres[:, t, :], rows[:, 1, :], ALU.add)
            step(last)

            def lower_part(u, i):
                b, k = UNITS[u]
                col = (COL_BK, COL_BQ)[i] + k
                dve.wait_ge(kq_hi, 2 * u + i + 1)
                nc.vector.scalar_tensor_tensor(out=parts[("k_lo", "q_lo")[i]], in0=ps[:, 7, :], scalar=cols[:, col:col + 1],
                                               in1=parts[("k_hi", "q_hi")[i]], op0=ALU.add, op1=ALU.subtract).then_inc(kq_lo, 1)

            lower_part(0, 0)
            lower_part(0, 1)

            def row_max(v):
                u, q, hp = STEPS[v]
                n = (q + 1) * P
                dve.wait_ge(at_s, v + 1)
                if v >= 3:
                    dve.wait_ge(at_exp, 2 * (v - 2))
                step(nc.vector.tensor_reduce(mx[:, v % 3, :], ps[:, 2 * (v % 2):2 * (v % 2) + 2, 0:n], AX.X, ALU.max))
                nc.vector.tensor_scalar(nmx[:, v % 3, :], mx[:, v % 3, :], -(HD ** -0.5), None, ALU.mult).then_inc(at_nm, 1)

            def normalise(v):
                u, q, hp = STEPS[v]
                n = (q + 1) * P
                dve.wait_ge(at_exp, 2 * (v + 1))
                step(nc.vector.reciprocal(rsum[:, v % 3, :], rsum[:, v % 3, :]))
                for h in range(2):
                    last = nc.vector.tensor_scalar(pr[v % 3][:, h, 0:n], pr[v % 3][:, h, 0:n], rsum[:, v % 3, h:h + 1],
                                                   None, ALU.mult)
                last.then_inc(at_p, 1)

            def probs_out(v):
                u, q, hp = STEPS[v]
                n = (q + 1) * P
                if v >= 4:
                    dve.wait_ge(at_pv, v // 2 - 1)
                dve.wait_ge(at_tr, 2 * v + 2)
                nc.vector.tensor_copy(pT[v % 4][:, 1, 0:n], ps[:, 5, 0:n]).then_inc(at_ev1, 1)

            def heads_out(u):
                b, k = UNITS[u]
                dve.wait_ge(at_pv, QT_N * (u + 1))
                nc.vector.tensor_copy(oT[:, k, b * T:(b + 1) * T], ps[:, 6, :]).then_inc(at_o, 1)

            row_max(0)
            for v in range(len(STEPS)):
                if v + 1 < len(STEPS):
                    row_max(v + 1)
                normalise(v)
                if v >= 1:
                    probs_out(v - 1)
                u, at_step = divmod(v, PER_UNIT)
                if u and at_step == 2:
                    heads_out(u - 1)
                if u + 1 < len(UNITS) and at_step in (2, 5):
                    lower_part(u + 1, (at_step - 2) // 3)
            probs_out(len(STEPS) - 1)
            heads_out(len(UNITS) - 1)
            for t in range(NT):
                dve.wait_ge(wo_mm, t + 1)
                nc.vector.tensor_tensor(xres[:, t, :], xres[:, t, :], ps[:, t, :], ALU.add).then_inc(wo_x, 1)
            dve.wait_ge(wo_x, NT)

            layernorm_stats(1)
            dve.wait_ge(rc_al, 2)
            step(nc.vector.tensor_scalar(colb[:, 4:8], colb[:, 4:8], -1.0, None, ALU.mult))
            step(nc.vector.tensor_tensor(colb[:, 0:4], cols[:, COL_BP:COL_BP + 4], cols[:, COL_DB:COL_DB + 4], ALU.add))
            layernorm_apply(1)

            def bank4(m, c):
                return ps[:, 4 * m + 2 * c:4 * m + 2 * c + 2, :].rearrange("p a n -> p (a n)")

            def tt(o, a, b, op):
                step(nc.vector.tensor_tensor(o, a, b, op))

            for pair in range(2):
                dve.wait_ge(rc_mm, 4 * pair + 1)
                for c in range(2):
                    nb = 2 * pair + c
                    last = nc.vector.tensor_scalar(t1[:, c, :], bank4(0, c), colb[:, nb:nb + 1], 20.0, ALU.add, ALU.min)
                last.then_inc(rc_cap, 1)
                dve.wait_ge(rc_sp, 2 * pair + 2)
                for c in range(2):
                    nb = 2 * pair + c
                    last = nc.vector.scalar_tensor_tensor(out=t1[:, c, :], in0=bank4(0, c), scalar=colb[:, nb:nb + 1],
                                                          in1=t1[:, c, :], op0=ALU.add, op1=ALU.max)
                last.then_inc(rc_delta, 1)
                dve.wait_ge(rc_a, 2 * pair + 2)
                nc.vector.tensor_scalar(rA, rA, 1.0 - 1e-4, None, ALU.min).then_inc(rc_amin, 1)
                dve.wait_ge(rc_amin, pair + 1)
                dve.wait_ge(rc_th, 4 * pair + 4)
                dve.wait_ge(rc_d, 3 * pair + 3)
                nc.vector.tensor_tensor(t2, rA, rB, ALU.mult).then_inc(rc_disc, 1)
                dve.wait_ge(rc_sq1, 3 * pair + 2)
                nc.vector.tensor_tensor(t3, t3, t2, ALU.add).then_inc(rc_disc, 1)
                dve.wait_ge(rc_sq1, 3 * pair + 3)
                nc.vector.tensor_tensor(t1, t1, t3, ALU.add).then_inc(rc_lam, 1)
                dve.wait_ge(rc_sq2, pair + 1)
                step(nc.vector.tensor_scalar(t1, t1, 1.0, None, ALU.max))
                step(nc.vector.reciprocal(t1, t1))
                nc.vector.tensor_tensor(rA, rA, t1, ALU.mult)
                tt(rB, rB, t1, ALU.mult)
                tt(rC, rC, t1, ALU.mult)
                dve.wait_ge(rc_mm, 4 * pair + 4)
                for c in range(2):
                    last = nc.vector.tensor_tensor(rB[:, c, :], rB[:, c, :], bank4(1, c), ALU.mult)
                last.then_inc(rc_bu, 1)
                dve.wait_ge(rc_bu, pair + 1)
                for c in range(2):
                    for b in range(B):
                        nc.vector.memset(yh[:, 2 * pair + c, b * T:b * T + 1], 0.0)
                        last = nc.vector.tensor_tensor_scan(rZ[:, c, b * T:(b + 1) * T], rA[:, c, b * T:(b + 1) * T],
                                                            rB[:, c, b * T:(b + 1) * T], 0.0, ALU.mult, ALU.add)
                step(last)
                for c in range(2):
                    for b in range(B):
                        last = nc.vector.tensor_tensor(yh[:, 2 * pair + c, b * T + 1:(b + 1) * T], rC[:, c, b * T + 1:(b + 1) * T],
                                                       rZ[:, c, b * T:(b + 1) * T - 1], ALU.mult)
                last.then_inc(rc_y, 1)
                dve.wait_ge(rc_y, pair + 1)
            for t in range(NT):
                dve.wait_ge(ro_mm, t + 1)
                nc.vector.scalar_tensor_tensor(out=xres[:, t, :], in0=ps[:, t, :], scalar=spec[:, 9:10],
                                               in1=xres[:, t, :], op0=ALU.mult, op1=ALU.add).then_inc(ro_x, 1)
            dve.wait_ge(ro_x, NT)

            layernorm_stats(2)
            layernorm_apply(2)
            dve.wait_ge(rt_lg, 1)
            nc.vector.tensor_copy(lg[:, :, :], ps[:, 7, 0:NT * E].rearrange("p (t e) -> p t e", t=NT)).then_inc(rt_lgs, 1)
            dve.wait_ge(rt_lgs, 1)
            for t in range(NT):
                last = nc.vector.max(top8[:, t, :], lg[:, t, :])
            last.then_inc(rt_max, 1)
            dve.wait_ge(rt_max, 1)
            for t in range(NT):
                last = nc.vector.max_index(idx8[:, t, :], top8[:, t, :], lg[:, t, :])
            step(last)
            step(nc.vector.tensor_copy(idxf[:, :], idx8[:, :, 0]))
            iota = consts[:, C_IOTA:C_IOTA + E]
            for t in range(NT):
                last = nc.vector.tensor_scalar(oh[:, t, :], iota, idxf[:, t:t + 1], None, ALU.is_equal)
            step(last)
            nc.vector.tensor_copy(ohb[:, :, :], oh[:, :, :]).then_inc(rt_oh, 1)
            dve.wait_ge(rt_rank, 1)
            step(nc.vector.tensor_scalar(ecnti[:, :], ps[:, 6, NT * E:NT * E + E], float(CAP - 1), None, ALU.add))
            step(nc.vector.tensor_scalar(ecnti[:, :], ecnti[:, :], CAP.bit_length() - 1, None, ALU.logical_shift_right))
            step(nc.vector.tensor_copy(ecnt[:, 0, :], ecnti[:, :]))
            step(nc.vector.tensor_scalar(ecnt[:, 0, :], ecnt[:, 0, :], -1.0, 0.0, ALU.add, ALU.max))
            step(nc.vector.tensor_tensor_scan(ecnt[:, 1, :], ones32[:, 0:E], ecnt[:, 0, :], 0.0, ALU.mult, ALU.add))
            step(nc.vector.tensor_tensor(ecnt[:, 2, :], ecnt[:, 1, :], ecnt[:, 0, :], ALU.subtract))
            step(nc.vector.tensor_tensor(lg[:, :, :], oh[:, :, :], ps[:, 6, 0:NT * E].rearrange("p (t e) -> p t e", t=NT), ALU.mult))
            step(nc.vector.tensor_reduce(pos[:, 0, :], lg[:, :, :], AX.X, ALU.add))
            step(nc.vector.tensor_tensor(lg[:, :, :], oh[:, :, :],
                                         ecnt[:, 2:3, :].broadcast_to([P, NT, E]), ALU.mult))
            step(nc.vector.tensor_reduce(pos[:, 1, :], lg[:, :, :], AX.X, ALU.add))
            step(nc.vector.tensor_scalar(pos[:, 2, :], idxf[:, :], float(CAP), None, ALU.mult))
            step(nc.vector.tensor_scalar(pos[:, 3, :], pos[:, 1, :], float(CAP), float(CAP * (E - 1)), ALU.mult, ALU.add))
            step(nc.vector.tensor_tensor(pos[:, 3, :], pos[:, 3, :], pos[:, 2, :], ALU.subtract))
            step(nc.vector.tensor_scalar(pos[:, 4, :], pos[:, 0, :], float(CAP), None, ALU.is_ge))
            step(nc.vector.tensor_tensor(pos[:, 3, :], pos[:, 3, :], pos[:, 4, :], ALU.mult))
            step(nc.vector.tensor_tensor(pos[:, 2, :], pos[:, 2, :], pos[:, 3, :], ALU.add))
            nc.vector.tensor_tensor(slot[:, :], pos[:, 0, :], pos[:, 2, :], ALU.add).then_inc(rt_slot, 1)
            for o in range(XTRA):
                last = nc.vector.tensor_scalar(ovl[:, o, :], ecnt[:, 1, :], float(o), None, ALU.is_le)
            step(last)
            step(nc.vector.tensor_reduce(ovs[:, 0:XTRA], ovl[:, :, :], AX.X, ALU.add))
            step(nc.vector.tensor_scalar(ovs[:, 0:XTRA], ovs[:, 0:XTRA], float(E - 1), None, ALU.min))
            step(nc.vector.tensor_copy(ovs[:, XTRA:XTRA + 1], ecnt[:, 1, E - 1:E]))
            nc.vector.tensor_copy(ovi[:, :], ovs[:, :]).then_inc(rt_tab, 1)
            dve.wait_ge(rt_sig, 1)
            step(nc.vector.tensor_tensor(score[:, :], score[:, :], rstd[:, :], ALU.mult))
            for t in range(NT):
                if t >= 6:
                    dve.wait_ge(sc_done[t - 6], 16)
                nc.vector.tensor_scalar(xsc[t % 6], xres[:, t, :], mv[:, t, 0:1], score[:, t:t + 1],
                                        ALU.subtract, ALU.mult).then_inc(rt_xs, 1)
            for t in range(NT):
                dve.wait_ge(sc_done[t], 16)

            def tile_x_out(n):
                dve.wait_ge(ex_tr, n)
                nc.vector.tensor_copy(xeT, ps[:, 4, :].rearrange("p (k n) -> p k n", k=KD)).then_inc(ex_xT, 1)

            dve.sem_inc(sh_x, 1)
            with dve.Fori(0, E // 4) as i:
                for j in range(4):
                    e = i * 4 + j
                    if j == 0:
                        tile_x_out(i * 2 + 1)
                    dve.wait_ge(ex_silu, e + 1)
                    dve.wait_ge(ex_u, e + 3)
                    nc.vector.tensor_tensor(he, ge, ps[:, 1, :], ALU.mult).then_inc(ex_h, 1)
                    if j == 1:
                        tile_x_out(i * 2 + 2)
                    dve.wait_ge(ex_ht, e + 1)
                    nc.vector.tensor_copy(heT, ps[:, 5, :].rearrange("p (c n) -> p c n", c=4)).then_inc(ex_hT, 1)
                    if j % 2 == 0:
                        dve.wait_ge(sh_silu, i * 2 + j // 2 + 1)
                        dve.wait_ge(sh_u, i * 2 + j // 2 + 1)
                        nc.vector.tensor_tensor(hs, sgt, ps[:, 3, :], ALU.mult).then_inc(sh_h, 1)
                    if j == 3:
                        dve.wait_ge(sh_y, i + 1)
                        xt = xres[:, bass.ds(i, 1), :].rearrange("p a n -> p (a n)")
                        nc.vector.tensor_tensor(xt, xt, ps[:, 7, :], ALU.add).then_inc(sh_x, 1)

            dve.wait_ge(rt_tab, 1)
            extra = dve.value_load(ovi[0:1, XTRA:XTRA + 1], min_val=0, max_val=XTRA)
            with dve.If(extra > 0):
                with dve.Fori(0, extra) as o:
                    dve.wait_ge(ov_silu, o + 1)
                    dve.wait_ge(ov_u, o + 2)
                    nc.vector.tensor_tensor(he, ge, ps[:, 1, :], ALU.mult).then_inc(ov_h, 1)
                    dve.wait_ge(ov_ht, o + 1)
                    nc.vector.tensor_copy(heT, ps[:, 5, :].rearrange("p (c n) -> p c n", c=4)).then_inc(ov_hT, 1)

            dve.wait_ge(sh_x, NT + 1)
            for t in range(NT):
                dve.wait_ge(gat[t], 16)
                nc.vector.tensor_tensor(fin[t], fin[t], xres[:, t, :], ALU.add).then_inc(fin_add, 1)

        @block.tensor
        def _(pe):
            mm = nc.tensor.matmul

            def gram(banks, w):
                for r in range(KD):
                    for k in range(KD):
                        last = mm(ps[:, banks + r, :], w[:, k, r * P:(r + 1) * P], w[:, k, :], start=(k == 0), stop=(k == KD - 1))
                return last

            pe.wait_ge(sp_conv, 2)
            for s in range(5):
                if s:
                    pe.wait_ge(sp_ev0, s)
                gram(0, spp[0][s % 2]).then_inc(sp_sq, 1)
                if s:
                    pe.wait_ge(sp_ev1, s)
                gram(4, spp[1][s % 2]).then_inc(sp_sq, 1)
            pe.wait_ge(zeroed, 1)
            pe.wait_ge(sp_sum, 2)
            mm(ps[:, 0, 0:2], ones32[:, :], spec[:, 0:2], start=True, stop=True).then_inc(sp_tot, 1)
            pe.wait_ge(sp_flag, 1)
            general = pe.value_load(flag[0:1, 0:1], min_val=0, max_val=1)
            with pe.If(general > 0):
                for m in range(2):
                    base = m * (GENERAL_STEPS + 2)
                    gram(0, spw[m]).then_inc(gp_mm, 1)
                    pe.wait_ge(gp_ssq, 3 * base + 1)
                    mm(ps[:, 4, 0:1], ones32[:, :], spec[:, 4:5], start=True, stop=True).then_inc(gp_tot, 1)
                    with pe.Fori(0, GENERAL_STEPS) as i:
                        pe.wait_ge(gp_nrm, i + (base + 1))
                        gram(0, g_p).then_inc(gp_mm, 1)
                        pe.wait_ge(gp_ssq, i * 3 + (3 * base + 4))
                        mm(ps[:, 4, 0:1], ones32[:, :], spec[:, 4:5], start=True, stop=True).then_inc(gp_tot, 1)
                    pe.wait_ge(gp_a, m + 1)
                    pe.wait_ge(gp_nrm, base + GENERAL_STEPS + 1)
                    for r in range(KD):
                        for k in range(KD):
                            last = mm(ps[:, r, :], g_a[:, k, r * P:(r + 1) * P], g_p[:, k, :], start=(k == 0), stop=(k == KD - 1))
                    last.then_inc(gp_mm, 1)
                    pe.wait_ge(gp_ssq, 3 * (base + GENERAL_STEPS + 1) + 2)
                    mm(ps[:, 4, 0:1], ones32[:, :], spec[:, 4:5], start=True, stop=True)
                    mm(ps[:, 4, 1:2], ones32[:, :], spec[:, 13:14], start=True, stop=True).then_inc(gp_tot, 1)
                    pe.wait_ge(gp_nrm, base + GENERAL_STEPS + 2)

            def product(dst, lhs, rhs, chunks=KD):
                for k in range(chunks):
                    last = mm(dst, lhs(k), rhs(k), start=(k == 0), stop=(k == chunks - 1))
                return last

            def transposes(n):
                for t in range(NT):
                    pe.wait_ge(ln_xn, n * NT + t + 1)
                    if t >= 2:
                        pe.wait_ge(ln_xT, n * NT + t - 1)
                    for k in range(KD):
                        last = mm(ps[:, t % 2, k * P:(k + 1) * P], xn[t % 2][:, k * P:(k + 1) * P], ident,
                                  start=True, stop=True, is_transpose=True)
                    last.then_inc(ln_tr, 1)

            pe.wait_ge(ld_ctx, 16)
            pe.wait_ge(ld_wv, 16)
            for t in range(NT):
                if t >= 5:
                    pe.wait_ge(v_out, t - 4)
                product(ps[:, 2 + t % 5, :], lambda k: cT[:, k, t * P:(t + 1) * P], lambda k: wv_s[:, k, :]).then_inc(v_mm, 1)
            pe.wait_ge(ld_const, 48)

            def project(u, i):
                b, k = UNITS[u]
                w, src = ((wk_s, cT), (wq_s, xT))[i]
                if 2 * u + i:
                    pe.wait_ge(kq_lo, 2 * u + i)
                product(ps[:, 7, :], lambda c: w[:, c, k * P:(k + 1) * P], lambda c: src[:, c, b * T:(b + 1) * T]).then_inc(kq_mm, 1)

            pe.wait_ge(ld_wk, 16)
            transposes(0)
            project(0, 0)
            pe.wait_ge(ld_wq, 16)
            pe.wait_ge(ln_xT, NT)
            project(0, 1)

            def scores(v):
                u, q, hp = STEPS[v]
                n = (q + 1) * P
                if v % PER_UNIT == 0:
                    pe.wait_ge(kq_ld[u % 2], 128 * (u // 2 + 1))
                if v >= 2:
                    pe.wait_ge(at_exp, 2 * (v - 1))
                for h in range(2):
                    bank = 2 * (v % 2) + h
                    mm(ps[:, bank, 0:n], qst[u % 2][:, 2 * hp + h, q * P:(q + 1) * P], kst[u % 2][:, 2 * hp + h, 0:n],
                       start=True, stop=True)
                    last = mm(ps[:, bank, q * P:n], identb[:, :], maskb[:, :], start=False, stop=True, skip_group_check=True)
                last.then_inc(at_s, 1)

            def probs_transposed(v):
                u, q, hp = STEPS[v]
                pe.wait_ge(at_p, v + 1)
                for h in range(2):
                    if v:
                        pe.wait_ge((at_ev0, at_ev1)[h], v)
                    for c in range(q + 1):
                        last = mm(ps[:, 4 + h, c * P:(c + 1) * P], pr[v % 3][:, h, c * P:(c + 1) * P], ident,
                                  start=True, stop=True, is_transpose=True)
                    last.then_inc(at_tr, 1)

            def values(w):
                u, q, _ = STEPS[2 * w]
                b, k = UNITS[u]
                pe.wait_ge(at_ev0, 2 * w + 2)
                pe.wait_ge(at_ev1, 2 * w + 2)
                if q == 0 and u:
                    pe.wait_ge(at_o, u)
                for c in range(q + 1):
                    for h in range(HB):
                        last = mm(ps[HD * h:HD * h + HD, 6, q * P:(q + 1) * P],
                                  vv[:, b * QT_N + c, k * P + HD * h:k * P + HD * h + HD],
                                  pT[(2 * w + h // 2) % 4][:, h % 2, c * P:(c + 1) * P], start=(c == 0), stop=(c == q))
                last.then_inc(at_pv, 1)

            pe.wait_ge(v_out, NT)
            pe.wait_ge(consts_b, 2)
            scores(0)
            for v in range(len(STEPS)):
                if v + 1 < len(STEPS):
                    scores(v + 1)
                if v >= 1:
                    probs_transposed(v - 1)
                u, at_step = divmod(v, PER_UNIT)
                if u + 1 < len(UNITS) and at_step in (2, 5):
                    project(u + 1, (at_step - 2) // 3)
                if v >= 3 and v % 2 == 1:
                    values((v - 3) // 2)
            probs_transposed(len(STEPS) - 1)
            values(len(STEPS) // 2 - 1)
            pe.wait_ge(ld_wo, 16)
            pe.wait_ge(at_o, len(UNITS))
            for t in range(NT):
                product(ps[:, t, :], lambda k: oT[:, k, t * P:(t + 1) * P], lambda k: wo_s[:, k, :]).then_inc(wo_mm, 1)

            transposes(1)
            pe.wait_ge(ln_xT, 2 * NT)
            pe.wait_ge(ld_rec, 48)
            for pair in range(2):
                for q in range(4):
                    if q == 0 and pair:
                        pe.wait_ge(rc_th, 4)
                    elif q == 1 and pair:
                        pe.wait_ge(rc_bu, 1)
                    elif q == 2:
                        pe.wait_ge(rc_delta, pair + 1)
                    elif q == 3:
                        pe.wait_ge(rc_th, 4 * pair + 2)
                    for c in range(2):
                        nb = 2 * pair + c
                        row = NCH * (0, 2, 1, 0)[q] + nb * P
                        w = (lambda k: wp_s[:, k, row:row + P]) if q < 3 else (
                            lambda k: win_s[:, k, nb * P:(nb + 1) * P])
                        for b in range(B):
                            last = product(ps[:, 4 * (q % 2) + 2 * c + b, :], w, lambda k: xT[:, k, b * T:(b + 1) * T])
                    last.then_inc(rc_mm, 1)
            pe.wait_ge(rc_y, 2)
            for t in range(NT):
                product(ps[:, t, :], lambda k: yh[:, k, t * P:(t + 1) * P], lambda k: wout_s[:, k, :]).then_inc(ro_mm, 1)

            transposes(2)
            pe.wait_ge(ln_xT, 3 * NT)
            pe.wait_ge(ld_gw, 16)
            for t in range(NT):
                last = product(ps[:, 7, t * E:(t + 1) * E], lambda k: xT[:, k, t * P:(t + 1) * P], lambda k: gw[:, k, :])
            last.then_inc(rt_lg, 1)

            def ranks():
                pe.wait_ge(rt_oh, 1)
                pe.wait_ge(ready_c, 1)
                for t in range(NT):
                    for j in range(t):
                        mm(ps[:, 6, t * E:(t + 1) * E], onesb[:, :], ohb[:, j, :], start=(j == 0), stop=False)
                    mm(ps[:, 6, t * E:(t + 1) * E], trib[:, :], ohb[:, t, :], start=(t == 0), stop=True)
                product(ps[:, 6, NT * E:NT * E + E], lambda k: onesb[:, :], lambda k: ohb[:, k, :], NT).then_inc(rt_rank, 1)

            ranks()

            def tile_x(j):
                for k in range(KD):
                    last = mm(ps[:, 4, k * P:(k + 1) * P], xe[j][:, k * P:(k + 1) * P], ident, start=True, stop=True,
                              is_transpose=True)
                return last

            def tile_up(j, w, bank):
                for k in range(KD):
                    for half in range(2):
                        last = mm(ps[CAP * half:CAP * half + CAP, bank, :], xeT[:, k, j * CAP:(j + 1) * CAP],
                                  w[:, k, half * 512:(half + 1) * 512], start=(k == 0), stop=(k == KD - 1))
                return last

            def tile_h():
                for c in range(4):
                    last = mm(ps[:, 5, c * P:(c + 1) * P], he[:, c * P:(c + 1) * P], ident, start=True, stop=True,
                              is_transpose=True)
                return last

            def tile_down(w):
                for c in range(I // P):
                    for half in range(2):
                        last = mm(ps[CAP * half:CAP * half + CAP, 6, 0:256], heT[:, c % 4, (c // 4) * CAP:(c // 4 + 1) * CAP],
                                  w[:, c, half * 256:(half + 1) * 256], start=(c == 0), stop=(c == I // P - 1))
                return last

            def shared_down(c, half):
                return mm(ps[:, 7, :], hsT[:, c, :], w_down(w_shared)[:, half * 4 + c, :],
                          start=(half == 0 and c == 0), stop=(half == 1 and c == 3))

            with pe.Fori(0, E // 4) as i:
                for j in range(4):
                    e, half = i * 4 + j, j // 2
                    n = i * 2 + half
                    wr = ring[j % 2]
                    loaded = i * 32 + 16 * (half + 1)
                    if j == 0:
                        pe.wait_ge(ex_x[0], i * 16 + 16)
                        tile_x(0).then_inc(ex_tr, 1)
                    if j % 2 == 0:
                        pe.wait_ge(ex_xT, n + 1)
                    pe.wait_ge(ld_gate[j % 2], loaded)
                    tile_up(j % 2, w_gate(wr), 0).then_inc(ex_g, 1)
                    if j % 2 == 1:
                        pe.wait_ge(sh_h, n + 1)
                        for c in range(4):
                            last = mm(ps[:, 4, c * P:(c + 1) * P], hs[:, c * P:(c + 1) * P], ident, start=True, stop=True,
                                      is_transpose=True)
                        last.then_inc(sh_tr, 1)
                    pe.wait_ge(ld_up[j % 2], loaded)
                    tile_up(j % 2, w_up(wr), 1).then_inc(ex_u, 1)
                    if j == 0:
                        pe.wait_ge(xs_cp, i + 1)
                        pe.wait_ge(ld_shared, 48)
                    if j % 2 == 0:
                        product(ps[:, 2, :], lambda k: xsT[:, k, :],
                                lambda k: w_gate(w_shared)[:, k, half * 512:(half + 1) * 512]).then_inc(sh_g, 1)
                    else:
                        pe.wait_ge(sh_T, n + 1)
                        if j == 1:
                            pe.wait_ge(ex_x[1], i * 16 + 16)
                            tile_x(1).then_inc(ex_tr, 1)
                            pe.wait_ge(sh_x, i + 1)
                        for c in range(2):
                            shared_down(c, half)
                    pe.wait_ge(ex_h, e + 1)
                    tile_h().then_inc(ex_ht, 1)
                    if j % 2 == 0:
                        product(ps[:, 3, :], lambda k: xsT[:, k, :],
                                lambda k: w_up(w_shared)[:, k, half * 512:(half + 1) * 512]).then_inc(sh_u, 1)
                    else:
                        for c in range(2, 4):
                            last = shared_down(c, half)
                        if j == 3:
                            last.then_inc(sh_y, 1)
                    pe.wait_ge(ex_hT, e + 1)
                    pe.wait_ge(ld_down[j % 2], loaded)
                    pe.wait_ge(ex_ye, e + 1)
                    tile_down(w_down(wr)).then_inc(ex_y, 1)

            pe.wait_ge(rt_tab, 1)
            extra = pe.value_load(ovi[0:1, XTRA:XTRA + 1], min_val=0, max_val=XTRA)
            with pe.If(extra > 0):
                pe.wait_ge(ex_ye, E + 1)
                with pe.Fori(0, extra) as o:
                    pe.wait_ge(ov_x, o * 16 + 16)
                    pe.wait_ge(ov_ye, o + 1)
                    tile_x(0).then_inc(ov_tr, 1)
                    pe.wait_ge(ov_xT, o + 1)
                    pe.wait_ge(ov_w[0], o * 16 + 16)
                    tile_up(0, w_gate(ring[0]), 0).then_inc(ov_g, 1)
                    pe.wait_ge(ov_w[1], o * 16 + 16)
                    tile_up(0, w_up(ring[0]), 1).then_inc(ov_u, 1)
                    pe.wait_ge(ov_h, o + 1)
                    tile_h().then_inc(ov_ht, 1)
                    pe.wait_ge(ov_hT, o + 1)
                    pe.wait_ge(ov_w[2], o * 16 + 16)
                    tile_down(w_down(ring[0])).then_inc(ov_y, 1)


def kernel(x, ctx_1024, L0_xattn_Wq, L0_xattn_bq, L0_xattn_Wk, L0_xattn_bk, L0_xattn_Wv, L0_xattn_bv, L0_xattn_Wo,
           L0_xattn_bo, L0_attn_W_in, L0_attn_W_out, L0_attn_Wp, L0_attn_bp, L0_attn_alpha_log, L0_attn_delta_bias,
           L0_attn_log_gamma, L0_ffn_gate_w, L0_ffn_shared_gate_w, L0_ffn_shared_up_w, L0_ffn_shared_down_w,
           L0_ffn_routed_gate_w, L0_ffn_routed_up_w, L0_ffn_routed_down_w):
    import numpy as np
    import concourse.bacc as bacc
    from concourse.bass_utils import run_bass_kernel_spmd

    def col(v):
        return np.asarray(v).reshape(-1, P).T

    consts = np.zeros((P, CONSTS), np.float32)
    consts[:, C_IDENT:C_IDENT + P] = np.eye(P)
    consts[:, C_MASK:C_MASK + P] = np.triu(np.full((P, P), MASKED), 1)
    consts[:, C_IOTA:C_IOTA + E] = np.arange(E)

    columns = np.concatenate([col(L0_xattn_bq), col(L0_xattn_bk), col(L0_attn_bp), col(L0_attn_delta_bias),
                              col(L0_attn_alpha_log), np.broadcast_to(np.asarray(L0_attn_log_gamma), (P, 1))], axis=1)
    rows = np.stack([np.broadcast_to(np.asarray(L0_xattn_bv), (P, D)), np.broadcast_to(np.asarray(L0_xattn_bo), (P, D))], axis=1)
    arrays = {
        "x": np.asarray(x).reshape(TOK, D),
        "ctxT": np.asarray(ctx_1024)[:, :T, :].transpose(2, 0, 1).reshape(D, TOK),
        "Wq": L0_xattn_Wq, "Wk": L0_xattn_Wk, "Wv": L0_xattn_Wv, "Wo": L0_xattn_Wo,
        "WinT": np.asarray(L0_attn_W_in).T, "WoutT": np.asarray(L0_attn_W_out).T, "WpT": np.asarray(L0_attn_Wp).T,
        "gate_w": L0_ffn_gate_w, "sg": L0_ffn_shared_gate_w, "su": L0_ffn_shared_up_w, "sd": L0_ffn_shared_down_w,
        "rg": L0_ffn_routed_gate_w, "ru": L0_ffn_routed_up_w, "rd": L0_ffn_routed_down_w,
        "cols": columns, "rows": rows, "consts": consts,
    }
    arrays = {"in_" + n: np.ascontiguousarray(a) for n, a in arrays.items()}
    nc = bacc.Bacc("TRN2", target_bir_lowering=False, num_devices=1)
    aps = [nc.dram_tensor(n, a.shape, mybir.dt.from_np(a.dtype), kind="ExternalInput").ap() for n, a in arrays.items()]
    out = nc.dram_tensor("out_0", (TOK, D), mybir.dt.float32, kind="ExternalOutput").ap()
    perceiver_layer(nc, *aps, out)
    r = run_bass_kernel_spmd(nc, [arrays], core_ids=[0])
    return r.results[0]["out_0"].reshape(B, T, D)
```

```python
import concourse.bass as bass
from concourse import mybir
from contextlib import ExitStack

B, T, D = 2, 512, 512
TOK = B * T
H, HD = 16, 32
NCH = 512
E, I = 32, 1024
P = 128
KD = D // P
NT = TOK // P
QT_N = T // P
HB = P // HD
CAP = 64
XTRA = TOK // CAP - 1
SLOTS = (E + XTRA + 1) * CAP
WORDS = 12288
GU = KD * I

COL_BQ, COL_BK, COL_BP, COL_DB, COL_AL, COL_LG = 0, 4, 8, 20, 24, 28
COLS = 29
C_IDENT, C_MASK, C_IOTA = 0, 128, 256
CONSTS = 288
MASKED = -1.0e30


def perceiver_layer(nc, x, ctxT, Wq, Wk, Wv, Wo, WinT, WoutT, WpT, gate_w, sg, su, sd, rg, ru, rd,
                    cols_in, rows_in, consts_in, out):
    f32, f32r, bf16, i32, u32 = (mybir.dt.float32, mybir.dt.float32r, mybir.dt.bfloat16, mybir.dt.int32,
                                 mybir.dt.uint32)
    ALU, ACT, AX = mybir.AluOpType, mybir.ActivationFunctionType, mybir.AxisListType

    kq_parts = nc.dram_tensor("kq_parts", [2, 2, 2, HB, HD, T], mybir.dt.float32, kind="Internal").ap()
    xs_sorted = nc.dram_tensor("xs_sorted", [SLOTS, D], f32, kind="Internal").ap()
    ys_sorted = nc.dram_tensor("ys_sorted", [SLOTS, D], f32, kind="Internal").ap()

    with ExitStack() as ctx:
        def sb(name, shape, dt=f32):
            return ctx.enter_context(nc.sbuf_tensor(name, shape, dt))

        def sem(name):
            return ctx.enter_context(nc.semaphore(name))

        FENCE, BASE = 49152, 16512
        fence = sb("fence", [P, FENCE])

        def place(name, off, shape, dt=f32):
            words = 1
            for n in shape:
                words *= n
            words = words // 2 if dt == bf16 else words
            assert off + words <= FENCE
            t = nc.alloc_sbuf_tensor_at(name, [P, *shape], dt, offset=BASE + 4 * off)
            return t[(slice(None),) * (len(shape) + 1)]

        consts = sb("consts", [P, CONSTS])
        cols = sb("cols", [P, COLS])
        rows = sb("rows", [P, 2, D])
        ones32 = sb("ones32", [P, P])
        onesb = sb("onesb", [P, P], bf16)
        trib = sb("trib", [P, P], bf16)
        eps = sb("eps", [P, 3])
        bnst = sb("bnst", [P, NT, 6])
        mv = sb("mv", [P, NT, 2])
        rstd = sb("rstd", [P, NT])
        colb = sb("colb", [P, 8])
        spec = sb("spec", [P, 16])
        zero = sb("zero", [P, D])
        flag = sb("flag", [P, 1], i32)
        mx = sb("mx", [P, 3, 2])
        nmx = sb("nmx", [P, 3, 2])
        rsum = sb("rsum", [P, 3, 2])
        identb = sb("identb", [P, P], bf16)
        maskb = sb("maskb", [P, P], bf16)
        gw = sb("gw", [P, KD, E])
        ohb = sb("ohb", [P, NT, E], bf16)
        top8 = sb("top8", [P, NT, 8])
        idx8 = sb("idx8", [P, NT, 8], u32)
        idxf = sb("idxf", [P, NT])
        score = sb("score", [P, NT])
        pos = sb("pos", [P, 6, NT])
        slot = sb("slot", [P, NT], i32)
        ecnt = sb("ecnt", [P, 6, E])
        ecnti = sb("ecnti", [P, E], i32)
        ovs = sb("ovs", [P, XTRA + 1])
        ovi = sb("ovi", [P, XTRA + 1], i32)
        tables = sb("tables", [P, (NT + XTRA) * E])
        prod = tables[:, 0:NT * E].rearrange("p (t e) -> p t e", t=NT)
        ovl = tables[:, NT * E:(NT + XTRA) * E].rearrange("p (o e) -> p o e", o=XTRA)
        xsT = tables[:, 0:D].rearrange("p (k n) -> p k n", k=KD)
        lgT = [prod[:, h * NT // 2:(h + 1) * NT // 2, :].rearrange("p t e -> p (t e)") for h in range(2)]
        ps = ctx.enter_context(nc.psum_tensor("ps", [P, 8, 512], f32))

        ident = consts[:, C_IDENT:C_IDENT + P]
        mask = consts[:, C_MASK:C_MASK + P]

        xres = place("xres", 0, [NT, D])
        xT = place("xT", 4096, [KD, TOK])
        xn = [[place(f"xn{t}", 22528 + 512 * t, [D]) for t in range(NT)],
              [place(f"xn1{j}", 32768 + 512 * j, [D]) for j in range(2)], [rows[:, j, :] for j in range(2)]]
        spw = [place(f"spw{m}", 38912 + 2048 * m, [KD, 512]) for m in range(2)]
        spp = [[place(f"spp{m}{j}", 43008 + 2048 * m + 1024 * j, [KD, 512], bf16) for j in range(2)] for m in range(2)]
        g_a, g_p, g_junk = (place(n, 43008 + 2048 * j, [KD, 512]) for j, n in enumerate(("g_a", "g_p", "g_junk")))
        cT = place("cT", 8192, [KD, TOK])
        wk_s, wq_s, wv_s = (place(n, 12288 + 2048 * j, [KD, D]) for j, n in enumerate(("wk_s", "wq_s", "wv_s")))
        vv = place("vv", 18432, [NT, D])
        oT = place("oT", 22528, [KD, TOK])
        wo_s = place("wo_s", 26624, [KD, D])
        parts = {n: place(n, 28672 + 512 * j, [T], f32r) for j, n in enumerate(("k_hi", "k_lo", "q_hi", "q_lo"))}
        kst = [place(f"kst{j}", 30720 + 4096 * j, [HB, T], f32r) for j in range(2)]
        qst = [place(f"qst{j}", 32768 + 4096 * j, [HB, T], f32r) for j in range(2)]
        pr = [place(f"pr{j}", 38912 + 1024 * j, [2, T]) for j in range(4)]
        pT = [place(f"pT{j}", 43008 + 1024 * j, [2, T]) for j in range(4)]
        wp_s = place("wp_s", 8192, [KD, 3 * NCH])
        win_s = place("win_s", 14336, [KD, NCH])
        wout_s = place("wout_s", 16384, [KD, D])
        rA, rB, rC, rZ, t1, t2, t3 = (place(n, 18432 + 2048 * j, [2, TOK])
                                      for j, n in enumerate(("rA", "rB", "rC", "rZ", "t1", "t2", "t3")))
        yh = place("yh", 32768, [4, TOK])
        w_shared = place("w_shared", 36864, [WORDS])
        ring = [place(f"ring{j}", 8192 + WORDS * j, [WORDS]) for j in range(2)]
        xsc = [place(f"xsc{t}", 32768 + 512 * t, [D]) for t in range(NT)]
        heT = place("heT", 32768, [4, P])
        hsT = place("hsT", 33280, [4, P])
        xe = [place(f"xe{j}", 33792 + 512 * j, [D]) for j in range(2)]
        xeT = place("xeT", 34816, [KD, P])
        hs = place("hs", 35328, [512])
        ye = [place(f"ye{j}", 35840 + 256 * j, [256]) for j in range(4)]
        ge, he, sgt = rows[:, 0, :], rows[:, 1, :], zero[:, :]
        fin = [place(f"fin{t}", 8192 + 512 * t, [D]) for t in range(NT)]

        def w_gate(w):
            return w[:, 0:GU].rearrange("p (k n) -> p k n", k=KD)

        def w_up(w):
            return w[:, GU:2 * GU].rearrange("p (k n) -> p k n", k=KD)

        def w_down(w):
            return w[:, 2 * GU:3 * GU].rearrange("p (k n) -> p k n", k=I // P)

        ld_spec, ld_const, ld_x, ld_ctx, ld_wk, ld_wv, ld_wq, ld_wo, ld_rec, ld_gw = (
            sem(n) for n in ("ld_spec", "ld_const", "ld_x", "ld_ctx", "ld_wk", "ld_wv", "ld_wq", "ld_wo", "ld_rec", "ld_gw"))
        ld_gate, ld_up, ld_down = ([sem(f"{n}{j}") for j in range(2)] for n in ("ld_gate", "ld_up", "ld_down"))
        zeroed, filled = sem("zeroed"), sem("filled")
        sp_conv, sp_sq, sp_ev0, sp_ev1 = sem("sp_conv"), sem("sp_sq"), sem("sp_ev0"), sem("sp_ev1")
        sp_sum, sp_tot, sp_flag, sp_done = sem("sp_sum"), sem("sp_tot"), sem("sp_flag"), sem("sp_done")
        gp_mm, gp_ev, gp_ssq, gp_tot, gp_rt, gp_nrm, gp_a = (sem(n) for n in ("gp_mm", "gp_ev", "gp_ssq", "gp_tot", "gp_rt", "gp_nrm", "gp_a"))
        lg_exp, ready_c = sem("lg_exp"), sem("ready_c")
        ln_stat, ln_sqrt, ln_xn, ln_tr, ln_xT = (sem(n) for n in ("ln_stat", "ln_sqrt", "ln_xn", "ln_tr", "ln_xT"))
        v_mm, v_out, kq_mm, kq_hi, kq_lo, kq_st, consts_b = (
            sem(n) for n in ("v_mm", "v_out", "kq_mm", "kq_hi", "kq_lo", "kq_st", "consts_b"))
        kq_ld = [sem(f"kq_ld{j}") for j in range(2)]
        at_s, at_nm, at_exp, at_p, at_tr, at_ev0, at_ev1, at_pv, at_o = (
            sem(n) for n in ("at_s", "at_nm", "at_exp", "at_p", "at_tr", "at_ev0", "at_ev1", "at_pv", "at_o"))
        wo_mm, wo_x = sem("wo_mm"), sem("wo_x")
        rc_mm, rc_cap, rc_sp, rc_delta, rc_a, rc_amin, rc_thc, rc_thb, rc_sq, rc_sqb, rc_q, rc_dif, rc_sum = (
            sem(n) for n in ("rc_mm", "rc_cap", "rc_sp", "rc_delta", "rc_a", "rc_amin", "rc_thc", "rc_thb", "rc_sq",
                             "rc_sqb", "rc_q", "rc_dif", "rc_sum"))
        rc_sq1, rc_disc, rc_root, rc_lam, rc_inv, rc_bu, rc_y, rc_al = (
            sem(n) for n in ("rc_sq1", "rc_disc", "rc_root", "rc_lam", "rc_inv", "rc_bu", "rc_y", "rc_al"))
        ro_mm, ro_x = sem("ro_mm"), sem("ro_x")
        rt_lgT, rt_lgs, rt_lg, rt_oh, rt_rank, rt_max, rt_sig, rt_slot, rt_xs, rt_tab = (
            sem(n) for n in ("rt_lgT", "rt_lgs", "rt_lg", "rt_oh", "rt_rank", "rt_max", "rt_sig", "rt_slot", "rt_xs",
                             "rt_tab"))
        sc_done = [sem(f"sc_done{t}") for t in range(NT)]
        ld_shared, xs_cp = sem("ld_shared"), sem("xs_cp")
        sh_g, sh_u, sh_silu, sh_h, sh_tr, sh_T, sh_y, sh_x = (
            sem(n) for n in ("sh_g", "sh_u", "sh_silu", "sh_h", "sh_tr", "sh_T", "sh_y", "sh_x"))
        ex_tr, ex_xT, ex_g, ex_u, ex_silu, ex_h, ex_ht, ex_hT, ex_y, ex_ye = (
            sem(n) for n in ("ex_tr", "ex_xT", "ex_g", "ex_u", "ex_silu", "ex_h", "ex_ht", "ex_hT", "ex_y", "ex_ye"))
        ex_x = [sem(f"ex_x{j}") for j in range(2)]
        ex_st = [sem(f"ex_st{j}") for j in range(4)]
        ov_w = [sem(f"ov_w{j}") for j in range(3)]
        ov_x, ov_tr, ov_xT, ov_g, ov_u, ov_silu, ov_h, ov_ht, ov_hT, ov_y, ov_ye, ov_st = (
            sem(n) for n in ("ov_x", "ov_tr", "ov_xT", "ov_g", "ov_u", "ov_silu", "ov_h", "ov_ht", "ov_hT", "ov_y",
                             "ov_ye", "ov_st"))
        moe_done = sem("moe_done")
        gat = [sem(f"gat{t}") for t in range(NT)]
        fin_add = sem("fin_add")
        stored = sem("stored")
        dve_own, dve_own2 = sem("dve_own"), sem("dve_own2")

        GENERAL_STEPS = 16
        UNITS = [(b, k) for b in range(B) for k in range(KD)]
        STEPS = [(u, q, hp) for u in range(len(UNITS)) for q in range(QT_N) for hp in range(2)]
        PER_UNIT = 2 * QT_N
        PROJECT = {1: (1, 1, (0, 1)), 2: (1, 1, (2, 3)), PER_UNIT - 2: (2, 0, (0, 1)), PER_UNIT - 1: (2, 0, (2, 3))}
        EVICT = {0: 0, 3: 1}
        FILL = (4, 5)

        def evicted_part(v):
            u, at_step = divmod(v, PER_UNIT)
            if at_step in EVICT and u + 1 < len(UNITS) and v:
                return u + 1, EVICT[at_step]

        def ln_bank(n, t):
            return 7 - t if n == 0 else t % 2

        NB = NCH // P
        RC_BANK = (2, 4, 6, 0)
        WO_BANK = [7 if t < NT // 2 else 2 + t - NT // 2 for t in range(NT)]
        RO_BANK = [2 + t % 6 for t in range(NT)]
        RO_EARLY = 6
        LGT_BANK, LG_BANK, RANK_BANK = (2, 3), (4, 6), 5

        block = ctx.enter_context(nc.Block())

        @block.sync
        def _(sp):
            def kmaj(w):
                return w.rearrange("(k p) n -> p k n", p=P)

            sp.dma_start(spw[0], kmaj(WinT)).then_inc(ld_spec, 16)
            sp.dma_start(spw[1], kmaj(WoutT)).then_inc(ld_spec, 16)
            sp.dma_start(consts[:, :], consts_in).then_inc(ld_const, 16)
            sp.dma_start(cols[:, :], cols_in).then_inc(ld_const, 16)
            sp.dma_start(rows[:, :, :], rows_in).then_inc(ld_const, 16)
            sp.dma_start(xres, x.rearrange("(t p) n -> p t n", p=P)).then_inc(ld_x, 16)
            sp.dma_start(wk_s, kmaj(Wk)).then_inc(ld_wk, 16)
            sp.dma_start(cT, kmaj(ctxT)).then_inc(ld_ctx, 16)
            sp.dma_start(wq_s, kmaj(Wq)).then_inc(ld_wq, 16)
            sp.dma_start(wv_s, kmaj(Wv)).then_inc(ld_wv, 16)
            sp.dma_start(wo_s, kmaj(Wo)).then_inc(ld_wo, 16)
            sp.dma_start(gw[:, :, :], kmaj(gate_w)).then_inc(ld_gw, 16)

            for u in range(len(UNITS)):
                for i, name in enumerate("kq"):
                    sp.wait_ge(kq_lo, 2 * u + i + 1)
                    if u >= 2:
                        sp.wait_ge(at_s, PER_UNIT * (u - 1))
                    for part, sfx in enumerate(("hi", "lo")):
                        sp.dma_start(kq_parts[u % 2, i, part, :, :, :].rearrange("h d n -> (h d) n"),
                                     parts[f"{name}_{sfx}"].bitcast(f32)).then_inc(kq_st, 16)
                    sp.wait_ge(kq_st, 32 * (2 * u + i + 1))
                    dst = (kst, qst)[i][u % 2]
                    for g in range(4):
                        part = g % 2 if i == 0 else g // 2
                        sp.dma_start(dst[HD * g:HD * g + HD, :, :].bitcast(f32),
                                     kq_parts[u % 2, i, part, :, :, :].rearrange("h d n -> d h n")).then_inc(kq_ld[u % 2], 16)
                if u == 1:
                    sp.wait_ge(zeroed, 1)
                    for t in range(SLOTS // P):
                        sp.dma_start(xs_sorted[t * P:(t + 1) * P, :], zero[:, :]).then_inc(filled, 16)
                    for t in range(E * CAP // P, SLOTS // P):
                        sp.dma_start(ys_sorted[t * P:(t + 1) * P, :], zero[:, :]).then_inc(ex_st[t % 4], 16)
            sp.wait_ge(kq_mm, 2 * len(UNITS))
            sp.dma_start(wp_s, kmaj(WpT)).then_inc(ld_rec, 16)
            sp.dma_start(win_s, kmaj(WinT)).then_inc(ld_rec, 16)
            sp.dma_start(wout_s, kmaj(WoutT)).then_inc(ld_rec, 16)
            sp.wait_ge(at_pv, len(UNITS) * QT_N)
            sp.dma_start(w_gate(w_shared), kmaj(sg)).then_inc(ld_shared, 16)
            sp.dma_start(w_up(w_shared), kmaj(su)).then_inc(ld_shared, 16)
            sp.dma_start(w_down(w_shared), kmaj(sd)).then_inc(ld_shared, 16)

            def load_expert(e, j, part):
                w, view, done = ((rg, w_gate, ld_gate), (ru, w_up, ld_up), (rd, w_down, ld_down))[part]
                sp.dma_start(view(ring[j]), w[e, :, :].rearrange("a (k p) n -> p (a k) n", p=P)).then_inc(done[j], 16)

            sp.sem_inc(ex_g, 2)
            sp.sem_inc(ex_u, 2)
            sp.sem_inc(ex_y, 2)
            sp.wait_ge(rc_mm, 4 * NB)
            for part in range(2):
                load_expert(slice(0, 1), 0, part)
            sp.wait_ge(rc_y, NB)
            for part in range(2):
                load_expert(slice(1, 2), 1, part)
            sp.wait_ge(ro_mm, NT)
            load_expert(slice(0, 1), 0, 2)
            load_expert(slice(1, 2), 1, 2)
            with sp.Fori(0, E // 2 - 1) as i:
                for j in range(2):
                    for part, used in enumerate((ex_g, ex_u, ex_y)):
                        sp.wait_ge(used, i * 2 + j + 3)
                        load_expert(bass.ds(i * 2 + j + 2, 1), j, part)
            sp.wait_ge(rt_tab, 1)
            extra = sp.value_load(ovi[0:1, XTRA:XTRA + 1], min_val=0, max_val=XTRA)
            with sp.If(extra > 0):
                sp.wait_ge(ex_y, E + 1)
                for used in (ov_g, ov_u, ov_y):
                    sp.sem_inc(used, 1)
                with sp.Fori(0, extra) as o:
                    e = sp.value_load(ovi[0:1, bass.ds(o, 1)], min_val=0, max_val=E - 1)
                    for part, (w, view, used) in enumerate(((rg, w_gate, ov_g), (ru, w_up, ov_u), (rd, w_down, ov_y))):
                        sp.wait_ge(used, o + 1)
                        sp.dma_start(view(ring[0]), w[bass.ds(e, 1), :, :].rearrange("a (k p) n -> p (a k) n", p=P)).then_inc(ov_w[part], 16)

        @block.gpsimd
        def _(pool):
            nc.gpsimd.memset(ones32[:, :], 1.0)
            nc.gpsimd.memset(onesb[:, :], 1.0)
            nc.gpsimd.memset(eps[:, 0:1], 1e-5)
            nc.gpsimd.memset(eps[:, 1:2], 1e-12)
            nc.gpsimd.memset(eps[:, 2:3], 1.0)
            nc.gpsimd.memset(zero[:, :], 0.0).then_inc(zeroed, 1)
            pool.wait_ge(zeroed, 1)
            nc.gpsimd.affine_select(out=trib[:, :], in_=onesb[:, :], compare_op=ALU.is_gt, fill=0.0, base=0,
                                    pattern=[[1, P]], channel_multiplier=-1).then_inc(ready_c, 1)

            pool.wait_ge(ld_const, 48)
            nc.gpsimd.tensor_copy(identb[:, :], ident).then_inc(consts_b, 1)
            nc.gpsimd.tensor_copy(maskb[:, :], mask).then_inc(consts_b, 1)

            for n in range(NB):
                pool.wait_ge(rc_dif, n + 1)
                nc.gpsimd.tensor_tensor(t1[:, n % 2, :], t1[:, n % 2, :], t2[:, n % 2, :], ALU.add).then_inc(rc_sum, 1)

            def load_pair(j, first_row):
                nc.gpsimd.dma_start(xe[j], xs_sorted[first_row, :]).then_inc(ex_x[j], 16)

            pool.wait_ge(filled, 16 * (SLOTS // P))
            pool.wait_ge(rt_slot, 1)
            for t in range(NT):
                pool.wait_ge(rt_xs, t + 1)
                nc.gpsimd.indirect_dma_start(
                    xs_sorted[:, :], bass.IndirectOffsetOnAxis(ap=slot[:, t:t + 1], axis=0), xsc[t], None,
                ).then_inc(sc_done[t], 16)
            for t in range(NT):
                pool.wait_ge(sc_done[t], 16)
            for j in range(2):
                load_pair(j, slice(j * P, (j + 1) * P))
            with pool.Fori(0, NT - 1) as i:
                for j in range(2):
                    pool.wait_ge(ex_tr, i * 2 + j + 1)
                    load_pair(j, bass.ds(i * (2 * P) + (j + 2) * P, P))

            pool.wait_ge(rt_tab, 1)
            extra = pool.value_load(ovi[0:1, XTRA:XTRA + 1], min_val=0, max_val=XTRA)
            with pool.If(extra > 0):
                pool.sem_inc(ov_tr, 1)
                pool.wait_ge(ex_tr, E // 2 - 1)
                with pool.Fori(0, extra) as o:
                    pool.wait_ge(ov_tr, o + 1)
                    nc.gpsimd.dma_start(xe[0], xs_sorted[bass.ds(o * CAP + E * CAP, P), :]).then_inc(ov_x, 16)

            pool.wait_ge(moe_done, 1)
            for t in range(NT):
                nc.gpsimd.indirect_dma_start(
                    fin[t], None, ys_sorted[:, :], bass.IndirectOffsetOnAxis(ap=slot[:, t:t + 1], axis=0),
                ).then_inc(gat[t], 16)

        @block.scalar
        def _(act):
            def layernorm_root(n, half):
                act.wait_ge(ln_stat, 2 * n + half + 1)
                tiles = slice(half * NT // 2, (half + 1) * NT // 2)
                nc.scalar.activation(rstd[:, tiles], mv[:, tiles, 1], ACT.Sqrt, bias=eps[:, 0:1]).then_inc(ln_sqrt, 1)

            act.wait_ge(ld_spec, 32)
            nc.scalar.copy(spp[0][0], spw[0]).then_inc(sp_conv, 1)
            for s in range(4):
                act.wait_ge(sp_sq, 2 * s + 1)
                nc.scalar.copy(spp[0][(s + 1) % 2], ps[:, 0:4, :]).then_inc(sp_ev0, 1)
            act.wait_ge(zeroed, 1)
            for half in range(2):
                layernorm_root(0, half)
            for m in range(2):
                act.wait_ge(sp_sq, 9 + m)
                nc.scalar.activation(spp[m][1], ps[:, 4 * m:4 * m + 4, :], ACT.Square,
                                     accum_out=spec[:, m:m + 1]).then_inc(sp_sum, 1)
            act.wait_ge(ld_const, 48)
            nc.scalar.activation(spec[:, 8:9], cols[:, COL_LG:COL_LG + 1], ACT.Exp).then_inc(lg_exp, 1)
            def transposed_out(n, t):
                act.wait_ge(ln_tr, n * NT + t + 1)
                nc.scalar.copy(xT[:, :, t * P:(t + 1) * P],
                               ps[:, ln_bank(n, t), :].rearrange("p (k n) -> p k n", k=KD)).then_inc(ln_xT, 1)

            def upper_part(u, i):
                b, k = UNITS[u]
                n = 2 * u + i
                act.wait_ge(kq_mm, n + 1)
                if u:
                    act.wait_ge(kq_st, 32 * (n - 1))
                nc.scalar.activation(parts[("k_hi", "q_hi")[i]], ps[:, 7, :], ACT.Identity,
                                     bias=cols[:, (COL_BK, COL_BQ)[i] + k:(COL_BK, COL_BQ)[i] + k + 1]).then_inc(kq_hi, 1)

            for t in range(NT):
                transposed_out(0, t)
            upper_part(0, 0)
            upper_part(0, 1)
            upper_part(1, 0)

            act.wait_ge(sp_flag, 1)
            general = act.value_load(flag[0:1, 0:1], min_val=0, max_val=1)
            with act.If(general > 0):
                for m in range(2):
                    with act.Fori(0, GENERAL_STEPS + 1) as i:
                        n = i + m * (GENERAL_STEPS + 2)
                        act.wait_ge(gp_tot, n + 1)
                        nc.scalar.activation(spec[:, 5:6], ps[:, 4, 0:1], ACT.Sqrt).then_inc(gp_rt, 1)
                    act.wait_ge(gp_nrm, (m + 1) * (GENERAL_STEPS + 2))
                    nc.scalar.activation(spec[:, 5:6], spec[:, 6:7], ACT.Sqrt).then_inc(gp_rt, 1)

            def exps(v):
                u, q, hp = STEPS[v]
                n = (q + 1) * P
                act.wait_ge(at_nm, v + 1)
                if v >= 4:
                    act.wait_ge(at_tr, 2 * (v - 3))
                for h in range(2):
                    nc.scalar.activation(pr[v % 4][:, h, 0:n], ps[:, 2 * (v % 2) + h, 0:n], ACT.Exp,
                                         bias=nmx[:, v % 3, h:h + 1], scale=HD ** -0.5,
                                         accum_out=rsum[:, v % 3, h:h + 1]).then_inc(at_exp, 1)

            def probs_out(v):
                u, q, hp = STEPS[v]
                n = (q + 1) * P
                if v >= 4:
                    act.wait_ge(at_pv, v // 2 - 1)
                act.wait_ge(at_tr, 2 * v + 1)
                nc.scalar.copy(pT[v % 4][:, 0, 0:n], ps[:, 4, 0:n]).then_inc(at_ev0, 1)

            for v in range(len(STEPS)):
                exps(v)
                if v >= 2:
                    probs_out(v - 2)
                if evicted_part(v):
                    upper_part(*evicted_part(v))
            for v in range(len(STEPS) - 2, len(STEPS)):
                probs_out(v)

            nc.scalar.activation(colb[:, 4:8], cols[:, COL_AL:COL_AL + 4], ACT.Exp).then_inc(rc_al, 1)
            act.wait_ge(rc_al, 1)
            nc.scalar.activation(colb[:, 4:8], colb[:, 4:8], ACT.Ln, bias=eps[:, 2:3]).then_inc(rc_al, 1)
            for half in range(2):
                layernorm_root(1, half)
                for t in range(half * NT // 2, (half + 1) * NT // 2):
                    transposed_out(1, t)

            def tanh(n, q, dst, done):
                act.wait_ge(rc_mm, 4 * n + q + 1)
                col = COL_BP + NB * (2 if q == 1 else 1) + n
                nc.scalar.activation(dst[:, n % 2, :], ps[:, RC_BANK[q]:RC_BANK[q] + 2, :].rearrange("p a n -> p (a n)"),
                                     ACT.Tanh, bias=cols[:, col:col + 1]).then_inc(done, 1)

            for n in range(NB):
                a, b_, c, z, u1, u2, u3 = (t[:, n % 2, :] for t in (rA, rB, rC, rZ, t1, t2, t3))
                act.wait_ge(rc_cap, n + 1)
                nc.scalar.activation(u1, u1, ACT.Exp).then_inc(rc_sp, 1)
                act.wait_ge(rc_sp, 2 * n + 1)
                nc.scalar.activation(u1, u1, ACT.Ln, bias=eps[:, 2:3]).then_inc(rc_sp, 1)
                act.wait_ge(rc_delta, n + 1)
                nc.scalar.activation(a, u1, ACT.Exp, scale=colb[:, 4 + n:5 + n]).then_inc(rc_a, 1)
                tanh(n, 1, rC, rc_thc)
                act.wait_ge(rc_amin, n + 1)
                nc.scalar.activation(u1, a, ACT.Square).then_inc(rc_sq, 1)
                act.wait_ge(rc_thc, n + 1)
                nc.scalar.activation(u3, c, ACT.Square).then_inc(rc_sq, 1)
                tanh(n, 2, rB, rc_thb)
                act.wait_ge(rc_thb, n + 1)
                nc.scalar.activation(u2, b_, ACT.Square).then_inc(rc_sqb, 1)
                act.wait_ge(rc_q, n + 1)
                nc.scalar.activation(z, z, ACT.Square, scale=2.0).then_inc(rc_sq1, 1)
                act.wait_ge(rc_dif, n + 1)
                nc.scalar.activation(u3, u3, ACT.Square).then_inc(rc_sq1, 1)
                act.wait_ge(rc_disc, n + 1)
                nc.scalar.activation(u3, u3, ACT.Sqrt, bias=eps[:, 1:2]).then_inc(rc_root, 1)
                act.wait_ge(rc_lam, n + 1)
                nc.scalar.activation(u1, u1, ACT.Ln, scale=0.5).then_inc(rc_inv, 1)
                act.wait_ge(rc_inv, 2 * n + 1)
                nc.scalar.activation(u1, u1, ACT.Exp, scale=-0.5).then_inc(rc_inv, 1)

            for half in range(2):
                layernorm_root(2, half)
                for t in range(half * NT // 2, (half + 1) * NT // 2):
                    transposed_out(2, t)
            act.wait_ge(rt_max, 2)
            nc.scalar.activation(score[:, :], top8[:, :, 0], ACT.Sigmoid).then_inc(rt_sig, 1)

            act.wait_ge(filled, 16 * (SLOTS // P))
            for j in range(4):
                act.wait_ge(ex_st[j], 32)
            act.sem_inc(ex_ye, 1)
            with act.Fori(0, E // 4) as i:
                for j in range(4):
                    e = i * 4 + j
                    if j % 2 == 0:
                        act.wait_ge(sh_g, i * 2 + j // 2 + 1)
                        nc.scalar.activation(sgt, ps[:, 2, :], ACT.Silu).then_inc(sh_silu, 1)
                    act.wait_ge(ex_g, e + 3)
                    nc.scalar.activation(ge, ps[:, 0, :], ACT.Silu).then_inc(ex_silu, 1)
                    if j % 2 == 1:
                        act.wait_ge(sh_tr, i * 2 + j // 2 + 1)
                        nc.scalar.copy(hsT, ps[:, 4, :].rearrange("p (k n) -> p k n", k=KD)).then_inc(sh_T, 1)
                    act.wait_ge(ex_y, e + 3)
                    act.wait_ge(ex_st[j], i * 32 + 32)
                    nc.scalar.copy(ye[j], ps[:, 6, 0:256]).then_inc(ex_ye, 1)
                    act.wait_ge(ex_ye, e + 2)
                    for half in range(2):
                        act.dma_start(ys_sorted[bass.ds(i * (4 * CAP) + j * CAP, CAP), half * 256:(half + 1) * 256],
                                      ye[j][half * CAP:(half + 1) * CAP, :]).then_inc(ex_st[j], 16)

            act.wait_ge(rt_tab, 1)
            extra = act.value_load(ovi[0:1, XTRA:XTRA + 1], min_val=0, max_val=XTRA)
            with act.If(extra > 0):
                act.wait_ge(ex_st[0], 32 * (E // 4) + 32)
                act.sem_inc(ov_st, 32)
                act.sem_inc(ov_ye, 1)
                with act.Fori(0, extra) as o:
                    act.wait_ge(ov_tr, o + 2)
                    nc.scalar.copy(xeT, ps[:, 4, :].rearrange("p (k n) -> p k n", k=KD)).then_inc(ov_xT, 1)
                    act.wait_ge(ov_g, o + 2)
                    nc.scalar.activation(ge, ps[:, 0, :], ACT.Silu).then_inc(ov_silu, 1)
                    act.wait_ge(ov_y, o + 2)
                    act.wait_ge(ov_st, o * 32 + 32)
                    nc.scalar.copy(ye[0], ps[:, 6, 0:256]).then_inc(ov_ye, 1)
                    act.wait_ge(ov_ye, o + 2)
                    for half in range(2):
                        act.dma_start(ys_sorted[bass.ds(o * CAP + E * CAP, CAP), half * 256:(half + 1) * 256],
                                      ye[0][half * CAP:(half + 1) * CAP, :]).then_inc(ov_st, 16)
                act.wait_ge(ov_st, extra * 32 + 32)
                act.sem_inc(ov_ye, 1)
            for j in range(4):
                act.wait_ge(ex_st[j], 32 * (E // 4) + 32)
            act.sem_inc(moe_done, 1)

            for t in range(NT):
                act.wait_ge(fin_add, t + 1)
                act.dma_start(out[t * P:(t + 1) * P, :], fin[t]).then_inc(stored, 16)
            act.wait_ge(stored, 16 * NT)

        @block.vector
        def _(dve):
            own = [0, dve_own]

            def step(ins):
                own[0] += 1
                ins.then_inc(own[1], 1)
                dve.wait_ge(own[1], own[0])

            def layernorm_stats(t, signal):
                step(nc.vector.bn_stats(bnst[:, t, :], xres[:, t, :]))
                last = nc.vector.bn_aggr(mv[:, t, :], bnst[:, t, :])
                if signal:
                    last.then_inc(ln_stat, 1)

            def layernorm_scale(n, half):
                tiles = slice(half * NT // 2, (half + 1) * NT // 2)
                dve.wait_ge(ln_sqrt, 2 * n + half + 1)
                step(nc.vector.reciprocal(rstd[:, tiles], rstd[:, tiles]))

            def layernorm_apply(n, t):
                if n and t >= 2:
                    dve.wait_ge(ln_tr, n * NT + t - 1)
                nc.vector.tensor_scalar(xn[n][t % len(xn[n])], xres[:, t, :], mv[:, t, 0:1], rstd[:, t:t + 1],
                                        ALU.subtract, ALU.mult).then_inc(ln_xn, 1)

            def residual_layernorm(n, add, late):
                for t in range(late):
                    add(t)
                    layernorm_stats(t, t == NT // 2 - 1)
                layernorm_scale(n, 0)
                layernorm_apply(n, 0)
                layernorm_apply(n, 1)
                for t in range(late, NT):
                    add(t)
                    layernorm_stats(t, t == NT - 1)
                layernorm_apply(n, 2)
                layernorm_apply(n, 3)
                layernorm_scale(n, 1)

            step(nc.vector.memset(spec[:, 2:4], 1.0))
            dve.wait_ge(ld_spec, 32)
            nc.vector.tensor_copy(spp[1][0], spw[1]).then_inc(sp_conv, 1)
            for s in range(4):
                dve.wait_ge(sp_sq, 2 * s + 2)
                nc.vector.tensor_copy(spp[1][(s + 1) % 2], ps[:, 4:8, :]).then_inc(sp_ev1, 1)
                if s in (1, 2):
                    dve.wait_ge(ld_x, 16)
                    for t in range((s - 1) * NT // 2, s * NT // 2):
                        layernorm_stats(t, t == s * NT // 2 - 1)
            for t in range(NT):
                if t % (NT // 2) == 0:
                    layernorm_scale(0, t // (NT // 2))
                layernorm_apply(0, t)
            dve.wait_ge(sp_tot, 1)
            step(nc.vector.tensor_scalar(spec[:, 10:12], ps[:, 0, 0:2], 0.01, None, ALU.is_le))
            step(nc.vector.tensor_tensor(spec[:, 12:13], spec[:, 10:11], spec[:, 11:12], ALU.mult))
            nc.vector.tensor_scalar(flag[:, :], spec[:, 12:13], -1.0, 1.0, ALU.mult, ALU.add).then_inc(sp_flag, 1)
            dve.wait_ge(ld_const, 48)
            dve.wait_ge(ln_xn, NT)
            for t in range(NT):
                last = nc.vector.tensor_tensor(xres[:, t, :], xres[:, t, :], rows[:, 1, :], ALU.add)
            step(last)

            def lower_part(u, i):
                b, k = UNITS[u]
                col = (COL_BK, COL_BQ)[i] + k
                dve.wait_ge(kq_hi, 2 * u + i + 1)
                nc.vector.scalar_tensor_tensor(out=parts[("k_lo", "q_lo")[i]], in0=ps[:, 7, :], scalar=cols[:, col:col + 1],
                                               in1=parts[("k_hi", "q_hi")[i]], op0=ALU.add, op1=ALU.subtract).then_inc(kq_lo, 1)

            lower_part(0, 0)
            lower_part(0, 1)
            lower_part(1, 0)

            def add_bv(t, bank):
                dve.wait_ge(v_mm, t + 1)
                nc.vector.tensor_tensor(vv[:, t, :], ps[:, bank, :], rows[:, 0, :], ALU.add).then_inc(v_out, 1)

            for t in range(NT // 2):
                add_bv(t, 2 + t)

            dve.wait_ge(sp_flag, 1)
            general = dve.value_load(flag[0:1, 0:1], min_val=0, max_val=1)
            with dve.If(general > 0):
                for m in range(2):
                    base = m * (GENERAL_STEPS + 2)
                    dve.wait_ge(gp_mm, base + 1)
                    nc.vector.tensor_copy(g_a, ps[:, 0:4, :]).then_inc(gp_a, 1)
                    with dve.Fori(0, GENERAL_STEPS + 1) as i:
                        dve.wait_ge(gp_mm, i + (base + 1))
                        nc.vector.tensor_copy(g_p, ps[:, 0:4, :]).then_inc(gp_ev, 1)
                        dve.wait_ge(gp_ev, i + (m * (GENERAL_STEPS + 1) + 1))
                        nc.vector.tensor_tensor_reduce(out=g_junk, in0=g_p, in1=g_p, scale=1.0, scalar=0.0,
                                                       op0=ALU.mult, op1=ALU.add, accum_out=spec[:, 4:5]).then_inc(gp_ssq, 1)
                        dve.wait_ge(gp_rt, i + (base + 1))
                        nc.vector.tensor_scalar(spec[:, 7:8], spec[:, 5:6], 1e-30, None, ALU.max).then_inc(gp_ssq, 1)
                        dve.wait_ge(gp_ssq, i * 3 + (3 * base + 2))
                        nc.vector.reciprocal(spec[:, 7:8], spec[:, 7:8]).then_inc(gp_ssq, 1)
                        dve.wait_ge(gp_ssq, i * 3 + (3 * base + 3))
                        nc.vector.tensor_scalar(g_p, g_p, spec[:, 7:8], None, ALU.mult).then_inc(gp_nrm, 1)
                    dve.wait_ge(gp_mm, base + GENERAL_STEPS + 2)
                    dve.wait_ge(gp_nrm, base + GENERAL_STEPS + 1)
                    k3 = 3 * (base + GENERAL_STEPS + 1)
                    nc.vector.tensor_tensor_reduce(out=g_junk, in0=ps[:, 0:4, :], in1=g_p, scale=1.0, scalar=0.0,
                                                   op0=ALU.mult, op1=ALU.add, accum_out=spec[:, 4:5]).then_inc(gp_ssq, 1)
                    dve.wait_ge(gp_ssq, k3 + 1)
                    nc.vector.tensor_tensor_reduce(out=g_junk, in0=g_p, in1=g_p, scale=1.0, scalar=0.0,
                                                   op0=ALU.mult, op1=ALU.add, accum_out=spec[:, 13:14]).then_inc(gp_ssq, 1)
                    dve.wait_ge(gp_tot, base + GENERAL_STEPS + 2)
                    nc.vector.reciprocal(spec[:, 14:15], ps[:, 4, 1:2]).then_inc(gp_ssq, 1)
                    dve.wait_ge(gp_ssq, k3 + 3)
                    step(nc.vector.tensor_tensor(spec[:, 15:16], ps[:, 4, 0:1], spec[:, 14:15], ALU.mult))
                    nc.vector.tensor_scalar(spec[:, 6:7], spec[:, 15:16], 1.0, None, ALU.max).then_inc(gp_nrm, 1)
                    dve.wait_ge(gp_rt, base + GENERAL_STEPS + 2)
                    step(nc.vector.reciprocal(spec[:, 2 + m:3 + m], spec[:, 5:6]))
            nc.vector.tensor_tensor(spec[:, 9:10], spec[:, 2:3], spec[:, 3:4], ALU.mult).then_inc(sp_done, 1)

            own[:] = [0, dve_own2]

            dve.wait_ge(sp_done, 1)
            dve.wait_ge(lg_exp, 1)
            step(nc.vector.tensor_tensor(spec[:, 9:10], spec[:, 9:10], spec[:, 8:9], ALU.mult))


            def row_max(v):
                u, q, hp = STEPS[v]
                n = (q + 1) * P
                dve.wait_ge(at_s, v + 1)
                if v >= 3:
                    dve.wait_ge(at_exp, 2 * (v - 2))
                step(nc.vector.tensor_reduce(mx[:, v % 3, :], ps[:, 2 * (v % 2):2 * (v % 2) + 2, 0:n], AX.X, ALU.max))
                nc.vector.tensor_scalar(nmx[:, v % 3, :], mx[:, v % 3, :], -(HD ** -0.5), None, ALU.mult).then_inc(at_nm, 1)

            def normalise(v):
                u, q, hp = STEPS[v]
                n = (q + 1) * P
                dve.wait_ge(at_exp, 2 * (v + 1))
                step(nc.vector.reciprocal(rsum[:, v % 3, :], rsum[:, v % 3, :]))
                for h in range(2):
                    last = nc.vector.tensor_scalar(pr[v % 4][:, h, 0:n], pr[v % 4][:, h, 0:n], rsum[:, v % 3, h:h + 1],
                                                   None, ALU.mult)
                last.then_inc(at_p, 1)

            def probs_out(v):
                u, q, hp = STEPS[v]
                n = (q + 1) * P
                if v >= 4:
                    dve.wait_ge(at_pv, v // 2 - 1)
                dve.wait_ge(at_tr, 2 * v + 2)
                nc.vector.tensor_copy(pT[v % 4][:, 1, 0:n], ps[:, 5, 0:n]).then_inc(at_ev1, 1)

            def heads_out(u):
                b, k = UNITS[u]
                dve.wait_ge(at_pv, QT_N * (u + 1))
                nc.vector.tensor_copy(oT[:, k, b * T:(b + 1) * T], ps[:, 6, :]).then_inc(at_o, 1)

            def add_wo(t):
                dve.wait_ge(wo_mm, t + 1)
                nc.vector.tensor_tensor(xres[:, t, :], xres[:, t, :], ps[:, WO_BANK[t], :], ALU.add).then_inc(wo_x, 1)
                dve.wait_ge(wo_x, t + 1)

            row_max(0)
            for v in range(len(STEPS)):
                if v + 1 < len(STEPS):
                    row_max(v + 1)
                u, at_step = divmod(v, PER_UNIT)
                if at_step == FILL[1] + 1:
                    if u < QT_N:
                        add_bv(QT_N + u, 7)
                    else:
                        add_wo(u - QT_N)
                        layernorm_stats(u - QT_N, u == len(UNITS) - 1)
                if v >= 2:
                    probs_out(v - 2)
                if u and at_step == 3:
                    heads_out(u - 1)
                normalise(v)
                if evicted_part(v):
                    lower_part(*evicted_part(v))
            for v in range(len(STEPS) - 2, len(STEPS)):
                probs_out(v)
            layernorm_scale(1, 0)
            layernorm_apply(1, 0)
            layernorm_apply(1, 1)
            heads_out(len(UNITS) - 1)
            layernorm_apply(1, 2)
            layernorm_apply(1, 3)
            for t in range(NT // 2, NT):
                add_wo(t)
                layernorm_stats(t, t == NT - 1)
            layernorm_scale(1, 1)
            for t in range(NT // 2, NT):
                layernorm_apply(1, t)
            dve.wait_ge(rc_al, 2)
            step(nc.vector.tensor_scalar(colb[:, 4:8], colb[:, 4:8], -1.0, None, ALU.mult))
            step(nc.vector.tensor_tensor(colb[:, 0:4], cols[:, COL_BP:COL_BP + 4], cols[:, COL_DB:COL_DB + 4], ALU.add))

            def banks(q):
                return ps[:, RC_BANK[q]:RC_BANK[q] + 2, :].rearrange("p a n -> p (a n)")

            for n in range(NB):
                a, b_, c, z, u1, u2, u3 = (t[:, n % 2, :] for t in (rA, rB, rC, rZ, t1, t2, t3))
                dve.wait_ge(rc_mm, 4 * n + 1)
                nc.vector.tensor_scalar(u1, banks(0), colb[:, n:n + 1], 20.0, ALU.add, ALU.min).then_inc(rc_cap, 1)
                dve.wait_ge(rc_sp, 2 * n + 2)
                nc.vector.scalar_tensor_tensor(out=u1, in0=banks(0), scalar=colb[:, n:n + 1], in1=u1,
                                               op0=ALU.add, op1=ALU.max).then_inc(rc_delta, 1)
                dve.wait_ge(rc_a, n + 1)
                nc.vector.tensor_scalar(a, a, 1.0 - 1e-4, None, ALU.min).then_inc(rc_amin, 1)
                dve.wait_ge(rc_amin, n + 1)
                dve.wait_ge(rc_sq, 2 * n + 2)
                step(nc.vector.tensor_tensor(u1, u1, u3, ALU.add))
                dve.wait_ge(rc_thb, n + 1)
                nc.vector.tensor_tensor(z, a, b_, ALU.mult).then_inc(rc_q, 1)
                dve.wait_ge(rc_sqb, n + 1)
                nc.vector.tensor_tensor(u3, u1, u2, ALU.subtract).then_inc(rc_dif, 1)
                dve.wait_ge(rc_sq1, 2 * n + 2)
                nc.vector.tensor_tensor(u3, u3, z, ALU.add).then_inc(rc_disc, 1)
                dve.wait_ge(rc_root, n + 1)
                dve.wait_ge(rc_sum, n + 1)
                step(nc.vector.tensor_tensor(u1, u1, u3, ALU.add))
                nc.vector.tensor_scalar(u1, u1, 2e-12, 2.0, ALU.add, ALU.max).then_inc(rc_lam, 1)
                dve.wait_ge(rc_mm, 4 * n + 4)
                nc.vector.tensor_tensor(b_, b_, banks(3), ALU.mult).then_inc(rc_bu, 1)
                dve.wait_ge(rc_bu, n + 1)
                dve.wait_ge(rc_inv, 2 * n + 2)
                nc.vector.tensor_tensor(a, a, u1, ALU.mult)
                step(nc.vector.tensor_tensor(b_, b_, u1, ALU.mult))
                for b in range(B):
                    nc.vector.tensor_tensor_scan(z[:, b * T:(b + 1) * T], a[:, b * T:(b + 1) * T], b_[:, b * T:(b + 1) * T],
                                                 0.0, ALU.mult, ALU.add)
                step(nc.vector.tensor_tensor(c, c, u1, ALU.mult))
                for b in range(B):
                    nc.vector.memset(yh[:, n, b * T:b * T + 1], 0.0)
                    last = nc.vector.tensor_tensor(yh[:, n, b * T + 1:(b + 1) * T], c[:, b * T + 1:(b + 1) * T],
                                                   z[:, b * T:(b + 1) * T - 1], ALU.mult)
                last.then_inc(rc_y, 1)
                dve.wait_ge(rc_y, n + 1)

            def add_ro(t):
                dve.wait_ge(ro_mm, t + 1)
                nc.vector.scalar_tensor_tensor(out=xres[:, t, :], in0=ps[:, RO_BANK[t], :], scalar=spec[:, 9:10],
                                               in1=xres[:, t, :], op0=ALU.mult, op1=ALU.add).then_inc(ro_x, 1)
                dve.wait_ge(ro_x, t + 1)

            iota = consts[:, C_IOTA:C_IOTA + E]

            def logits_out(half):
                dve.wait_ge(rt_lgT, half + 1)
                nc.vector.tensor_copy(lgT[half], ps[:, LGT_BANK[half], 0:P]).then_inc(rt_lgs, 1)

            def choose(half):
                dve.wait_ge(rt_lg, half + 1)
                tiles = range(half * NT // 2, (half + 1) * NT // 2)

                def logits(t):
                    g = t - half * NT // 2
                    return ps[:, LG_BANK[half], g * E:(g + 1) * E]

                for t in tiles:
                    last = nc.vector.max(top8[:, t, :], logits(t))
                last.then_inc(rt_max, 1)
                dve.wait_ge(rt_max, half + 1)
                for t in tiles:
                    last = nc.vector.max_index(idx8[:, t, :], top8[:, t, :], logits(t))
                step(last)
                step(nc.vector.tensor_copy(idxf[:, tiles[0]:tiles[-1] + 1], idx8[:, tiles[0]:tiles[-1] + 1, 0]))
                for t in tiles:
                    last = nc.vector.tensor_scalar(ohb[:, t, :], iota, idxf[:, t:t + 1], None, ALU.is_equal)
                last.then_inc(rt_oh, 1)

            residual_layernorm(2, add_ro, RO_EARLY)
            layernorm_apply(2, 4)
            layernorm_apply(2, 5)
            logits_out(0)
            layernorm_apply(2, 6)
            layernorm_apply(2, 7)
            choose(0)
            logits_out(1)
            choose(1)
            dve.wait_ge(rt_oh, 2)
            step(nc.vector.tensor_scalar(pos[:, 2, :], idxf[:, :], float(CAP), None, ALU.mult))
            dve.wait_ge(rt_rank, 1)
            step(nc.vector.tensor_scalar(ecnti[:, :], ps[:, RANK_BANK, NT * E:NT * E + E], float(CAP - 1), None, ALU.add))
            step(nc.vector.tensor_scalar(ecnti[:, :], ecnti[:, :], CAP.bit_length() - 1, None, ALU.logical_shift_right))
            step(nc.vector.tensor_copy(ecnt[:, 0, :], ecnti[:, :]))
            step(nc.vector.tensor_scalar(ecnt[:, 0, :], ecnt[:, 0, :], -1.0, 0.0, ALU.add, ALU.max))
            step(nc.vector.tensor_tensor_scan(ecnt[:, 1, :], ones32[:, 0:E], ecnt[:, 0, :], 0.0, ALU.mult, ALU.add))
            step(nc.vector.tensor_tensor(ecnt[:, 2, :], ecnt[:, 1, :], ecnt[:, 0, :], ALU.subtract))
            step(nc.vector.tensor_tensor(prod[:, :, :], ohb[:, :, :], ps[:, RANK_BANK, 0:NT * E].rearrange("p (t e) -> p t e", t=NT), ALU.mult))
            step(nc.vector.tensor_reduce(pos[:, 0, :], prod[:, :, :], AX.X, ALU.add))
            step(nc.vector.tensor_tensor(prod[:, :, :], ohb[:, :, :],
                                         ecnt[:, 2:3, :].broadcast_to([P, NT, E]), ALU.mult))
            step(nc.vector.tensor_reduce(pos[:, 1, :], prod[:, :, :], AX.X, ALU.add))
            step(nc.vector.tensor_scalar(pos[:, 3, :], pos[:, 1, :], float(CAP), float(CAP * (E - 1)), ALU.mult, ALU.add))
            step(nc.vector.tensor_tensor(pos[:, 3, :], pos[:, 3, :], pos[:, 2, :], ALU.subtract))
            step(nc.vector.tensor_scalar(pos[:, 4, :], pos[:, 0, :], float(CAP), None, ALU.is_ge))
            step(nc.vector.tensor_tensor(pos[:, 3, :], pos[:, 3, :], pos[:, 4, :], ALU.mult))
            step(nc.vector.tensor_tensor(pos[:, 2, :], pos[:, 2, :], pos[:, 3, :], ALU.add))
            nc.vector.tensor_tensor(slot[:, :], pos[:, 0, :], pos[:, 2, :], ALU.add).then_inc(rt_slot, 1)
            dve.wait_ge(rt_sig, 1)
            step(nc.vector.tensor_tensor(score[:, :], score[:, :], rstd[:, :], ALU.mult))
            for t in range(NT):
                nc.vector.tensor_scalar(xsc[t], xres[:, t, :], mv[:, t, 0:1], score[:, t:t + 1],
                                        ALU.subtract, ALU.mult).then_inc(rt_xs, 1)
            for o in range(XTRA):
                last = nc.vector.tensor_scalar(ovl[:, o, :], ecnt[:, 1, :], float(o), None, ALU.is_le)
            step(last)
            step(nc.vector.tensor_reduce(ovs[:, 0:XTRA], ovl[:, :, :], AX.X, ALU.add))
            step(nc.vector.tensor_scalar(ovs[:, 0:XTRA], ovs[:, 0:XTRA], float(E - 1), None, ALU.min))
            step(nc.vector.tensor_copy(ovs[:, XTRA:XTRA + 1], ecnt[:, 1, E - 1:E]))
            nc.vector.tensor_copy(ovi[:, :], ovs[:, :]).then_inc(rt_tab, 1)
            dve.wait_ge(rt_tab, 1)

            def tile_x_out(n):
                dve.wait_ge(ex_tr, n)
                nc.vector.tensor_copy(xeT, ps[:, 4, :].rearrange("p (k n) -> p k n", k=KD)).then_inc(ex_xT, 1)

            dve.sem_inc(sh_x, 1)
            with dve.Fori(0, E // 4) as i:
                for j in range(4):
                    e = i * 4 + j
                    if j == 0:
                        nc.vector.tensor_copy(xsT, xT[:, :, bass.ds(i * P, P)]).then_inc(xs_cp, 1)
                        tile_x_out(i * 2 + 1)
                    dve.wait_ge(ex_silu, e + 1)
                    dve.wait_ge(ex_u, e + 3)
                    nc.vector.tensor_tensor(he, ge, ps[:, 1, :], ALU.mult).then_inc(ex_h, 1)
                    if j == 1:
                        tile_x_out(i * 2 + 2)
                    dve.wait_ge(ex_ht, e + 1)
                    nc.vector.tensor_copy(heT, ps[:, 5, :].rearrange("p (c n) -> p c n", c=4)).then_inc(ex_hT, 1)
                    if j % 2 == 0:
                        dve.wait_ge(sh_silu, i * 2 + j // 2 + 1)
                        dve.wait_ge(sh_u, i * 2 + j // 2 + 1)
                        nc.vector.tensor_tensor(hs, sgt, ps[:, 3, :], ALU.mult).then_inc(sh_h, 1)
                    if j == 3:
                        dve.wait_ge(sh_y, i + 1)
                        xt = xres[:, bass.ds(i, 1), :].rearrange("p a n -> p (a n)")
                        nc.vector.tensor_tensor(xt, xt, ps[:, 7, :], ALU.add).then_inc(sh_x, 1)

            dve.wait_ge(rt_tab, 1)
            extra = dve.value_load(ovi[0:1, XTRA:XTRA + 1], min_val=0, max_val=XTRA)
            with dve.If(extra > 0):
                with dve.Fori(0, extra) as o:
                    dve.wait_ge(ov_silu, o + 1)
                    dve.wait_ge(ov_u, o + 2)
                    nc.vector.tensor_tensor(he, ge, ps[:, 1, :], ALU.mult).then_inc(ov_h, 1)
                    dve.wait_ge(ov_ht, o + 1)
                    nc.vector.tensor_copy(heT, ps[:, 5, :].rearrange("p (c n) -> p c n", c=4)).then_inc(ov_hT, 1)

            dve.wait_ge(sh_x, NT + 1)
            for t in range(NT):
                dve.wait_ge(gat[t], 16)
                nc.vector.tensor_tensor(fin[t], fin[t], xres[:, t, :], ALU.add).then_inc(fin_add, 1)

        @block.tensor
        def _(pe):
            mm = nc.tensor.matmul

            def gram(banks, w):
                for r in range(KD):
                    for k in range(KD):
                        last = mm(ps[:, banks + r, :], w[:, k, r * P:(r + 1) * P], w[:, k, :], start=(k == 0), stop=(k == KD - 1))
                return last

            pe.wait_ge(sp_conv, 2)
            for s in range(5):
                if s:
                    pe.wait_ge(sp_ev0, s)
                gram(0, spp[0][s % 2]).then_inc(sp_sq, 1)
                if s:
                    pe.wait_ge(sp_ev1, s)
                gram(4, spp[1][s % 2]).then_inc(sp_sq, 1)
            pe.wait_ge(zeroed, 1)
            pe.wait_ge(sp_sum, 2)
            mm(ps[:, 0, 0:2], ones32[:, :], spec[:, 0:2], start=True, stop=True).then_inc(sp_tot, 1)
            def product(dst, lhs, rhs, chunks=KD):
                for k in range(chunks):
                    last = mm(dst, lhs(k), rhs(k), start=(k == 0), stop=(k == chunks - 1))
                return last

            def transpose_tile(n, t):
                pe.wait_ge(ln_xn, n * NT + t + 1)
                if n and t >= 2:
                    pe.wait_ge(ln_xT, n * NT + t - 1)
                for k in range(KD):
                    last = mm(ps[:, ln_bank(n, t), k * P:(k + 1) * P], xn[n][t % len(xn[n])][:, k * P:(k + 1) * P], ident,
                              start=True, stop=True, is_transpose=True)
                last.then_inc(ln_tr, 1)

            def project(u, i, chunks=range(KD)):
                b, k = UNITS[u]
                w, src = ((wk_s, cT), (wq_s, xT))[i]
                if 2 * u + i and chunks[0] == 0:
                    pe.wait_ge(kq_lo, 2 * u + i)
                if i == 0 and u >= 2 and chunks[0] == 0:
                    if u - 2 < QT_N:
                        pe.wait_ge(v_out, QT_N + u - 1)
                    else:
                        pe.wait_ge(wo_x, u - 1 - QT_N)
                for c in chunks:
                    last = mm(ps[:, 7, :], w[:, c, k * P:(k + 1) * P], src[:, c, b * T:(b + 1) * T], start=(c == 0), stop=(c == KD - 1))
                if chunks[-1] == KD - 1:
                    last.then_inc(kq_mm, 1)

            pe.wait_ge(ld_const, 48)
            for t in range(NT):
                if t == NT - 1:
                    pe.wait_ge(sp_flag, 1)
                transpose_tile(0, t)
            pe.wait_ge(ld_wk, 16)
            pe.wait_ge(ld_ctx, 16)
            pe.wait_ge(ln_xT, 1)
            project(0, 0)
            pe.wait_ge(ld_wq, 16)
            pe.wait_ge(ln_xT, NT)
            project(0, 1)
            project(1, 0)
            pe.wait_ge(ld_wv, 16)
            for t in range(NT // 2):
                product(ps[:, 2 + t, :], lambda k: cT[:, k, t * P:(t + 1) * P], lambda k: wv_s[:, k, :]).then_inc(v_mm, 1)

            pe.wait_ge(v_out, NT // 2)
            pe.wait_ge(sp_flag, 1)
            general = pe.value_load(flag[0:1, 0:1], min_val=0, max_val=1)
            with pe.If(general > 0):
                for m in range(2):
                    base = m * (GENERAL_STEPS + 2)
                    gram(0, spw[m]).then_inc(gp_mm, 1)
                    pe.wait_ge(gp_ssq, 3 * base + 1)
                    mm(ps[:, 4, 0:1], ones32[:, :], spec[:, 4:5], start=True, stop=True).then_inc(gp_tot, 1)
                    with pe.Fori(0, GENERAL_STEPS) as i:
                        pe.wait_ge(gp_nrm, i + (base + 1))
                        gram(0, g_p).then_inc(gp_mm, 1)
                        pe.wait_ge(gp_ssq, i * 3 + (3 * base + 4))
                        mm(ps[:, 4, 0:1], ones32[:, :], spec[:, 4:5], start=True, stop=True).then_inc(gp_tot, 1)
                    pe.wait_ge(gp_a, m + 1)
                    pe.wait_ge(gp_nrm, base + GENERAL_STEPS + 1)
                    for r in range(KD):
                        for k in range(KD):
                            last = mm(ps[:, r, :], g_a[:, k, r * P:(r + 1) * P], g_p[:, k, :], start=(k == 0), stop=(k == KD - 1))
                    last.then_inc(gp_mm, 1)
                    pe.wait_ge(gp_ssq, 3 * (base + GENERAL_STEPS + 1) + 2)
                    mm(ps[:, 4, 0:1], ones32[:, :], spec[:, 4:5], start=True, stop=True)
                    mm(ps[:, 4, 1:2], ones32[:, :], spec[:, 13:14], start=True, stop=True).then_inc(gp_tot, 1)
                    pe.wait_ge(gp_nrm, base + GENERAL_STEPS + 2)


            def scores(v):
                u, q, hp = STEPS[v]
                n = (q + 1) * P
                if v % PER_UNIT == 0:
                    pe.wait_ge(kq_ld[u % 2], 128 * (u // 2 + 1))
                if v >= 2:
                    pe.wait_ge(at_exp, 2 * (v - 1))
                for h in range(2):
                    bank = 2 * (v % 2) + h
                    mm(ps[:, bank, 0:n], qst[u % 2][:, 2 * hp + h, q * P:(q + 1) * P], kst[u % 2][:, 2 * hp + h, 0:n],
                       start=True, stop=True)
                    last = mm(ps[:, bank, q * P:n], identb[:, :], maskb[:, :], start=False, stop=True, skip_group_check=True)
                last.then_inc(at_s, 1)

            def probs_transposed(v):
                u, q, hp = STEPS[v]
                pe.wait_ge(at_p, v + 1)
                for h in range(2):
                    if v:
                        pe.wait_ge((at_ev0, at_ev1)[h], v)
                    for c in range(q + 1):
                        last = mm(ps[:, 4 + h, c * P:(c + 1) * P], pr[v % 4][:, h, c * P:(c + 1) * P], ident,
                                  start=True, stop=True, is_transpose=True)
                    last.then_inc(at_tr, 1)

            def fill(u, chunks):
                t = QT_N + u if u < QT_N else u - QT_N
                if chunks[0] == 0:
                    pe.wait_ge(kq_lo, 2 * min(u + 2, len(UNITS)))
                    if u == QT_N:
                        pe.wait_ge(ld_wo, 16)
                        pe.wait_ge(at_o, QT_N)
                    elif u > QT_N:
                        pe.wait_ge(wo_x, u - QT_N)
                src, w, done = (cT, wv_s, v_mm) if u < QT_N else (oT, wo_s, wo_mm)
                for k in chunks:
                    last = mm(ps[:, 7, :], src[:, k, t * P:(t + 1) * P], w[:, k, :], start=(k == 0), stop=(k == KD - 1))
                if chunks[-1] == KD - 1:
                    last.then_inc(done, 1)

            def values(w):
                u, q, _ = STEPS[2 * w]
                b, k = UNITS[u]
                pe.wait_ge(at_ev0, 2 * w + 2)
                pe.wait_ge(at_ev1, 2 * w + 2)
                if q == 0 and u == QT_N:
                    pe.wait_ge(v_out, NT)
                if q == 0 and u:
                    pe.wait_ge(at_o, u)
                for c in range(q + 1):
                    for h in range(HB):
                        last = mm(ps[HD * h:HD * h + HD, 6, q * P:(q + 1) * P],
                                  vv[:, b * QT_N + c, k * P + HD * h:k * P + HD * h + HD],
                                  pT[(2 * w + h // 2) % 4][:, h % 2, c * P:(c + 1) * P], start=(c == 0), stop=(c == q))
                last.then_inc(at_pv, 1)

            pe.wait_ge(v_out, NT // 2)
            pe.wait_ge(consts_b, 2)
            scores(0)
            for v in range(len(STEPS)):
                if v + 1 < len(STEPS):
                    scores(v + 1)
                if v >= 2:
                    probs_transposed(v - 2)
                if v >= 4 and v % 2 == 0:
                    values((v - 4) // 2)
                u, at_step = divmod(v, PER_UNIT)
                if at_step in PROJECT:
                    ahead, i, chunks = PROJECT[at_step]
                    if u + ahead < len(UNITS):
                        project(u + ahead, i, chunks)
                if at_step in FILL:
                    fill(u, range(2 * (at_step - FILL[0]), 2 * (at_step - FILL[0] + 1)))
            for v in range(len(STEPS) - 2, len(STEPS)):
                probs_transposed(v)
            for w in range(len(STEPS) // 2 - 2, len(STEPS) // 2):
                values(w)

            def wo_product(t):
                product(ps[:, WO_BANK[t], :], lambda k: oT[:, k, t * P:(t + 1) * P], lambda k: wo_s[:, k, :]).then_inc(wo_mm, 1)

            transpose_tile(1, 0)
            transpose_tile(1, 1)
            pe.wait_ge(at_o, len(UNITS))
            wo_product(4)
            wo_product(5)
            transpose_tile(1, 2)
            transpose_tile(1, 3)
            wo_product(6)
            wo_product(7)

            pe.wait_ge(ld_rec, 48)
            for n in range(NB):
                for q in range(4):
                    used = (rc_delta, rc_thc, rc_thb, rc_bu)[q]
                    if n:
                        pe.wait_ge(used, n)
                    row = NCH * (0, 2, 1, 0)[q] + n * P
                    w = (lambda k: wp_s[:, k, row:row + P]) if q < 3 else (lambda k: win_s[:, k, n * P:(n + 1) * P])
                    for b in range(B):
                        if n == 0 and q == 0:
                            if b == 1:
                                for t in range(NT // 2, NT):
                                    transpose_tile(1, t)
                            pe.wait_ge(wo_x, 5 + b)
                            pe.wait_ge(ln_xT, NT + (b + 1) * NT // 2)
                        elif n == 0 and q == 1:
                            pe.wait_ge(wo_x, NT)
                        last = product(ps[:, RC_BANK[q] + b, :], w, lambda k: xT[:, k, b * T:(b + 1) * T])
                    last.then_inc(rc_mm, 1)

            def ro_part(t, chunks):
                for k in chunks:
                    last = mm(ps[:, RO_BANK[t], :], yh[:, k, t * P:(t + 1) * P], wout_s[:, k, :], start=(k == 0), stop=(k == NB - 1))
                return last

            pe.wait_ge(rc_delta, NB)
            pe.wait_ge(rc_thc, NB)
            pe.wait_ge(rc_thb, NB)
            pe.wait_ge(rc_y, NB - 1)
            for t in range(RO_EARLY):
                ro_part(t, range(NB - 1))
            pe.wait_ge(rc_y, NB)
            for t in range(RO_EARLY):
                ro_part(t, range(NB - 1, NB)).then_inc(ro_mm, 1)
            for t in range(RO_EARLY, NT):
                pe.wait_ge(ro_x, t - RO_EARLY + 1)
                ro_part(t, range(NB)).then_inc(ro_mm, 1)

            def router(half):
                pe.wait_ge(ln_xT, 2 * NT + (half + 1) * NT // 2)
                for k in range(KD):
                    for g in range(NT // 2):
                        t = half * NT // 2 + g
                        last = mm(ps[E * g:E * g + E, LGT_BANK[half], 0:P], gw[:, k, :], xT[:, k, t * P:(t + 1) * P],
                                  start=(k == 0), stop=(k == KD - 1))
                last.then_inc(rt_lgT, 1)

            def logits(half):
                pe.wait_ge(rt_lgs, half + 1)
                mm(ps[:, LG_BANK[half], 0:P], lgT[half], ident, start=True, stop=True, is_transpose=True).then_inc(rt_lg, 1)

            def ranks(t):
                pe.wait_ge(rt_oh, t // (NT // 2) + 1)
                for j in range(t):
                    mm(ps[:, RANK_BANK, t * E:(t + 1) * E], onesb[:, :], ohb[:, j, :], start=(j == 0), stop=False)
                mm(ps[:, RANK_BANK, t * E:(t + 1) * E], trib[:, :], ohb[:, t, :], start=(t == 0), stop=True)

            pe.wait_ge(ld_gw, 16)
            pe.wait_ge(ready_c, 1)
            pe.wait_ge(ro_x, NT)
            for t in range(NT):
                transpose_tile(2, t)
                if t == 4:
                    router(0)
                elif t == 5:
                    logits(0)
            router(1)
            for t in range(NT // 2):
                ranks(t)
            logits(1)
            for t in range(NT // 2, NT):
                ranks(t)
            product(ps[:, RANK_BANK, NT * E:NT * E + E], lambda k: onesb[:, :], lambda k: ohb[:, k, :], NT).then_inc(rt_rank, 1)

            def tile_x(j):
                for k in range(KD):
                    last = mm(ps[:, 4, k * P:(k + 1) * P], xe[j][:, k * P:(k + 1) * P], ident, start=True, stop=True,
                              is_transpose=True)
                return last

            def tile_up(j, w, bank):
                for k in range(KD):
                    for half in range(2):
                        last = mm(ps[CAP * half:CAP * half + CAP, bank, :], xeT[:, k, j * CAP:(j + 1) * CAP],
                                  w[:, k, half * 512:(half + 1) * 512], start=(k == 0), stop=(k == KD - 1))
                return last

            def tile_h():
                for c in range(4):
                    last = mm(ps[:, 5, c * P:(c + 1) * P], he[:, c * P:(c + 1) * P], ident, start=True, stop=True,
                              is_transpose=True)
                return last

            def tile_down(w):
                for c in range(I // P):
                    for half in range(2):
                        last = mm(ps[CAP * half:CAP * half + CAP, 6, 0:256], heT[:, c % 4, (c // 4) * CAP:(c // 4 + 1) * CAP],
                                  w[:, c, half * 256:(half + 1) * 256], start=(c == 0), stop=(c == I // P - 1))
                return last

            def shared_gate(k, half):
                return mm(ps[:, 2, :], xsT[:, k, :], w_gate(w_shared)[:, k, half * 512:(half + 1) * 512],
                          start=(k == 0), stop=(k == KD - 1))

            def shared_up(k, half):
                return mm(ps[:, 3, :], xsT[:, k, :], w_up(w_shared)[:, k, half * 512:(half + 1) * 512],
                          start=(k == 0), stop=(k == KD - 1))

            def shared_down(c, half):
                return mm(ps[:, 7, :], hsT[:, c, :], w_down(w_shared)[:, half * 4 + c, :],
                          start=(half == 0 and c == 0), stop=(half == 1 and c == 3))

            with pe.Fori(0, E // 4) as i:
                for j in range(4):
                    e, half = i * 4 + j, j // 2
                    n = i * 2 + half
                    wr = ring[j % 2]
                    loaded = i * 32 + 16 * (half + 1)
                    if j == 0:
                        pe.wait_ge(xs_cp, i + 1)
                        pe.wait_ge(ld_shared, 48)
                    if j % 2 == 0:
                        for k in range(KD):
                            last = shared_gate(k, half)
                        last.then_inc(sh_g, 1)
                        if j == 0:
                            pe.wait_ge(ex_x[0], i * 16 + 16)
                            tile_x(0).then_inc(ex_tr, 1)
                        shared_up(0, half)
                    if j % 2 == 0:
                        pe.wait_ge(ex_xT, n + 1)
                    pe.wait_ge(ld_gate[j % 2], loaded)
                    tile_up(j % 2, w_gate(wr), 0).then_inc(ex_g, 1)
                    if j % 2 == 1:
                        pe.wait_ge(sh_h, n + 1)
                        for c in range(4):
                            last = mm(ps[:, 4, c * P:(c + 1) * P], hs[:, c * P:(c + 1) * P], ident, start=True, stop=True,
                                      is_transpose=True)
                        last.then_inc(sh_tr, 1)
                    pe.wait_ge(ld_up[j % 2], loaded)
                    tile_up(j % 2, w_up(wr), 1).then_inc(ex_u, 1)
                    if j % 2 == 0:
                        shared_up(1, half)
                    else:
                        pe.wait_ge(sh_T, n + 1)
                        if j == 1:
                            pe.wait_ge(ex_x[1], i * 16 + 16)
                            tile_x(1).then_inc(ex_tr, 1)
                            pe.wait_ge(sh_x, i + 1)
                        for c in range(2):
                            shared_down(c, half)
                    pe.wait_ge(ex_h, e + 1)
                    tile_h().then_inc(ex_ht, 1)
                    if j % 2 == 0:
                        for k in range(2, KD):
                            last = shared_up(k, half)
                        last.then_inc(sh_u, 1)
                    else:
                        for c in range(2, 4):
                            last = shared_down(c, half)
                        if j == 3:
                            last.then_inc(sh_y, 1)
                    pe.wait_ge(ex_hT, e + 1)
                    pe.wait_ge(ld_down[j % 2], loaded)
                    pe.wait_ge(ex_ye, e + 1)
                    tile_down(w_down(wr)).then_inc(ex_y, 1)

            pe.wait_ge(rt_tab, 1)
            extra = pe.value_load(ovi[0:1, XTRA:XTRA + 1], min_val=0, max_val=XTRA)
            with pe.If(extra > 0):
                pe.wait_ge(ex_ye, E + 1)
                with pe.Fori(0, extra) as o:
                    pe.wait_ge(ov_x, o * 16 + 16)
                    pe.wait_ge(ov_ye, o + 1)
                    tile_x(0).then_inc(ov_tr, 1)
                    pe.wait_ge(ov_xT, o + 1)
                    pe.wait_ge(ov_w[0], o * 16 + 16)
                    tile_up(0, w_gate(ring[0]), 0).then_inc(ov_g, 1)
                    pe.wait_ge(ov_w[1], o * 16 + 16)
                    tile_up(0, w_up(ring[0]), 1).then_inc(ov_u, 1)
                    pe.wait_ge(ov_h, o + 1)
                    tile_h().then_inc(ov_ht, 1)
                    pe.wait_ge(ov_hT, o + 1)
                    pe.wait_ge(ov_w[2], o * 16 + 16)
                    tile_down(w_down(ring[0])).then_inc(ov_y, 1)


def kernel(x, ctx_1024, L0_xattn_Wq, L0_xattn_bq, L0_xattn_Wk, L0_xattn_bk, L0_xattn_Wv, L0_xattn_bv, L0_xattn_Wo,
           L0_xattn_bo, L0_attn_W_in, L0_attn_W_out, L0_attn_Wp, L0_attn_bp, L0_attn_alpha_log, L0_attn_delta_bias,
           L0_attn_log_gamma, L0_ffn_gate_w, L0_ffn_shared_gate_w, L0_ffn_shared_up_w, L0_ffn_shared_down_w,
           L0_ffn_routed_gate_w, L0_ffn_routed_up_w, L0_ffn_routed_down_w):
    import numpy as np
    import concourse.bacc as bacc
    from concourse.bass_utils import run_bass_kernel_spmd

    def col(v):
        return np.asarray(v).reshape(-1, P).T

    consts = np.zeros((P, CONSTS), np.float32)
    consts[:, C_IDENT:C_IDENT + P] = np.eye(P)
    consts[:, C_MASK:C_MASK + P] = np.triu(np.full((P, P), MASKED), 1)
    consts[:, C_IOTA:C_IOTA + E] = np.arange(E)

    columns = np.concatenate([col(L0_xattn_bq), col(L0_xattn_bk), col(L0_attn_bp), col(L0_attn_delta_bias),
                              col(L0_attn_alpha_log), np.broadcast_to(np.asarray(L0_attn_log_gamma), (P, 1))], axis=1)
    rows = np.stack([np.broadcast_to(np.asarray(L0_xattn_bv), (P, D)), np.broadcast_to(np.asarray(L0_xattn_bo), (P, D))], axis=1)
    arrays = {
        "x": np.asarray(x).reshape(TOK, D),
        "ctxT": np.asarray(ctx_1024)[:, :T, :].transpose(2, 0, 1).reshape(D, TOK),
        "Wq": L0_xattn_Wq, "Wk": L0_xattn_Wk, "Wv": L0_xattn_Wv, "Wo": L0_xattn_Wo,
        "WinT": np.asarray(L0_attn_W_in).T, "WoutT": np.asarray(L0_attn_W_out).T, "WpT": np.asarray(L0_attn_Wp).T,
        "gate_w": L0_ffn_gate_w, "sg": L0_ffn_shared_gate_w, "su": L0_ffn_shared_up_w, "sd": L0_ffn_shared_down_w,
        "rg": L0_ffn_routed_gate_w, "ru": L0_ffn_routed_up_w, "rd": L0_ffn_routed_down_w,
        "cols": columns, "rows": rows, "consts": consts,
    }
    arrays = {"in_" + n: np.ascontiguousarray(a) for n, a in arrays.items()}
    nc = bacc.Bacc("TRN2", target_bir_lowering=False, num_devices=1)
    aps = [nc.dram_tensor(n, a.shape, mybir.dt.from_np(a.dtype), kind="ExternalInput").ap() for n, a in arrays.items()]
    out = nc.dram_tensor("out_0", (TOK, D), mybir.dt.float32, kind="ExternalOutput").ap()
    perceiver_layer(nc, *aps, out)
    r = run_bass_kernel_spmd(nc, [arrays], core_ids=[0])
    return r.results[0]["out_0"].reshape(B, T, D)
```
